# Optimizing a Trainium2 kernel written in Bass

```python
import numpy as np
import jax
import jax.numpy as jnp

def _softmax(x, axis=-1):
    return jax.nn.softmax(x, axis=axis)

def _gelu(x):
    return jax.nn.gelu(x, approximate=True)

def _silu(x):
    return jax.nn.silu(x)

def _sigmoid(x):
    return jax.nn.sigmoid(x)

def _layernorm(x, axis=-1, eps=1e-05):
    m = jnp.mean(x, axis=axis, keepdims=True)
    v = jnp.var(x, axis=axis, keepdims=True)
    return (x - m) / jnp.sqrt(v + eps)

def _scatter_add(tgt, idx, src, axis=0):
    return tgt.at[idx].add(src)

def _segment_sum(src, seg, n):
    return jax.ops.segment_sum(src, seg, n)
kernel_name = 'mk_decoder_postln_d2_seqx_r8_6ccbb5'

def setup_inputs(seed: int=0):
    np.random.seed(seed)
    _w = jnp.asarray

    def _rec_inputs():
        import jax
        import jax.numpy as jnp
        _rk = jax.random.key(seed)
        x = 7.22e-05 + 1 * jax.random.normal(jax.random.fold_in(_rk, 1), (4, 512, 128), jnp.float32)
        _lenS = 512 - jax.random.randint(jax.random.fold_in(_rk, 7), (4,), 0, max(1, 512 // 4) + 1, jnp.int32)
        _lenS2 = 154 - jax.random.randint(jax.random.fold_in(_rk, 8), (4,), 0, max(1, 154 // 4) + 1, jnp.int32)
        _ctx_1024P = jax.random.normal(jax.random.fold_in(_rk, 11), (4, 16, 128), jnp.float32)
        _ctx_1024c = jax.random.dirichlet(jax.random.fold_in(_rk, 511), 0.3 * jnp.ones((16,), jnp.float32), (4, 154))
        _ctx_1024t = jnp.einsum('bsk,bkd->bsd', _ctx_1024c, _ctx_1024P)
        _ctx_1024t = _ctx_1024t * jax.lax.rsqrt(jnp.mean(jnp.square(_ctx_1024t)) + 1e-12) * 0.953939
        ctx_1024 = 4.13588e-05 + 0.999923 * (_ctx_1024t + 0.3 * jax.random.normal(jax.random.fold_in(_rk, 611), (4, 154, 128), jnp.float32))
        return (x, ctx_1024)
    x, ctx_1024 = _rec_inputs()

    def _L0_attn_setup():
        import jax, jax.numpy as jnp
        import numpy as np
        D_MODEL = 128
        N_HEADS = 16
        LN_EPS = 1e-06

        def _layernorm(t, scale):
            mu = jnp.mean(t, axis=-1, keepdims=True)
            var = jnp.var(t, axis=-1, keepdims=True)
            return (t - mu) * jax.lax.rsqrt(var + LN_EPS) * scale
        key = jax.random.key(seed)
        k1, k2, k3 = jax.random.split(key, 3)
        B, S = (2, 256)
        x = jax.random.normal(k1, (B, S, D_MODEL), dtype=jnp.float32)
        W_qkv = jax.random.normal(k2, (D_MODEL, 3 * D_MODEL), dtype=jnp.float32) / np.sqrt(D_MODEL)
        W_out = jax.random.normal(k3, (D_MODEL, D_MODEL), dtype=jnp.float32) / np.sqrt(D_MODEL)
        q_scale = jnp.ones((D_MODEL,), dtype=jnp.float32)
        k_scale = jnp.ones((D_MODEL,), dtype=jnp.float32)
        return {'x': x, 'W_qkv': W_qkv, 'q_scale': q_scale, 'k_scale': k_scale, 'W_out': W_out}
    _L0_attn_all = _L0_attn_setup()
    _L0_attn_in = {k: v for k, v in _L0_attn_all.items() if k in ('W_qkv', 'q_scale', 'k_scale', 'W_out')}
    del _L0_attn_all

    def _L0_xattn_setup():
        import jax, jax.numpy as jnp
        import numpy as np
        D_MODEL = 128
        NUM_HEADS = 16
        HEAD_DIM = D_MODEL // NUM_HEADS
        B, T = (4, 256)
        key = jax.random.key(seed)
        ks = jax.random.split(key, 11)
        s = 0.02
        return {'q': jax.random.normal(ks[0], (B, T, D_MODEL), jnp.float32), 'k': jax.random.normal(ks[1], (B, T, D_MODEL), jnp.float32), 'v': jax.random.normal(ks[2], (B, T, D_MODEL), jnp.float32), 'Wq': jax.random.normal(ks[3], (D_MODEL, D_MODEL), jnp.float32) * s, 'bq': jnp.zeros((D_MODEL,), jnp.float32), 'Wk': jax.random.normal(ks[4], (D_MODEL, D_MODEL), jnp.float32) * s, 'bk': jnp.zeros((D_MODEL,), jnp.float32), 'Wv': jax.random.normal(ks[5], (D_MODEL, D_MODEL), jnp.float32) * s, 'bv': jnp.zeros((D_MODEL,), jnp.float32), 'Wo': jax.random.normal(ks[6], (D_MODEL, D_MODEL), jnp.float32) * s, 'bo': jnp.zeros((D_MODEL,), jnp.float32)}
    _L0_xattn_all = _L0_xattn_setup()
    _L0_xattn_in = {k: v for k, v in _L0_xattn_all.items() if k in ('Wq', 'bq', 'Wk', 'bk', 'Wv', 'bv', 'Wo', 'bo')}
    del _L0_xattn_all

    def _L0_ffn_setup():
        import jax, jax.numpy as jnp
        import numpy as np
        THRESHOLD = 0.1
        key = jax.random.key(seed)
        k1, k2, k3 = jax.random.split(key, 3)
        B, S, D, E = (4, 512, 128, 8)
        inputs = jax.random.normal(k1, (B, S, D), dtype=jnp.float32)
        gate_w = jax.random.normal(k2, (D, E), dtype=jnp.float32) * 0.02
        gate_b = jnp.zeros((E,), dtype=jnp.float32)
        expert_w = jax.random.normal(k3, (E, D, D), dtype=jnp.float32) * 0.02
        expert_b = jnp.zeros((E, D), dtype=jnp.float32)
        return {'inputs': inputs, 'gate_w': gate_w, 'gate_b': gate_b, 'expert_w': expert_w, 'expert_b': expert_b}
    _L0_ffn_all = _L0_ffn_setup()
    _L0_ffn_in = {k: v for k, v in _L0_ffn_all.items() if k in ('gate_w', 'gate_b', 'expert_w', 'expert_b')}
    del _L0_ffn_all

    def _L1_attn_setup():
        import jax, jax.numpy as jnp
        import numpy as np
        CHUNK = 128

        def phi(x):
            return jax.nn.elu(x) + 1.0
        key = jax.random.key(seed)
        ks = jax.random.split(key, 9)
        B, T, D = (4, 256, 128)
        s = 1.0 / np.sqrt(D)
        return {'x': jax.random.normal(ks[0], (B, T, D), dtype=jnp.float32), 'Wq': jax.random.normal(ks[1], (D, D), dtype=jnp.float32) * s, 'bq': jax.random.normal(ks[2], (D,), dtype=jnp.float32) * 0.01, 'Wk': jax.random.normal(ks[3], (D, D), dtype=jnp.float32) * s, 'bk': jax.random.normal(ks[4], (D,), dtype=jnp.float32) * 0.01, 'Wv': jax.random.normal(ks[5], (D, D), dtype=jnp.float32) * s, 'bv': jax.random.normal(ks[6], (D,), dtype=jnp.float32) * 0.01, 'Wo': jax.random.normal(ks[7], (D, D), dtype=jnp.float32) * s, 'bo': jax.random.normal(ks[8], (D,), dtype=jnp.float32) * 0.01}
    _L1_attn_all = _L1_attn_setup()
    _L1_attn_in = {k: v for k, v in _L1_attn_all.items() if k in ('Wq', 'bq', 'Wk', 'bk', 'Wv', 'bv', 'Wo', 'bo')}
    del _L1_attn_all

    def _L1_xattn_setup():
        import jax, jax.numpy as jnp
        import numpy as np
        B, Q, K, D, H, DH = (4, 64, 512, 128, 8, 128)
        key = jax.random.key(seed)
        ks = jax.random.split(key, 5)
        s = 1.0 / np.sqrt(D)
        return {'inputs_q': jax.random.normal(ks[0], (B, Q, D), jnp.float32), 'inputs_kv': jax.random.normal(ks[1], (B, K, D), jnp.float32), 'Wq': jax.random.normal(ks[2], (D, H, DH), jnp.float32) * s, 'Wkv': jax.random.normal(ks[3], (D, H, 2 * DH), jnp.float32) * s, 'Wproj': jax.random.normal(ks[4], (H, DH, D), jnp.float32) * (1.0 / np.sqrt(H * DH)), 'b_proj': jnp.zeros((D,), jnp.float32)}
    _L1_xattn_all = _L1_xattn_setup()
    _L1_xattn_in = {k: v for k, v in _L1_xattn_all.items() if k in ('Wq', 'Wkv', 'Wproj', 'b_proj')}
    del _L1_xattn_all

    def _L1_ffn_setup():
        import jax, jax.numpy as jnp
        import numpy as np
        DIM = 128
        HIDDEN = 384
        SCALE = 1.0 / 127.0

        def _dequant(w_int, dtype):
            return w_int.astype(dtype) * jnp.asarray(SCALE, dtype)
        key = jax.random.key(seed)
        k_x, k_g, k_u, k_d = jax.random.split(key, 4)
        x = jax.random.normal(k_x, (4, 256, DIM), dtype=jnp.float32)
        w_gate = jax.random.randint(k_g, (HIDDEN, DIM), -127, 128, dtype=jnp.int32)
        w_up = jax.random.randint(k_u, (HIDDEN, DIM), -127, 128, dtype=jnp.int32)
        w_down = jax.random.randint(k_d, (DIM, HIDDEN), -127, 128, dtype=jnp.int32)
        return {'x': x, 'w_gate': w_gate, 'w_up': w_up, 'w_down': w_down}
    _L1_ffn_all = _L1_ffn_setup()
    _L1_ffn_in = {k: v for k, v in _L1_ffn_all.items() if k in ('w_gate', 'w_up', 'w_down')}
    del _L1_ffn_all
    return {'x': x, 'ctx_1024': ctx_1024, 'L0_attn_W_qkv': _L0_attn_in['W_qkv'], 'L0_attn_q_scale': _L0_attn_in['q_scale'], 'L0_attn_k_scale': _L0_attn_in['k_scale'], 'L0_attn_W_out': _L0_attn_in['W_out'], 'L0_xattn_Wq': _L0_xattn_in['Wq'], 'L0_xattn_bq': _L0_xattn_in['bq'], 'L0_xattn_Wk': _L0_xattn_in['Wk'], 'L0_xattn_bk': _L0_xattn_in['bk'], 'L0_xattn_Wv': _L0_xattn_in['Wv'], 'L0_xattn_bv': _L0_xattn_in['bv'], 'L0_xattn_Wo': _L0_xattn_in['Wo'], 'L0_xattn_bo': _L0_xattn_in['bo'], 'L0_ffn_gate_w': _L0_ffn_in['gate_w'], 'L0_ffn_gate_b': _L0_ffn_in['gate_b'], 'L0_ffn_expert_w': _L0_ffn_in['expert_w'], 'L0_ffn_expert_b': _L0_ffn_in['expert_b'], 'L1_attn_Wq': _L1_attn_in['Wq'], 'L1_attn_bq': _L1_attn_in['bq'], 'L1_attn_Wk': _L1_attn_in['Wk'], 'L1_attn_bk': _L1_attn_in['bk'], 'L1_attn_Wv': _L1_attn_in['Wv'], 'L1_attn_bv': _L1_attn_in['bv'], 'L1_attn_Wo': _L1_attn_in['Wo'], 'L1_attn_bo': _L1_attn_in['bo'], 'L1_xattn_Wq': _L1_xattn_in['Wq'], 'L1_xattn_Wkv': _L1_xattn_in['Wkv'], 'L1_xattn_Wproj': _L1_xattn_in['Wproj'], 'L1_xattn_b_proj': _L1_xattn_in['b_proj'], 'L1_ffn_w_gate': _L1_ffn_in['w_gate'], 'L1_ffn_w_up': _L1_ffn_in['w_up'], 'L1_ffn_w_down': _L1_ffn_in['w_down']}

def reference(x, ctx_1024, L0_attn_W_qkv, L0_attn_q_scale, L0_attn_k_scale, L0_attn_W_out, L0_xattn_Wq, L0_xattn_bq, L0_xattn_Wk, L0_xattn_bk, L0_xattn_Wv, L0_xattn_bv, L0_xattn_Wo, L0_xattn_bo, L0_ffn_gate_w, L0_ffn_gate_b, L0_ffn_expert_w, L0_ffn_expert_b, L1_attn_Wq, L1_attn_bq, L1_attn_Wk, L1_attn_bk, L1_attn_Wv, L1_attn_bv, L1_attn_Wo, L1_attn_bo, L1_xattn_Wq, L1_xattn_Wkv, L1_xattn_Wproj, L1_xattn_b_proj, L1_ffn_w_gate, L1_ffn_w_up, L1_ffn_w_down):
    import jax
    import jax.numpy as jnp

    def _L0_attn_ref(x, W_qkv, q_scale, k_scale, W_out):
        import jax, jax.numpy as jnp
        import numpy as np
        D_MODEL = 128
        N_HEADS = 16
        LN_EPS = 1e-06

        def _layernorm(t, scale):
            mu = jnp.mean(t, axis=-1, keepdims=True)
            var = jnp.var(t, axis=-1, keepdims=True)
            return (t - mu) * jax.lax.rsqrt(var + LN_EPS) * scale
        B, S, D = x.shape
        H = N_HEADS
        Hd = D // H
        qkv = jnp.einsum('bsd,de->bse', x, W_qkv)
        q, k, v = jnp.split(qkv, 3, axis=-1)
        q = _layernorm(q, q_scale)
        k = _layernorm(k, k_scale)
        q = q.reshape(B, S, H, Hd)
        k = k.reshape(B, S, H, Hd)
        v = v.reshape(B, S, H, Hd)
        scores = jnp.einsum('bshd,bthd->bhst', q / jnp.sqrt(Hd).astype(q.dtype), k)
        future = jnp.triu(jnp.ones((S, S), dtype=bool), 1)
        scores = jnp.where(future[None, None, :, :], jnp.finfo(scores.dtype).min, scores)
        attn = jax.nn.softmax(scores, axis=-1)
        ctx = jnp.einsum('bhst,bthd->bshd', attn, v)
        out = jnp.einsum('bsd,de->bse', ctx.reshape(B, S, D), W_out)
        return out

    def _L0_xattn_ref(q, k, v, Wq, bq, Wk, bk, Wv, bv, Wo, bo):
        import jax, jax.numpy as jnp
        import numpy as np
        D_MODEL = 128
        NUM_HEADS = 16
        HEAD_DIM = D_MODEL // NUM_HEADS
        B, T = (4, 256)
        Bq, Tq, _ = q.shape
        Tk = k.shape[1]
        qh = (q @ Wq + bq).reshape(Bq, Tq, NUM_HEADS, HEAD_DIM).transpose(0, 2, 1, 3)
        kh = (k @ Wk + bk).reshape(Bq, Tk, NUM_HEADS, HEAD_DIM).transpose(0, 2, 1, 3)
        vh = (v @ Wv + bv).reshape(Bq, Tk, NUM_HEADS, HEAD_DIM).transpose(0, 2, 1, 3)
        scale = 1.0 / jnp.sqrt(jnp.asarray(HEAD_DIM, qh.dtype))
        scores = jnp.einsum('bhqd,bhkd->bhqk', qh, kh) * scale
        attn = jax.nn.softmax(scores, axis=-1)
        out = jnp.einsum('bhqk,bhkd->bhqd', attn, vh)
        out = out.transpose(0, 2, 1, 3).reshape(Bq, Tq, D_MODEL)
        return out @ Wo + bo

    def _L0_ffn_ref(inputs, gate_w, gate_b, expert_w, expert_b):
        import jax, jax.numpy as jnp
        import numpy as np
        THRESHOLD = 0.1
        d = inputs.shape[-1]
        x = inputs.reshape(-1, d)
        gate_logits = jax.nn.softmax(x @ gate_w + gate_b, axis=-1)
        selected = (gate_logits >= THRESHOLD).astype(x.dtype)
        weights = gate_logits * selected
        wsum = jnp.sum(weights, axis=-1, keepdims=True)
        weights = weights / jnp.where(wsum == 0, jnp.ones_like(wsum), wsum)
        E = expert_w.shape[0]
        out = jnp.zeros((x.shape[0], expert_w.shape[-1]), dtype=x.dtype)
        for e in range(E):
            out = out + weights[:, e:e + 1] * (x @ expert_w[e] + expert_b[e])
        return out.reshape(*inputs.shape[:-1], out.shape[-1])

    def _L1_attn_ref(x, Wq, bq, Wk, bk, Wv, bv, Wo, bo):
        import jax, jax.numpy as jnp
        import numpy as np
        CHUNK = 128

        def phi(x):
            return jax.nn.elu(x) + 1.0
        B, T, D = x.shape
        C = CHUNK
        N = T // C
        Qp = phi(x @ Wq.T + bq)
        Kp = phi(x @ Wk.T + bk)
        V = x @ Wv.T + bv
        Qr = Qp.reshape(B, N, C, D)
        Kr = Kp.reshape(B, N, C, D)
        Vr = V.reshape(B, N, C, D)
        KV = jnp.einsum('bncd,bnce->bnde', Kr, Vr)
        S = jnp.cumsum(KV, axis=1) - KV
        inter = jnp.einsum('bnde,bncd->bnce', S, Qr)
        mask = jnp.tril(jnp.ones((C, C), dtype=x.dtype))
        A = jnp.einsum('bncd,bnsd->bncs', Qr, Kr) * mask
        intra = jnp.einsum('bncs,bnse->bnce', A, Vr)
        num = (inter + intra).reshape(B, T, D)
        Z = jnp.cumsum(Kp, axis=1)
        den = jnp.sum(Z * Qp, axis=-1, keepdims=True) + 1e-06
        O = num / den
        return O @ Wo.T + bo

    def _L1_xattn_ref(inputs_q, inputs_kv, Wq, Wkv, Wproj, b_proj):
        import jax, jax.numpy as jnp
        import numpy as np
        B, Q, K, D, H, DH = (4, 64, 512, 128, 8, 128)
        q = jnp.einsum('bqd,dhe->bqhe', inputs_q, Wq)
        kv = jnp.einsum('bkd,dhe->bkhe', inputs_kv, Wkv)
        k, v = (kv[..., :DH], kv[..., DH:])
        attn = jnp.einsum('bqhd,bkhd->bhqk', q, k) / np.sqrt(DH)
        attn = jax.nn.softmax(attn.astype(jnp.float32), axis=-1).astype(v.dtype)
        o = jnp.einsum('bhqk,bkhd->bqhd', attn, v)
        return jnp.einsum('bqhd,hdo->bqo', o, Wproj) + b_proj

    def _L1_ffn_ref(x, w_gate, w_up, w_down):
        import jax, jax.numpy as jnp
        import numpy as np
        DIM = 128
        HIDDEN = 384
        SCALE = 1.0 / 127.0

        def _dequant(w_int, dtype):
            return w_int.astype(dtype) * jnp.asarray(SCALE, dtype)
        wg = _dequant(w_gate, x.dtype)
        wu = _dequant(w_up, x.dtype)
        wd = _dequant(w_down, x.dtype)
        gate = jnp.einsum('bsd,hd->bsh', x, wg)
        up = jnp.einsum('bsd,hd->bsh', x, wu)
        h = jax.nn.silu(gate) * up
        return jnp.einsum('bsh,dh->bsd', h, wd)
    x = _layernorm(x + _L0_attn_ref(x, L0_attn_W_qkv, L0_attn_q_scale, L0_attn_k_scale, L0_attn_W_out), axis=-1)
    x = _layernorm(x + _L0_xattn_ref(x, ctx_1024, ctx_1024, L0_xattn_Wq, L0_xattn_bq, L0_xattn_Wk, L0_xattn_bk, L0_xattn_Wv, L0_xattn_bv, L0_xattn_Wo, L0_xattn_bo), axis=-1)
    x = _layernorm(x + _L0_ffn_ref(x, L0_ffn_gate_w, L0_ffn_gate_b, L0_ffn_expert_w, L0_ffn_expert_b), axis=-1)
    x = _layernorm(x + _L1_attn_ref(x, L1_attn_Wq, L1_attn_bq, L1_attn_Wk, L1_attn_bk, L1_attn_Wv, L1_attn_bv, L1_attn_Wo, L1_attn_bo), axis=-1)
    x = _layernorm(x + _L1_xattn_ref(x, ctx_1024, L1_xattn_Wq, L1_xattn_Wkv, L1_xattn_Wproj, L1_xattn_b_proj), axis=-1)
    x = _layernorm(x + _L1_ffn_ref(x, L1_ffn_w_gate, L1_ffn_w_up, L1_ffn_w_down), axis=-1)
    return x

_drawn_inputs = setup_inputs


def setup_inputs(seed=0):
    import zlib

    import numpy as np

    out = dict(_drawn_inputs(seed))
    spreads = {'L0_attn_q_scale': (1.0, 0.2),
     'L0_attn_k_scale': (1.0, 0.2),
     'L0_xattn_bq': (0.0, 0.8),
     'L0_xattn_bk': (0.0, 0.8),
     'L0_xattn_bv': (0.0, 0.1),
     'L0_xattn_bo': (0.0, 0.1),
     'L0_ffn_gate_b': (0.0, 0.1),
     'L0_ffn_expert_b': (0.0, 0.1),
     'L1_xattn_b_proj': (0.0, 0.1)}
    factors = {'L0_xattn_Wq': 8.0,
     'L0_xattn_Wk': 8.0,
     'L1_attn_Wq': 8.0,
     'L1_attn_bq': 8.0,
     'L1_attn_Wk': 4.473,
     'L1_attn_bk': 8.0,
     'L1_attn_bv': 4.17,
     'L1_attn_bo': 4.34}
    for name, (base, spread) in spreads.items():
        noise = np.random.default_rng([zlib.crc32(name.encode()), seed]).standard_normal(out[name].shape)
        drawn = base * np.exp(spread * noise) if base else spread * noise
        out[name] = jnp.asarray(drawn.astype(out[name].dtype))
    for name, factor in factors.items():
        out[name] = (out[name] * factor).astype(out[name].dtype)
    return out
```

```python
from contextlib import ExitStack

import concourse.bass as bass
from concourse import mybir

F32 = mybir.dt.float32
BF16 = mybir.dt.bfloat16
I32 = mybir.dt.int32
ALU = mybir.AluOpType
ACT = mybir.ActivationFunctionType
AX = mybir.AxisListType

P = 128
B, S, D = 4, 512, 128
NB = S // P
H, HD = 16, 8
NQ = H // 4
C = 154
CR = C - P
CP = P + 32
XH = 8
E = 8
HID = 384
HC = HID // P
HEAD_SCALE = float(HD) ** -0.5
X_SCALE = float(D) ** -0.5
LN_EPS, QK_EPS = 1e-5, 1e-6
MASKED = -1e30
Q_PARTS = [0, 0, 0, 1, 1, 2]
K_PARTS = [0, 1, 2, 0, 1, 0]
SPLIT_ROWS = 96
MAX_ROW = 96


BANKS = {
    "x0T": (6,), "qkv": (0, 1, 2, 3), "qkT": (4, 5),
    "S": (0, 1, 2), "ST": (3, 4, 5), "PV": (6,), "mT": (7,), "cT": (7,),
    "ctxT": (6,), "out": (7,), "xT": (6,),
    "wT": (0, 1, 2, 3, 4, 5, 6, 7), "wM": (0, 1, 2, 3, 4, 5, 6, 7),
    "xq": (4,), "xk": (5,), "xv": (0,), "G": (0, 1, 2, 3), "Vm": (4, 5), "Vr": (6,),
    "gate": (6,), "gT": (7,), "mb": (7,), "ex": (0, 1, 2, 3, 4, 5),
    "lq": (0,), "lk": (1,), "lv": (2,), "kp": (3,), "A": (4,), "KV": (5,), "lo": (6, 7),
    "XS": (0, 1, 2, 3), "PT": (4, 5), "PR": (6,), "XO": (7,), "XOT": (6,),
    "hid": (0, 1, 2, 3, 4, 5), "down": (6,),
}
SELF_PIECES = []
for pair in (0, 2):
    SELF_PIECES += [[(0, pair, 3)], [(0, pair + 1, 3)],
                    [(0, pair, 2), (384, pair, 0)], [(0, pair + 1, 2), (384, pair + 1, 0)],
                    [(0, pair, 1), (256, pair + 1, 1)]]
SELF_T_PIECES = []
for pair in (0, 2):
    SELF_T_PIECES += [[(0, pair, 0)], [(0, pair + 1, 0)],
                      [(0, pair, 1), (384, pair, 3)], [(0, pair + 1, 1), (384, pair + 1, 3)],
                      [(0, pair, 2), (256, pair + 1, 2)]]
X_PIECES = [[(0, pair, q), (C, pair + 1, q)] for q in range(NB) for pair in (0, 2)]
AHEAD = 4


def attention_steps(units, t_units):
    for t in range(NQ + 2):
        if t < NQ:
            yield from (("S", t, u) for u in range(AHEAD))
        if t >= 2:
            yield "PV", t - 2, 0
        for i in range(max(units - AHEAD, t_units)):
            if t < NQ and AHEAD + i < units:
                yield "S", t, AHEAD + i
            if 1 <= t <= NQ and i < t_units:
                yield "ST", t - 1, i
        if t < NQ:
            yield "mT", t, 0
        if t >= 2:
            yield "cT", t - 2, 0


def fills():
    def prep(b):
        yield b, "x0T", 0
        yield from ((b, "qkv", n) for n in range(NB))
        yield from ((b, "qkT", n) for n in range(2))

    def attention(b, layer, units, t_units):
        yield from ((b, what, (layer, g, u)) for what, g, u in attention_steps(units, t_units))
        yield b, "ctxT", layer
        yield b, "out", layer

    yield from prep(0)
    for b in range(B):
        yield from attention(b, 0, len(SELF_PIECES), len(SELF_T_PIECES))
        if b == 0:
            yield from ((0, "wT", n) for n in range(SETUP_TRANSPOSES))
            yield from ((0, "wM", n) for n in range(SETUP_PRODUCTS))
        yield from ((b, "xk", 0), (b, "xv", 0), (b, "xT", 1), (b, "xq", 0))
        yield from ((b, "G", n) for n in range(XH // 2))
        yield from ((b, "Vm", n) for n in range(2))
        yield b, "Vr", 0
        if b + 1 < B:
            yield from prep(b + 1)
        yield from attention(b, 1, len(X_PIECES), 5)
        yield from ((b, "xT", 2), (b, "gate", 0))
        yield from ((b, "ex", n) for n in range(2))
        yield b, "gT", 0
        yield b, "mb", 0
        yield from ((b, "ex", n) for n in range(2, 2 * NB))
        yield b, "xT", 3
        yield from ((b, "lk", 0), (b, "lq", 0), (b, "lv", 0), (b, "kp", 0), (b, "A", 0), (b, "KV", 0))
        yield from ((b, "lo", n) for n in range(2))
        yield b, "xT", 4
        for u in range(2 * NB + 1):
            if u < 2 * NB:
                yield from ((b, "XS", 2 * u + n) for n in range(2))
            if u >= 1:
                yield from ((b, "PT", u - 1), (b, "PR", u - 1))
        yield b, "XO", 0
        yield b, "XOT", 0
        yield b, "xT", 5
        yield from ((b, "hid", n) for n in range(2 * HC))
        yield b, "down", 0


SETUP_TRANSPOSES = B + 3 * XH // 4 + 1 + 3
SETUP_PRODUCTS = 2 * XH // 4 + 1


def plan():
    place, count, turn = {}, [0] * 8, {}
    for key in fills():
        banks = BANKS[key[1]]
        n = turn.get(key[1], 0)
        turn[key[1]] = n + 1
        bank = banks[n % len(banks)]
        place[key] = bank, count[bank]
        count[bank] += 1
    return place


def build(nc, x, ctx_1024, L0_attn_W_qkv, L0_attn_q_scale, L0_attn_k_scale, L0_attn_W_out,
          L0_xattn_Wq, L0_xattn_bq, L0_xattn_Wk, L0_xattn_bk, L0_xattn_Wv, L0_xattn_bv,
          L0_xattn_Wo, L0_xattn_bo, L0_ffn_gate_w, L0_ffn_gate_b, L0_ffn_expert_w,
          L0_ffn_expert_b, L1_attn_Wq, L1_attn_bq, L1_attn_Wk, L1_attn_bk, L1_attn_Wv,
          L1_attn_bv, L1_attn_Wo, L1_attn_bo, L1_xattn_Wq, L1_xattn_Wkv, L1_xattn_Wproj,
          L1_xattn_b_proj, L1_ffn_w_gate, L1_ffn_w_up, L1_ffn_w_down, out):
    place = plan()
    with ExitStack() as stack:
        def sb(name, shape, dt=F32):
            return stack.enter_context(nc.sbuf_tensor(name, shape, dt))

        def sem(name):
            return stack.enter_context(nc.semaphore(name))

        psum = stack.enter_context(nc.psum_tensor("psum", [P, 8, 512], F32))
        bank_filled = [sem(f"bank_filled{n}") for n in range(8)]
        bank_drained = [sem(f"bank_drained{n}") for n in range(8)]

        def bank(key):
            return psum[:, place[key][0], :]

        def filled(eng, key):
            k, n = place[key]
            eng.wait_ge(bank_filled[k], n + 1)
            return psum[:, k, :]

        def drained(eng, key):
            k, n = place[key]
            eng.wait_ge(bank_drained[k], n + 1)

        def drains(ins, key):
            return ins.then_inc(bank_drained[place[key][0]], 1)

        ident = sb("ident", [P, P])
        identb = sb("identb", [P, P], BF16)
        ones = sb("ones", [P, P])
        causal = sb("causal", [P, P])
        maskS = sb("maskS", [P, P], BF16)
        maskT = sb("maskT", [P, P], BF16)
        power = sb("power", [P, 8])

        X0 = sb("X0", [P, 2, NB, D])
        X = [None] + 3 * [sb("X_odd", [P, NB, D]), sb("X_even", [P, NB, D])]
        XB = sb("XB", [P, NB, D])
        Y = sb("Y", [P, NB, D])
        xT0 = sb("xT0", [P, S])
        xT = [None] + 3 * [sb("xT_odd", [P, S]), sb("xT_even", [P, S])]
        stats = sb("stats", [P, NB, 6])
        moments = sb("moments", [P, NB, 2])
        rstd = sb("rstd", [P, NB])
        qkstats = sb("qkstats", [P, NB, 2, 6])
        qkmoments = sb("qkmoments", [P, NB, 2, 2])
        qkrstd = sb("qkrstd", [P, NB, 2])

        wqkv = sb("wqkv", [P, 3 * D])
        wqkv_p = sb("wqkv_p", [P, 3 * D])
        cols = sb("cols", [P, 16])
        COL = {n: i for i, n in enumerate(
            ("q_scale", "k_scale", "xbq", "xbk", "lbq", "lbk", "lbv", "bproj"))}
        QS, XBQ = 8, 9

        def col(i):
            i = COL.get(i, i)
            return cols[:, i:i + 1]

        wout = sb("wout", [P, D])
        Q6 = [sb(f"Q6_{n}", [P, H, S], BF16) for n in range(2)]
        K6 = [sb("K6_0", [P, H, S], BF16), sb("K6_1", [P, H, CP], BF16)]
        EX = sb("EX", [P, 2, 10, 512])
        flat_ex = EX[:, :, :, :].rearrange("p a u q -> p (a u q)")

        def within(at, n, m):
            return flat_ex[:, at:at + n * m].rearrange("p (n m) -> p n m", n=n)

        qkf = within(0, 2, S)
        rest = within(2 * S, 2, S)
        phi = within(10 * S, 2, S)
        kp = within(12 * S, NB, D)
        AT = within(13 * S, NB, P)
        hT = within(14 * S, HC, S)
        hexp = within(17 * S, HC, S)
        qkn = hexp[:, 0:2, :].rearrange("p w (n d) -> p w n d", n=NB)
        parts = sb("parts", [P, 2, 3, S], BF16)
        xf, xrest = qkf, rest
        xparts = sb("xparts", [P, 2, 3, S], BF16)
        V = sb("V", [P, NB, H, 32])
        VX = sb("VX", [P, H, 32])
        VXR = sb("VXR", [P, NQ, P])
        nmax = sb("nmax", [P, 4, NB])
        nrest = sb("nrest", [P, 16])
        mparts = sb("mparts", [P, 2, 3, 16], BF16)
        mrows = sb("mrows", [48, 2, P], BF16)
        pvraw = sb("pvraw", [P, 512])
        rsum = sb("rsum", [P, NB, 4])
        ctx = sb("ctx", [P, NB, H, HD])
        ctxT = sb("ctxT", [P, S])

        cx = sb("cx", [P, B, D])
        cxr = sb("cxr", [CR, B, D])
        cT = sb("cT", [P, B, CP])
        xwq = sb("xwq", [P, 2, D])
        xwk = sb("xwk", [P, 2, D])
        xwv = sb("xwv", [P, D])
        xwo = sb("xwo", [P, D])
        rows = sb("rows", [P, 4, D])
        BV, BO, LBO, LBV = range(4)

        gw = sb("gw", [P, E])
        gb = sb("gb", [P, E])
        ew = sb("ew", [P, E, D])
        eb = sb("eb", [NB * E, NB, D])
        gl = sb("gl", [P, NB, E])
        ge = sb("ge", [P, NB, E])
        gs = sb("gs", [P, NB])
        gr = sb("gr", [P, NB])
        gT = sb("gT", [NB * E, P])

        lw = sb("lw", [P, 4, D])
        lwT = sb("lwT", [P, 3, D])
        lwv = sb("lwv", [P, D])
        bvb = sb("bvb", [P, P])
        lexp, lpos = qkf, rest
        vaug = sb("vaug", [P, NB, D + 2])
        state = sb("state", [P, 3, D + 1])
        den = sb("den", [P, NB])

        aT = sb("aT", [P, XH, D])
        mv = sb("mv", [P, XH, D])
        VM = sb("VM", [P, XH, D])
        VR = sb("VR", [P, 2, D])
        GP = sb("GP", [P, XH * C + 2 * 4 * CP])
        G = GP[:, 0:XH * C].rearrange("p (h c) -> p h c", h=XH)
        XP = GP[:, XH * C:].rearrange("p (n c) -> p n c", n=2)
        nxmax = sb("nxmax", [P, 2, 4])
        xbias = sb("xbias", [P, 2, 4])
        xsum = sb("xsum", [P, 2, 4])
        xrs = sb("xrs", [P, 2, 4])
        fT = sb("fT", [P, 3, HID])
        raw = Q6[1][:, :, :].rearrange("p h t -> p (h t)").bitcast(F32)
        rq = raw[:, 0:XH * D].rearrange("p (h e) -> p h e", h=XH)
        rkv = raw[:, XH * D:3 * XH * D].rearrange("p (h e) -> p h e", h=XH)
        wp = raw[:, 3 * XH * D:4 * XH * D].rearrange("p (h e) -> p h e", h=XH)
        fi = xparts[:, :, :, :].rearrange("p a b t -> p (a b t)")[:, 0:6 * HID].bitcast(
            I32).rearrange("p (w h) -> p w h", w=3)
        whT = flat_ex[:, 0:3 * XH * D].rearrange("p (w h e) -> p w h e", w=3, h=XH)
        ff = within(3 * XH * D, 3, HID)
        XPT = within(0, XH, S)
        XPR = within(XH * S, 2, S)
        XE = flat_ex[:, 14 * S:14 * S + 8 * C].rearrange("p (n h c) -> p n h c", n=2, h=4)
        xoT = flat_ex[:, 10 * S:11 * S]

        x_loaded = [sem(f"x_loaded{b}") for b in range(B)]
        qkv_loaded = sem("qkv_loaded")
        early_loaded = sem("early_loaded")
        late_loaded = sem("late_loaded")
        consts_ready = sem("consts_ready")
        zeros_ready = sem("zeros_ready")
        wqkv_ready = sem("wqkv_ready")
        x0_weights_ready = sem("x0_weights_ready")
        bias_cols_ready = sem("bias_cols_ready")
        ff_ready = sem("ff_ready")
        bvb_ready = sem("bvb_ready")
        eb_loaded = sem("eb_loaded")
        dve_step = sem("dve_step")
        pool_step = sem("pool_step")
        v_copied = sem("v_copied")
        qk_stats_ready = sem("qk_stats_ready")
        qk_rstd_ready = sem("qk_rstd_ready")
        parts_ready = [sem("parts_ready0"), sem("parts_ready1")]
        qk_placed = [sem("qk_placed0"), sem("qk_placed1")]
        mparts_ready = sem("mparts_ready")
        max_placed = [sem("max_placed0"), sem("max_placed1")]
        exps_ready = sem("exps_ready")
        ctx_ready = sem("ctx_ready")
        stats_ready = [sem(f"stats_ready{n}") for n in range(6)]
        rstd_ready = [sem(f"rstd_ready{n}") for n in range(6)]
        x_ready = [None] + [sem(f"x_ready{n}") for n in range(1, 7)]
        xb_ready = sem("xb_ready")
        gate_shifted = sem("gate_shifted")
        gate_exps = sem("gate_exps")
        gates_ready = sem("gates_ready")
        phi_clamped = sem("phi_clamped")
        phi_exps = sem("phi_exps")
        phi_ready = sem("phi_ready")
        vaug_ready = sem("vaug_ready")
        xmax_ready = sem("xmax_ready")
        xrs_ready = sem("xrs_ready")
        xp_ready = sem("xp_ready")
        hexp_ready = sem("hexp_ready")
        hsum_ready = sem("hsum_ready")
        q_cleared = sem("q_cleared")
        stored = sem("stored")

        N_EARLY, N_LATE = 16, 13
        QK_DMAS = len(Q_PARTS) + len(K_PARTS)

        block = stack.enter_context(nc.Block())

        @block.sync
        def _(sp):
            def row(vec):
                return vec.rearrange("(o d) -> o d", o=1).partition_broadcast(P)

            def column(vec):
                return vec.rearrange("(d o) -> d o", o=1)

            def head_column(vec):
                return vec.rearrange("(h d) -> d h", d=HD)

            def load_x(b):
                sp.dma_start(X0[:, b % 2, :, :], x[b].rearrange("(n p) d -> p n d", p=P)
                             ).then_inc(x_loaded[b], 16)

            load_x(0)
            sp.dma_start(wqkv[:, :], L0_attn_W_qkv).then_inc(qkv_loaded, 16)
            sp.dma_start(col("q_scale"), head_column(L0_attn_q_scale),
                         allow_slow_non_contiguous=True).then_inc(qkv_loaded, 16)
            sp.dma_start(col("k_scale"), head_column(L0_attn_k_scale),
                         allow_slow_non_contiguous=True).then_inc(qkv_loaded, 16)

            early = [
                (wout[:, :], L0_attn_W_out),
                (cx[:, :, :], ctx_1024[:, 0:P, :].rearrange("b p d -> p b d")),
                (cxr[:, :, :], ctx_1024[:, P:C, :].rearrange("b p d -> p b d")),
                (xwq[:, 0, :], L0_xattn_Wq), (xwk[:, 0, :], L0_xattn_Wk),
                (xwv[:, :], L0_xattn_Wv), (xwo[:, :], L0_xattn_Wo),
                (rows[:, BV:BV + 1, :].rearrange("p o d -> p (o d)"), row(L0_xattn_bv)),
                (rows[:, BO:BO + 1, :].rearrange("p o d -> p (o d)"), row(L0_xattn_bo)),
                (rows[:, LBO:LBO + 1, :].rearrange("p o d -> p (o d)"), row(L1_attn_bo)),
                (col("xbq"), head_column(L0_xattn_bq)), (col("xbk"), head_column(L0_xattn_bk)),
                (col("lbq"), column(L1_attn_bq)), (col("lbk"), column(L1_attn_bk)),
                (col("lbv"), column(L1_attn_bv)), (col("bproj"), column(L1_xattn_b_proj)),
            ]
            assert len(early) == N_EARLY
            late = [
                (gw[:, :], L0_ffn_gate_w), (gb[:, :], row(L0_ffn_gate_b)),
                (ew[:, :, :], L0_ffn_expert_w.rearrange("e d f -> d e f")),
                (lw[:, 0, :], L1_attn_Wq), (lw[:, 1, :], L1_attn_Wk),
                (lw[:, 2, :], L1_attn_Wo), (lw[:, 3, :], L1_attn_Wv),
                (rq, L1_xattn_Wq), (rkv, L1_xattn_Wkv),
                (wp, L1_xattn_Wproj.rearrange("h e o -> e h o")),
                (fi[:, 0, :].rearrange("p (c d) -> p c d", c=HC),
                 L1_ffn_w_gate.rearrange("(c p) d -> p c d", p=P)),
                (fi[:, 1, :].rearrange("p (c d) -> p c d", c=HC),
                 L1_ffn_w_up.rearrange("(c p) d -> p c d", p=P)),
                (fi[:, 2, :], L1_ffn_w_down),
            ]
            assert len(late) == N_LATE
            for dst, src in early:
                sp.dma_start(dst, src, allow_slow_non_contiguous=True).then_inc(early_loaded, 16)
            for dst, src in late:
                sp.dma_start(dst, src).then_inc(late_loaded, 16)

            def place_parts(a, b):
                sp.wait_ge(parts_ready[a], 2 * (b + 1))
                if b == 0:
                    sp.wait_ge(q_cleared if a else zeros_ready, 1)
                n = S if a == 0 else C
                src = parts if a == 0 else xparts
                for s in range(6):
                    sp.dma_start(K6[a][HD * s:HD * s + HD, :, 0:n],
                                 src[:, 1, K_PARTS[s], 0:n]).then_inc(qk_placed[a], 16)
                    sp.dma_start(Q6[a][HD * s:HD * s + HD, :, :],
                                 src[:, 0, Q_PARTS[s], :]).then_inc(qk_placed[a], 16)

            def place_max(a, b):
                for g in range(NQ):
                    drained(sp, (b, "mT", (a, g, 0)))
                    for p in range(3):
                        sp.dma_start(
                            Q6[a][MAX_ROW + p:MAX_ROW + p + 1, 4 * g:4 * g + 4, :].rearrange(
                                "o h (n q) -> o (h n) q", q=P),
                            mrows[16 * p:16 * p + 16, g % 2, :]).then_inc(max_placed[a], 16)

            place_parts(0, 0)
            load_x(1)
            sp.wait_ge(zeros_ready, 1)
            for n in range(NB):
                sp.dma_start(eb[E * n:E * n + E, n, :], L0_ffn_expert_b).then_inc(eb_loaded, 16)
            for b in range(B):
                place_max(0, b)
                if 1 <= b < B - 1:
                    drained(sp, (b - 1, "out", 0))
                    load_x(b + 1)
                place_parts(1, b)
                if b + 1 < B:
                    place_parts(0, b + 1)
                place_max(1, b)
                sp.wait_ge(x_ready[6], NB * (b + 1))
                sp.dma_start(out[b].rearrange("(n p) d -> p n d", p=P), XB[:, :, :]
                             ).then_inc(stored, 16)
            sp.wait_ge(stored, 16 * B)

        @block.gpsimd
        def _(pool):
            done = [0]

            def step(ins):
                ins.then_inc(pool_step, 1)
                done[0] += 1
                pool.wait_ge(pool_step, done[0])

            nc.gpsimd.memset(power[:, :], -0.5)
            step(nc.gpsimd.memset(ones[:, :], 1.0))
            step(nc.gpsimd.affine_select(out=ident[:, :], in_=ones[:, :], pattern=[[-1, P]],
                                         compare_op=ALU.is_equal, fill=0.0, base=0,
                                         channel_multiplier=1))
            nc.gpsimd.tensor_copy(identb[:, :], ident[:, :])
            step(nc.gpsimd.affine_select(out=causal[:, :], in_=ones[:, :], pattern=[[1, P]],
                                         compare_op=ALU.is_ge, fill=0.0, base=0,
                                         channel_multiplier=-1))
            nc.gpsimd.tensor_scalar(maskT[:, :], causal[:, :], -1.0, -MASKED, ALU.add, ALU.mult)
            step(nc.gpsimd.affine_select(out=bvb[:, :], in_=ones[:, :], pattern=[[-1, P]],
                                         compare_op=ALU.is_ge, fill=0.0, base=0,
                                         channel_multiplier=1))
            nc.gpsimd.tensor_scalar(maskS[:, :], bvb[:, :], -1.0, -MASKED, ALU.add, ALU.mult
                                    ).then_inc(consts_ready, 1)
            for t in (Q6[0], K6[0], K6[1]):
                step(nc.gpsimd.memset(t[:, :, :].rearrange("p h t -> p (h t)").bitcast(F32), 0.0))
            for t in (K6[0], K6[1]):
                step(nc.gpsimd.memset(t[MAX_ROW:MAX_ROW + 3, :, :], 1.0))
            step(nc.gpsimd.memset(VXR[:, :, :], 0.0))
            for j in range(4):
                step(nc.gpsimd.memset(VXR[32 * j:32 * j + CR, :, 32 * j + HD:32 * j + HD + 1], 1.0))
            step(nc.gpsimd.memset(eb[:, :, :], 0.0))
            nc.gpsimd.memset(XP, 0.0)
            nc.gpsimd.memset(cT[:, :, :], 0.0)
            nc.gpsimd.memset(vaug[:, :, :], 1.0).then_inc(zeros_ready, 1)

            def root(mom, res, half, eps, ready, made, n):
                pool.wait_ge(ready, n)
                step(nc.gpsimd.tensor_scalar(res, mom, eps, None, ALU.add))
                nc.gpsimd.tensor_tensor(res, res, half, ALU.pow).then_inc(made, 1)

            def norm(n, b):
                root(moments[:, :, 1], rstd[:, :], power[:, 0:NB], LN_EPS, stats_ready[n],
                     rstd_ready[n], b + 1)

            def qk_norm(b):
                root(qkmoments[:, :, :, 1], qkrstd[:, :, :],
                     power[:, :].rearrange("p (n w) -> p n w", n=NB), QK_EPS, qk_stats_ready,
                     qk_rstd_ready, b + 1)

            def with_bias(b, src, which, n):
                pool.wait_ge(x_ready[n], NB * (b + 1))
                nc.gpsimd.tensor_tensor(XB[:, :, :], src, rows[:, which:which + 1, :].to_broadcast(
                    [P, NB, D]), ALU.add).then_inc(xb_ready, 1)

            qk_norm(0)
            for b in range(B):
                norm(0, b)
                if b == 0:
                    pool.wait_ge(early_loaded, 16 * N_EARLY)
                else:
                    pool.wait_ge(stored, 16 * b)
                with_bias(b, X[1][:, :, :], BO, 1)
                if b + 1 < B:
                    qk_norm(b + 1)
                norm(1, b)
                norm(2, b)
                with_bias(b, X[3][:, :, :], LBO, 3)
                norm(3, b)
                for u in range(2 * NB):
                    pool.wait_ge(xrs_ready, 2 * NB * b + u + 1)
                    if u >= 2 or b:
                        k, n = place[(b, "PR", u - 2) if u >= 2 else (b - 1, "PR", 2 * NB + u - 2)]
                        pool.wait_ge(bank_filled[k], n + 1)
                    for at, c0, c1 in ((0, 0, P), (4 * P, P, C)):
                        n = P if c0 == 0 else CP - P
                        last = nc.gpsimd.tensor_tensor(
                            XP[:, u % 2, at:at + 4 * n].rearrange(
                                "p (h c) -> p h c", h=4)[:, :, 0:c1 - c0],
                            XE[:, u % 2, :, c0:c1],
                            xrs[:, u % 2, :].rearrange("p (h o) -> p h o", o=1).to_broadcast(
                                [P, 4, c1 - c0]), ALU.mult)
                    last.then_inc(xp_ready, 1)
                norm(4, b)
                for c in range(HC):
                    pool.wait_ge(hexp_ready, HC * b + c + 1)
                    nc.gpsimd.tensor_scalar(hexp[:, c, :], hexp[:, c, :], 1.0, None, ALU.add
                                            ).then_inc(hsum_ready, 1)
                norm(5, b)

        @block.tensor
        def _(pe):
            def fill(key):
                k, n = place[key]
                if n:
                    pe.wait_ge(bank_drained[k], n)
                return psum[:, k, :]

            def fills_(ins, key):
                return ins.then_inc(bank_filled[place[key][0]], 1)

            mm = nc.tensor.matmul

            def transposes(key, pieces):
                to = fill(key)
                for at, src in pieces:
                    m = src.shape[0]
                    n = 1
                    for k in src.shape[1:]:
                        n *= k
                    last = nc.tensor.transpose(to[0:n, at:at + m], src, ident[0:m, 0:m])
                fills_(last, key)

            def to_features(key, src):
                transposes(key, [(P * n, src[:, n, :]) for n in range(NB)])

            def prep(b):
                pe.wait_ge(x_loaded[b], 16)
                to_features((b, "x0T", 0), X0[:, b % 2, :, :])
                drained(pe, (b, "x0T", 0))
                if b == 0:
                    pe.wait_ge(wqkv_ready, 1)
                for n in range(NB):
                    key = (b, "qkv", n)
                    fills_(mm(fill(key)[:, 0:3 * D], xT0[:, P * n:P * n + P], wqkv_p[:, :]), key)
                for w in range(2):
                    for n in range(NB):
                        drained(pe, (b, "qkv", n))
                    to_features((b, "qkT", w), qkn[:, w, :, :])

            def scores(b, a, g, u):
                to = fill((b, "S", (a, g, u)))
                pieces = (X_PIECES if a else SELF_PIECES)[u]
                for at, h, q in pieces:
                    n = C if a else P * (q + 1)
                    last = mm(to[:, at:at + n], Q6[a][0:SPLIT_ROWS, 4 * g + h, P * q:P * q + P],
                              K6[a][0:SPLIT_ROWS, 4 * g + h, 0:n], start=True, stop=bool(a))
                    if not a:
                        last = mm(to[:, at + n - P:at + n], identb[:, :], maskS[:, :],
                                  start=False, stop=True)
                fills_(last, (b, "S", (a, g, u)))

            def scores_T(b, a, g, u):
                key = (b, "ST", (a, g, u))
                to = fill(key)
                if a and u == 4:
                    for h in range(4):
                        last = mm(to[32 * h:32 * h + 32, :], K6[1][:, 4 * g + h, P:CP],
                                  Q6[1][:, 4 * g + h, :], start=True, stop=True)
                elif a:
                    last = mm(to, K6[1][:, 4 * g + u, 0:P], Q6[1][:, 4 * g + u, :],
                              start=True, stop=True)
                else:
                    for at, h, k in SELF_T_PIECES[u]:
                        n = S - P * k
                        mm(to[:, at:at + n], K6[0][:, 4 * g + h, P * k:P * k + P],
                           Q6[0][:, 4 * g + h, P * k:S], start=True, stop=False)
                        last = mm(to[:, at:at + P], identb[:, :], maskT[:, :],
                                  start=False, stop=True)
                fills_(last, key)

            def values(b, a, g):
                key = (b, "PV", (a, g, 0))
                to = fill(key)
                drained(pe, (b, "ST", (a, g, 4 if a else 9)))
                buf = g % 2
                if a:
                    for h in range(4):
                        mm(to[32 * h:32 * h + 32, :], VX[:, 4 * g + h, :], EX[:, buf, h, :],
                           start=True, stop=False, skip_group_check=True)
                    last = mm(to, VXR[:, g, :], EX[:, buf, 4, :], start=False, stop=True,
                              skip_group_check=True)
                else:
                    for k in range(NB):
                        for h in range(4):
                            for u, pieces in enumerate(SELF_T_PIECES):
                                for at, hh, kk in pieces:
                                    if (hh, kk) == (h, k):
                                        n = S - P * k
                                        last = mm(to[32 * h:32 * h + 32, P * k:S],
                                                  V[:, k, 4 * g + h, :],
                                                  EX[:, buf, u, at:at + n],
                                                  start=k == 0, stop=k == NB - 1)
                fills_(last, key)

            def attention(b, a):
                pe.wait_ge(qk_placed[a], 16 * QK_DMAS * (b + 1))
                for what, g, u in attention_steps(*((len(X_PIECES), 5) if a else (10, 10))):
                    if what == "S":
                        scores(b, a, g, u)
                    elif what == "ST":
                        if u == 0:
                            pe.wait_ge(max_placed[a], 48 * (NQ * b + g + 1))
                        scores_T(b, a, g, u)
                    elif what == "PV":
                        values(b, a, g)
                    elif what == "mT":
                        key = (b, "mT", (a, g, 0))
                        to = fill(key)
                        pe.wait_ge(mparts_ready, NQ * (2 * b + a) + g + 1)
                        fills_(nc.tensor.transpose(
                            to[0:48, 0:64].bitcast(BF16),
                            mparts[:, g % 2, :, :].rearrange("p a b -> p (a b)"),
                            identb[:, :]), key)
                    else:
                        drained(pe, (b, "PV", (a, g, 0)))
                        transposes((b, "cT", (a, g, 0)),
                                   [(P * n, pvraw[:, P * n:P * n + P]) for n in range(NB)])
                drained(pe, (b, "cT", (a, NQ - 1, 0)))
                to_features((b, "ctxT", a), ctx[:, :, :, :].rearrange("p n h d -> p n (h d)"))
                drained(pe, (b, "ctxT", a))
                key = (b, "out", a)
                to = fill(key)
                for n in range(NB):
                    last = mm(to[:, P * n:P * n + P], ctxT[:, P * n:P * n + P],
                              (xwo if a else wout)[:, :])
                fills_(last, key)

            def setup():
                pe.wait_ge(late_loaded, 16 * N_LATE)
                n = 0
                for b in range(B):
                    transposes((0, "wT", n), [(0, cx[:, b, :]), (P, cxr[:, b, :])])
                    n += 1
                for h in range(0, XH, 4):
                    for w, src in enumerate((rq, rkv[:, :, 0:D], rkv[:, :, D:2 * D])):
                        transposes((0, "wT", n), [(P * i, src[:, h + i, :]) for i in range(4)])
                        n += 1
                transposes((0, "wT", n), [(P * i, lw[:, i, :]) for i in range(3)])
                n += 1
                pe.wait_ge(ff_ready, 1)
                for i in range(3):
                    transposes((0, "wT", n), [(P * c, ff[:, i, P * c:P * c + P])
                                              for c in range(HC)])
                    n += 1
                assert n == SETUP_TRANSPOSES
                for i in range(n):
                    drained(pe, (0, "wT", i))
                for h in range(0, XH, 4):
                    key = (0, "wM", h // 2)
                    to = fill(key)
                    for i in range(4):
                        last = mm(to[:, P * i:P * i + P], whT[:, 1, h + i, :], whT[:, 0, h + i, :])
                    fills_(last, key)
                    key = (0, "wM", h // 2 + 1)
                    to = fill(key)
                    for i in range(4):
                        last = mm(to[:, P * i:P * i + P], whT[:, 2, h + i, :], wp[:, h + i, :])
                    fills_(last, key)
                key = (0, "wM", 4)
                to = fill(key)
                mm(to[:, 0:P], lw[:, 3, :], lwT[:, 2, :])
                pe.wait_ge(bvb_ready, 1)
                fills_(mm(to[:, P:2 * P], bvb[:, :], lwT[:, 2, :]), key)
                for i in range(SETUP_PRODUCTS):
                    drained(pe, (0, "wM", i))

            def context_heads(b):
                if b == 0:
                    pe.wait_ge(x0_weights_ready, 1)
                key = (b, "xk", 0)
                fills_(mm(fill(key)[:, 0:C], xwk[:, 1, :], cT[:, b, 0:C]), key)
                key = (b, "xv", 0)
                to = fill(key)
                mm(to[:, 0:P], cT[:, b, 0:P], xwv[:, :])
                for j in range(4):
                    last = mm(to[32 * j:32 * j + 32, P:2 * P], cT[:, b, P:CP], xwv[:, :])
                fills_(last, key)

            def features_of(b, n):
                pe.wait_ge(x_ready[n], NB * (b + 1))
                to_features((b, "xT", n), X[n])
                drained(pe, (b, "xT", n))

            def context_products(b):
                for n in range(XH // 2):
                    key = (b, "G", n)
                    to = fill(key)
                    for i in range(2):
                        last = mm(to[:, C * i:C * i + C], aT[:, 2 * n + i, :], cT[:, b, 0:C])
                    fills_(last, key)
                for n in range(2):
                    key = (b, "Vm", n)
                    fills_(mm(fill(key), cT[:, b, 0:P],
                              mv[:, 4 * n:4 * n + 4, :].rearrange("p h o -> p (h o)")), key)
                key = (b, "Vr", 0)
                to = fill(key)
                for g in range(2):
                    for j in range(4):
                        last = mm(to[32 * j:32 * j + 32, P * g:P * g + P], cT[:, b, P:CP],
                                  mv[:, 4 * g + j, :])
                fills_(last, key)

            def experts(b):
                key = (b, "gate", 0)
                to = fill(key)
                for n in range(NB):
                    last = mm(to[:, E * n:E * n + E], xT[2][:, P * n:P * n + P], gw[:, :])
                fills_(last, key)

                def expert(i):
                    n, half = i // 2, i % 2
                    key = (b, "ex", i)
                    fills_(mm(fill(key), xT[2][:, P * n:P * n + P],
                              ew[:, 4 * half:4 * half + 4, :].rearrange("p e d -> p (e d)")), key)

                expert(0)
                expert(1)
                pe.wait_ge(gates_ready, b + 1)
                transposes((b, "gT", 0), [(0, gl[:, :, :].rearrange("p n e -> p (n e)"))])
                drained(pe, (b, "gT", 0))
                if b == 0:
                    pe.wait_ge(eb_loaded, 16 * NB)
                key = (b, "mb", 0)
                to = fill(key)
                for n in range(NB):
                    last = mm(to[:, P * n:P * n + P], gT[:, :], eb[:, n, :])
                fills_(last, key)
                for i in range(2, 2 * NB):
                    expert(i)

            def linear(b):
                for w, what in ((1, "lk"), (0, "lq")):
                    key = (b, what, 0)
                    fills_(mm(fill(key), lwT[:, w, :], xT[3][:, :]), key)
                key = (b, "lv", 0)
                to = fill(key)
                for n in range(NB):
                    last = mm(to[:, P * n:P * n + P], xT[3][:, P * n:P * n + P], lwv[:, :])
                fills_(last, key)
                pe.wait_ge(phi_ready, 2 * b + 1)
                transposes((b, "kp", 0), [(P * n, phi[:, 1, P * n:P * n + P]) for n in range(NB)])
                pe.wait_ge(phi_ready, 2 * b + 2)
                key = (b, "A", 0)
                to = fill(key)
                for n in range(NB):
                    last = mm(to[:, P * n:P * n + P], phi[:, 1, P * n:P * n + P],
                              phi[:, 0, P * n:P * n + P])
                fills_(last, key)
                drained(pe, (b, "kp", 0))
                drained(pe, (b, "lv", 0))
                key = (b, "KV", 0)
                to = fill(key)
                for n in range(NB - 1):
                    last = mm(to[:, (D + 1) * n:(D + 1) * (n + 1)], kp[:, n, :],
                              vaug[:, n, 0:D + 1])
                fills_(last, key)
                drained(pe, (b, "A", 0))
                drained(pe, (b, "KV", 0))
                for i in range(2):
                    key = (b, "lo", i)
                    to = fill(key)
                    for n in (2 * i, 2 * i + 1):
                        at = (D + 1) * (n % 2)
                        last = mm(to[:, at:at + D + 1], AT[:, n, :], vaug[:, n, 0:D + 1],
                                  start=True, stop=n == 0)
                        if n:
                            last = mm(to[:, at:at + D + 1], phi[:, 0, P * n:P * n + P],
                                      state[:, n - 1, :], start=False, stop=True)
                    fills_(last, key)

            def cross(b):
                for u in range(2 * NB + 1):
                    if u < 2 * NB:
                        q, half = u // 2, u % 2
                        for i in range(2):
                            key = (b, "XS", 2 * u + i)
                            h = 4 * half + 2 * i
                            fills_(mm(fill(key)[:, 0:2 * C], xT[4][:, P * q:P * q + P],
                                      G[:, h:h + 2, :].rearrange("p h c -> p (h c)")), key)
                    if u >= 1:
                        v = u - 1
                        pe.wait_ge(xp_ready, 2 * NB * b + v + 1)
                        transposes((b, "PT", v), [(P * h, XP[:, v % 2, P * h:P * h + P])
                                                   for h in range(4)])
                        transposes((b, "PR", v), [(0, XP[:, v % 2, 4 * P:4 * P + P])])
                key = (b, "XO", 0)
                to = fill(key)
                for v in range(2 * NB):
                    drained(pe, (b, "PT", v))
                    drained(pe, (b, "PR", v))
                for h in range(XH):
                    mm(to, VM[:, h, :], XPT[:, h, :], start=h == 0, stop=False)
                for g in range(2):
                    last = mm(to, VR[:, g, :], XPR[:, g, :], start=False, stop=g == 1)
                fills_(last, key)
                drained(pe, (b, "XO", 0))
                transposes((b, "XOT", 0), [(P * n, xoT[:, P * n:P * n + P]) for n in range(NB)])

            def feed_forward(b):
                for c in range(HC):
                    for w in range(2):
                        key = (b, "hid", 2 * c + w)
                        fills_(mm(fill(key), fT[:, w, P * c:P * c + P], xT[5][:, :]), key)
                key = (b, "down", 0)
                to = fill(key)
                for c in range(HC):
                    drained(pe, (b, "hid", 2 * c))
                for n in range(NB):
                    for c in range(HC):
                        last = mm(to[:, P * n:P * n + P], hT[:, c, P * n:P * n + P],
                                  fT[:, 2, P * c:P * c + P], start=c == 0, stop=c == HC - 1)
                fills_(last, key)

            pe.wait_ge(consts_ready, 1)
            prep(0)
            for b in range(B):
                if b == 0:
                    pe.wait_ge(zeros_ready, 1)
                    pe.wait_ge(early_loaded, 16 * N_EARLY)
                attention(b, 0)
                if b == 0:
                    setup()
                context_heads(b)
                features_of(b, 1)
                key = (b, "xq", 0)
                fills_(mm(fill(key), xwq[:, 1, :], xT[1][:, :]), key)
                context_products(b)
                if b + 1 < B:
                    prep(b + 1)
                attention(b, 1)
                features_of(b, 2)
                experts(b)
                features_of(b, 3)
                linear(b)
                features_of(b, 4)
                cross(b)
                features_of(b, 5)
                feed_forward(b)

        @block.scalar
        def _(act):
            copy = nc.scalar.copy

            def move(dst, key, n=512, rows_=P):
                src = filled(act, key)[0:rows_, 0:n]
                drains(copy(dst, src), key)

            def prep(b):
                move(xT0[:, :], (b, "x0T", 0))
                for n in range(NB):
                    key = (b, "qkv", n)
                    src = filled(act, key)
                    copy(V[:, n, :, 0:HD], src[:, 2 * D:3 * D].rearrange("p (h d) -> p h d", d=HD)
                         ).then_inc(v_copied, 1)
                if b == 0:
                    act.wait_ge(bias_cols_ready, 1)
                for w in range(2):
                    key = (b, "qkT", w)
                    src = filled(act, key)
                    if b:
                        act.wait_ge(qk_placed[0], 16 * QK_DMAS * b)
                    scale = col(QS) if w == 0 else col("k_scale")
                    nc.scalar.activation(parts[:, w, 0, :], src, ACT.Copy, scale=scale)
                    drains(nc.scalar.activation(qkf[:, w, :], src, ACT.Copy, scale=scale), key)

            def cross_split(b, w, key, n):
                src = filled(act, key)[:, 0:n]
                if b:
                    act.wait_ge(qk_placed[1], 16 * QK_DMAS * b)
                scale = HEAD_SCALE if w == 0 else 1.0
                bias = col(XBQ) if w == 0 else col("xbk")
                nc.scalar.activation(xparts[:, w, 0, 0:n], src, ACT.Identity, bias=bias, scale=scale)
                drains(nc.scalar.activation(xf[:, w, 0:n], src, ACT.Identity, bias=bias,
                                            scale=scale), key)

            def attention(b, a):
                t_units = 5 if a else 10
                for what, g, u in attention_steps(*((len(X_PIECES), 5) if a else (10, 10))):
                    if what == "ST":
                        key = (b, "ST", (a, g, u))
                        src = filled(act, key)
                        if u == 0 and (g >= 2 or a or b):
                            prev = ((b, "PV", (a, g - 2, 0)) if g >= 2 else
                                    (b, "PV", (0, g + 2, 0)) if a else
                                    (b - 1, "PV", (1, g + 2, 0)))
                            filled(act, prev)
                        drains(nc.scalar.activation(EX[:, g % 2, u, :], src, ACT.Exp), key)
                    elif what == "mT":
                        key = (b, "mT", (a, g, 0))
                        src = filled(act, key)
                        n = NQ * b + g
                        if g >= 2:
                            act.wait_ge(max_placed[a], 48 * (n - 1))
                        drains(copy(mrows[:, g % 2, :], src[0:48, 0:64].bitcast(BF16)), key)
                    elif what == "cT":
                        key = (b, "PV", (a, g, 0))
                        src = filled(act, key)
                        drains(copy(pvraw[:, :], src), key)
                move(ctxT[:, :], (b, "ctxT", a))

            def setup():
                n = 0
                for b in range(B):
                    key = (0, "wT", n)
                    drains(copy(cT[:, b, 0:C], filled(act, key)[:, 0:C]), key)
                    n += 1
                for h in range(0, XH, 4):
                    for w in range(3):
                        move(whT[:, w, h:h + 4, :].rearrange("p h e -> p (h e)"), (0, "wT", n))
                        n += 1
                move(lwT[:, :, :].rearrange("p a b -> p (a b)"), (0, "wT", n), 3 * D)
                n += 1
                for i in range(3):
                    move(fT[:, i, :], (0, "wT", n), HID)
                    n += 1
                for h in range(0, XH, 4):
                    move(aT[:, h:h + 4, :].rearrange("p h e -> p (h e)"), (0, "wM", h // 2))
                    move(mv[:, h:h + 4, :].rearrange("p h e -> p (h e)"), (0, "wM", h // 2 + 1))
                key = (0, "wM", 4)
                src = filled(act, key)
                copy(lwv[:, :], src[:, 0:D])
                drains(copy(rows[:, LBV, :], src[:, D:2 * D]), key)

            def context_products(b):
                for n in range(XH // 2):
                    move(G[:, 2 * n:2 * n + 2, :].rearrange("p h c -> p (h c)"), (b, "G", n), 2 * C)
                for n in range(2):
                    move(VM[:, 4 * n:4 * n + 4, :].rearrange("p h o -> p (h o)"), (b, "Vm", n))
                move(VR[:, :, :].rearrange("p g o -> p (g o)"), (b, "Vr", 0), 2 * D)

            def cross(b):
                for u in range(2 * NB):
                    act.wait_ge(xmax_ready, 2 * NB * b + u + 1)
                    if u >= 2:
                        act.wait_ge(xp_ready, 2 * NB * b + u - 1)
                    for h in range(4):
                        key = (b, "XS", 2 * u + h // 2)
                        src = filled(act, key)
                        i = h % 2
                        last = nc.scalar.activation(
                            XE[:, u % 2, h, :], src[:, C * i:C * i + C], ACT.Exp,
                            bias=xbias[:, u % 2, h:h + 1], scale=X_SCALE,
                            accum_out=xsum[:, u % 2, h:h + 1])
                        if i:
                            drains(last, key)
                key = (b, "XO", 0)
                src = filled(act, key)
                drains(nc.scalar.activation(xoT, src, ACT.Identity, bias=col("bproj")), key)

            act.wait_ge(consts_ready, 1)
            prep(0)
            for b in range(B):
                attention(b, 0)
                if b == 0:
                    act.wait_ge(zeros_ready, 1)
                    setup()
                cross_split(b, 1, (b, "xk", 0), C)
                move(xT[1][:, :], (b, "xT", 1))
                cross_split(b, 0, (b, "xq", 0), S)
                context_products(b)
                if b + 1 < B:
                    prep(b + 1)
                attention(b, 1)
                move(xT[2][:, :], (b, "xT", 2))
                act.wait_ge(gate_shifted, b + 1)
                nc.scalar.activation(ge[:, :, :], gl[:, :, :], ACT.Exp).then_inc(gate_exps, 1)
                move(gT[:, :], (b, "gT", 0), P, NB * E)
                move(xT[3][:, :], (b, "xT", 3))
                for i, w in enumerate((1, 0)):
                    act.wait_ge(phi_clamped, 2 * b + i + 1)
                    nc.scalar.activation(lexp[:, w, :], lexp[:, w, :], ACT.Exp
                                         ).then_inc(phi_exps, 1)
                move(kp[:, :, :].rearrange("p n d -> p (n d)"), (b, "kp", 0))
                move(xT[4][:, :], (b, "xT", 4))
                cross(b)
                move(xT[5][:, :], (b, "xT", 5))
                for c in range(HC):
                    src = filled(act, (b, "hid", 2 * c))
                    nc.scalar.activation(hexp[:, c, :], src, ACT.Exp, scale=-1.0
                                         ).then_inc(hexp_ready, 1)

        @block.vector
        def _(dve):
            vec = nc.vector
            done = [0]

            def step(ins):
                ins.then_inc(dve_step, 1)
                done[0] += 1

            def now():
                dve.wait_ge(dve_step, done[0])

            def prep(b):
                for n in range(NB):
                    src = filled(dve, (b, "qkv", n))
                    dve.wait_ge(v_copied, NB * b + n + 1)
                    for w in range(2):
                        last = vec.bn_stats(qkstats[:, n, w, :], src[:, D * w:D * w + D])
                step(last)
                now()
                for n in range(NB):
                    for w in range(2):
                        last = vec.bn_aggr(qkmoments[:, n, w, :], qkstats[:, n, w, :])
                last.then_inc(qk_stats_ready, 1)
                dve.wait_ge(qk_rstd_ready, b + 1)
                for n in range(NB):
                    key = (b, "qkv", n)
                    for w in range(2):
                        last = vec.tensor_scalar(
                            qkn[:, w, n, :], bank(key)[:, D * w:D * w + D],
                            qkmoments[:, n, w, 0:1], qkrstd[:, n, w:w + 1],
                            ALU.subtract, ALU.mult)
                    drains(last, key)
                for w in range(2):
                    drained(dve, (b, "qkT", w))
                    split(qkf[:, w, :], rest[:, w, :], parts[:, w, :, :]
                          ).then_inc(parts_ready[0], 1)

            def split(whole, left, three):
                step(vec.tensor_tensor(left, whole, three[:, 0, :], ALU.subtract))
                now()
                step(vec.tensor_copy(three[:, 1, :], left))
                now()
                return vec.tensor_tensor(three[:, 2, :], left, three[:, 1, :], ALU.subtract)

            def norm(n, b, dst):
                now()
                for i in range(NB):
                    last = vec.bn_stats(stats[:, i, :], Y[:, i, :])
                step(last)
                now()
                for i in range(NB):
                    last = vec.bn_aggr(moments[:, i, :], stats[:, i, :])
                last.then_inc(stats_ready[n], 1)
                dve.wait_ge(rstd_ready[n], b + 1)
                for i in range(NB):
                    vec.tensor_scalar(dst[:, i, :], Y[:, i, :], moments[:, i, 0:1],
                                      rstd[:, i:i + 1], ALU.subtract, ALU.mult
                                      ).then_inc(x_ready[n + 1], 1)

            def flat(t):
                return t.rearrange("p n d -> p (n d)")

            def attention_sums(b, a):
                for what, g, u in attention_steps(*((len(X_PIECES), 5) if a else (10, 10))):
                    if what == "S":
                        key = (b, "S", (a, g, u))
                        src = filled(dve, key)
                        pieces = (X_PIECES if a else SELF_PIECES)[u]
                        if len(pieces) == 2 and pieces[0][2] == pieces[1][2]:
                            (at, h, q), (w, _, _) = pieces
                            n = C if a else w
                            drains(vec.tensor_reduce(
                                nmax[:, h:h + 2, q:q + 1],
                                src[:, 0:2 * n].rearrange("p (h k) -> p h k", h=2),
                                AX.X, ALU.max, negate=True), key)
                        else:
                            for at, h, q in pieces:
                                last = vec.tensor_reduce(
                                    nmax[:, h, q:q + 1], src[:, at:at + P * (q + 1)],
                                    AX.X, ALU.max, negate=True)
                            drains(last, key)
                        if u == len(X_PIECES if a else SELF_PIECES) - 1:
                            drained(dve, key)
                            if g >= 2:
                                filled(dve, (b, "mT", (a, g - 2, 0)))
                            m = nmax[:, :, :].rearrange("p h q -> p (h q)")
                            three = mparts[:, g % 2, :, :]
                            step(vec.tensor_copy(three[:, 0, :], m))
                            now()
                            step(vec.tensor_tensor(nrest[:, :], m, three[:, 0, :], ALU.subtract))
                            now()
                            step(vec.tensor_copy(three[:, 1, :], nrest[:, :]))
                            now()
                            vec.tensor_tensor(three[:, 2, :], nrest[:, :], three[:, 1, :],
                                              ALU.subtract).then_inc(mparts_ready, 1)
                    elif what == "cT":
                        key = (b, "cT", (a, g, 0))
                        src = filled(dve, key).rearrange("p (n h d) -> p n h d", n=NB, h=4)
                        step(vec.reciprocal(rsum[:, :, :], src[:, :, :, HD]))
                        now()
                        drains(vec.tensor_tensor(
                            ctx[:, :, 4 * g:4 * g + 4, :], src[:, :, :, 0:HD],
                            rsum[:, :, :].rearrange("p n (h o) -> p n h o", o=1).to_broadcast(
                                [P, NB, 4, HD]), ALU.mult), key)

            def attention_norm(b, a):
                key = (b, "out", a)
                src = filled(dve, key)
                if a:
                    dve.wait_ge(xb_ready, 2 * b + 1)
                    res = flat(XB[:, :, :])
                else:
                    res = flat(X0[:, b % 2, :, :])
                drains(vec.tensor_tensor(flat(Y[:, :, :]), src, res, ALU.add), key)
                drained(dve, key)
                norm(a, b, X[a + 1])

            def context_values(b):
                key = (b, "xv", 0)
                src = filled(dve, key)
                for j in range(4):
                    at = slice(32 * j, 32 * j + CR)
                    vec.tensor_tensor(
                        VXR[at, :, 32 * j:32 * j + HD],
                        src[at, P:2 * P].rearrange("p (g h d) -> p g h d", g=NQ, h=4)[:, :, j, :],
                        rows[at, BV, :].rearrange("p (g h d) -> p g h d", g=NQ, h=4)[:, :, j, :],
                        ALU.add)
                drains(vec.tensor_tensor(VX[:, :, 0:HD],
                                         src[:, 0:P].rearrange("p (h d) -> p h d", d=HD),
                                         rows[:, BV, :].rearrange("p (h d) -> p h d", d=HD),
                                         ALU.add), key)

            def gates(b):
                key = (b, "gate", 0)
                src = filled(dve, key)[:, 0:NB * E].rearrange("p (n e) -> p n e", n=NB)
                bias = gb[:, :].rearrange("p (o e) -> p o e", o=1).to_broadcast([P, NB, E])
                drains(vec.tensor_tensor(gl[:, :, :], src, bias, ALU.add), key)
                drained(dve, key)

                def over(t):
                    return t[:, :].rearrange("p (n o) -> p n o", o=1).to_broadcast([P, NB, E])

                step(vec.tensor_reduce(gs[:, :], gl[:, :, :], AX.X, ALU.max))
                now()
                vec.tensor_tensor(gl[:, :, :], gl[:, :, :], over(gs), ALU.subtract
                                  ).then_inc(gate_shifted, 1)
                dve.wait_ge(gate_exps, b + 1)
                step(vec.tensor_reduce(gs[:, :], ge[:, :, :], AX.X, ALU.add))
                now()
                step(vec.reciprocal(gr[:, :], gs[:, :]))
                now()
                step(vec.tensor_tensor(ge[:, :, :], ge[:, :, :], over(gr), ALU.mult))
                now()
                step(vec.scalar_tensor_tensor(gl[:, :, :], ge[:, :, :], 0.1, ge[:, :, :],
                                              ALU.is_ge, ALU.mult))
                now()
                step(vec.tensor_reduce(gs[:, :], gl[:, :, :], AX.X, ALU.add))
                now()
                step(vec.scalar_tensor_tensor(gr[:, :], gs[:, :], 0.0, gs[:, :],
                                              ALU.is_equal, ALU.add))
                now()
                step(vec.reciprocal(gs[:, :], gr[:, :]))
                now()
                vec.tensor_tensor(gl[:, :, :], gl[:, :, :], over(gs), ALU.mult
                                  ).then_inc(gates_ready, 1)

            def experts(b):
                gates(b)
                dve.wait_ge(gates_ready, b + 1)
                made = {}
                for n in range(0, NB, 2):
                    for e in range(E):
                        for i in (n, n + 1):
                            key = (b, "ex", 2 * i + e // 4)
                            src = filled(dve, key)
                            at = P * (e % 4)
                            if e == 4:
                                drained(dve, (b, "ex", 2 * i))
                            elif e:
                                dve.wait_ge(dve_step, made[i])
                            last = vec.scalar_tensor_tensor(
                                Y[:, i, :], src[:, at:at + P], gl[:, i, e:e + 1],
                                Y[:, i, :] if e else X[2][:, i, :], ALU.mult, ALU.add)
                            if e % 4 == 3:
                                drains(last, key)
                            else:
                                step(last)
                                made[i] = done[0]
                for n in range(NB):
                    drained(dve, (b, "ex", 2 * n + 1))
                key = (b, "mb", 0)
                src = filled(dve, key)
                drains(vec.tensor_tensor(flat(Y[:, :, :]), flat(Y[:, :, :]), src, ALU.add), key)
                drained(dve, key)
                norm(2, b, X[3])

            def linear(b):
                for w, what in ((1, "lk"), (0, "lq")):
                    key = (b, what, 0)
                    src = filled(dve, key)
                    bias = col("lbk" if w else "lbq")
                    vec.tensor_scalar(lexp[:, w, :], src, bias, 0.0, ALU.add, ALU.min
                                      ).then_inc(phi_clamped, 1)
                    drains(vec.tensor_scalar(lpos[:, w, :], src, bias, 0.0, ALU.add, ALU.max), key)
                for i, w in enumerate((1, 0)):
                    dve.wait_ge(phi_exps, 2 * b + i + 1)
                    drained(dve, (b, "lk" if w else "lq", 0))
                    vec.tensor_tensor(phi[:, w, :], lexp[:, w, :], lpos[:, w, :], ALU.add
                                      ).then_inc(phi_ready, 1)
                key = (b, "lv", 0)
                src = filled(dve, key).rearrange("p (n d) -> p n d", n=NB)
                drains(vec.tensor_tensor(vaug[:, :, 0:D], src,
                                         rows[:, LBV:LBV + 1, :].to_broadcast([P, NB, D]),
                                         ALU.add), key)
                key = (b, "A", 0)
                src = filled(dve, key).rearrange("p (n d) -> p n d", n=NB)
                drains(vec.tensor_tensor(
                    AT[:, :, :], src, causal[:, :].rearrange("p (o q) -> p o q", o=1).to_broadcast(
                        [P, NB, P]), ALU.mult), key)
                key = (b, "KV", 0)
                src = filled(dve, key)[:, 0:3 * (D + 1)].rearrange("p (n d) -> p n d", n=3)
                step(vec.tensor_copy(state[:, 0, :], src[:, 0, :]))
                now()
                step(vec.tensor_tensor(state[:, 1, :], src[:, 1, :], state[:, 0, :], ALU.add))
                now()
                drains(vec.tensor_tensor(state[:, 2, :], src[:, 2, :], state[:, 1, :], ALU.add),
                       key)
                dve.wait_ge(xb_ready, 2 * b + 2)
                for i in range(2):
                    key = (b, "lo", i)
                    src = filled(dve, key)[:, 0:2 * (D + 1)].rearrange("p (n d) -> p n d", n=2)
                    step(vec.tensor_scalar(den[:, 2 * i:2 * i + 2], src[:, :, D], 1e-6, None,
                                           ALU.add))
                    now()
                    step(vec.reciprocal(den[:, 2 * i:2 * i + 2], den[:, 2 * i:2 * i + 2]))
                    now()
                    for n in range(2):
                        m = 2 * i + n
                        last = vec.scalar_tensor_tensor(Y[:, m, :], src[:, n, 0:D],
                                                        den[:, m:m + 1], XB[:, m, :],
                                                        ALU.mult, ALU.add)
                    drains(last, key)
                drained(dve, key)
                norm(3, b, X[4])

            def cross(b):
                def front(u):
                    for i in range(2):
                        filled(dve, (b, "XS", 2 * u + i))
                    k = place[(b, "XS", 2 * u)][0]
                    src = psum[:, k:k + 2, 0:2 * C].rearrange("p a (h c) -> p a h c", h=2)
                    step(vec.tensor_reduce(
                        nxmax[:, u % 2, :].rearrange("p (a h) -> p a h", a=2), src,
                        AX.X, ALU.max, negate=True))
                    now()
                    vec.tensor_scalar(xbias[:, u % 2, :], nxmax[:, u % 2, :], X_SCALE, None,
                                      ALU.mult).then_inc(xmax_ready, 1)

                def back(u):
                    g, q = u % 2, u // 2
                    key = (b, "PT", u)
                    src = filled(dve, key).rearrange("p (h q) -> p h q", h=4)
                    drains(vec.tensor_copy(XPT[:, 4 * g:4 * g + 4, P * q:P * q + P], src), key)
                    key = (b, "PR", u)
                    src = filled(dve, key)
                    drains(vec.tensor_copy(XPR[:, g, P * q:P * q + P], src[:, 0:P]), key)

                for u in range(2 * NB):
                    front(u)
                    if u >= 1:
                        back(u - 1)
                    drained(dve, (b, "XS", 2 * u + 1))
                    vec.reciprocal(xrs[:, u % 2, :], xsum[:, u % 2, :]).then_inc(xrs_ready, 1)
                back(2 * NB - 1)
                key = (b, "XOT", 0)
                src = filled(dve, key)
                drains(vec.tensor_tensor(flat(Y[:, :, :]), src, flat(X[4][:, :, :]), ALU.add), key)
                drained(dve, key)
                norm(4, b, X[5])

            def feed_forward(b):
                for c in range(HC):
                    up, gate = (b, "hid", 2 * c + 1), (b, "hid", 2 * c)
                    dve.wait_ge(hsum_ready, HC * b + c + 1)
                    step(vec.reciprocal(hT[:, c, :], hexp[:, c, :]))
                    now()
                    src = filled(dve, up)
                    drains(vec.tensor_tensor(hT[:, c, :], src, hT[:, c, :], ALU.mult), up)
                    drained(dve, up)
                    drains(vec.tensor_tensor(hT[:, c, :], bank(gate), hT[:, c, :], ALU.mult), gate)
                key = (b, "down", 0)
                src = filled(dve, key)
                drains(vec.tensor_tensor(flat(Y[:, :, :]), src, flat(X[5][:, :, :]), ALU.add), key)
                drained(dve, key)
                norm(5, b, XB)

            def cross_split(b, w, key, n):
                drained(dve, key)
                split(xf[:, w, 0:n], xrest[:, w, 0:n], xparts[:, w, :, 0:n]
                      ).then_inc(parts_ready[1], 1)

            def by_feature(w):
                return w.rearrange("p (h d) -> p d h", d=HD)

            def by_head(w):
                return w.rearrange("p (d h) -> p d h", d=HD)

            dve.wait_ge(qkv_loaded, 48)
            for w in range(2):
                vec.tensor_copy(by_head(wqkv_p[:, D * w:D * w + D]),
                                by_feature(wqkv[:, D * w:D * w + D]))
            vec.tensor_copy(wqkv_p[:, 2 * D:3 * D], wqkv[:, 2 * D:3 * D]).then_inc(wqkv_ready, 1)
            vec.tensor_scalar(col(QS), col("q_scale"), HEAD_SCALE, None, ALU.mult
                              ).then_inc(bias_cols_ready, 1)
            vec.memset(V[:, :, :, HD:32], 0.0)
            step(vec.memset(VX[:, :, HD:32], 0.0))
            now()
            vec.memset(V[:, :, :, HD:HD + 1], 1.0)
            vec.memset(VX[:, :, HD:HD + 1], 1.0)
            prep(0)
            dve.wait_ge(early_loaded, 16 * N_EARLY)
            vec.tensor_scalar(col(XBQ), col("xbq"), HEAD_SCALE, None, ALU.mult)
            vec.tensor_copy(by_head(xwq[:, 1, :]), by_feature(xwq[:, 0, :]))
            vec.tensor_copy(by_head(xwk[:, 1, :]), by_feature(xwk[:, 0, :])
                            ).then_inc(x0_weights_ready, 1)
            for b in range(B):
                attention_sums(b, 0)
                if b == 0:
                    dve.wait_ge(late_loaded, 16 * N_LATE)
                    filled(dve, (0, "PV", (0, NQ - 1, 0)))
                    dve.wait_ge(zeros_ready, 1)
                    vec.tensor_scalar(ff, fi, 1.0 / 127.0, None, ALU.mult).then_inc(ff_ready, 1)
                    vec.tensor_copy(bvb[:, :], col("lbv").to_broadcast([P, P])
                                    ).then_inc(bvb_ready, 1)
                attention_norm(b, 0)
                if b == 0:
                    filled(dve, (0, "wM", SETUP_PRODUCTS - 1))
                    vec.memset(raw, 0.0).then_inc(q_cleared, 1)
                cross_split(b, 1, (b, "xk", 0), C)
                context_values(b)
                cross_split(b, 0, (b, "xq", 0), S)
                if b + 1 < B:
                    prep(b + 1)
                attention_sums(b, 1)
                attention_norm(b, 1)
                experts(b)
                linear(b)
                cross(b)
                feed_forward(b)


_INS = ["x", "ctx_1024", "L0_attn_W_qkv", "L0_attn_q_scale", "L0_attn_k_scale", "L0_attn_W_out",
        "L0_xattn_Wq", "L0_xattn_bq", "L0_xattn_Wk", "L0_xattn_bk", "L0_xattn_Wv", "L0_xattn_bv",
        "L0_xattn_Wo", "L0_xattn_bo", "L0_ffn_gate_w", "L0_ffn_gate_b", "L0_ffn_expert_w",
        "L0_ffn_expert_b", "L1_attn_Wq", "L1_attn_bq", "L1_attn_Wk", "L1_attn_bk", "L1_attn_Wv",
        "L1_attn_bv", "L1_attn_Wo", "L1_attn_bo", "L1_xattn_Wq", "L1_xattn_Wkv", "L1_xattn_Wproj",
        "L1_xattn_b_proj", "L1_ffn_w_gate", "L1_ffn_w_up", "L1_ffn_w_down"]


def kernel(**inputs):
    import numpy as np
    import concourse.bacc as bacc
    from concourse.bass_utils import run_bass_kernel_spmd

    nc = bacc.Bacc("TRN2", target_bir_lowering=False, num_devices=1)
    arrays, args = {}, []
    for name in _INS:
        a = np.ascontiguousarray(inputs[name])
        arrays[f"in_{name}"] = a
        args.append(nc.dram_tensor(f"in_{name}", a.shape, mybir.dt.from_np(a.dtype),
                                   kind="ExternalInput").ap())
    out = nc.dram_tensor("out", (B, S, D), F32, kind="ExternalOutput").ap()
    build(nc, *args, out)
    return run_bass_kernel_spmd(nc, [arrays], core_ids=[0]).results[0]["out"]
```

```python
from contextlib import ExitStack

import concourse.bass as bass
from concourse import mybir

F32 = mybir.dt.float32
BF16 = mybir.dt.bfloat16
I32 = mybir.dt.int32
ALU = mybir.AluOpType
ACT = mybir.ActivationFunctionType
AX = mybir.AxisListType

P = 128
B, S, D = 4, 512, 128
NB = S // P
H, HD = 16, 8
NQ = H // 4
C = 154
CR = C - P
CP = P + 32
XH = 8
E = 8
HID = 384
HC = HID // P
HEAD_SCALE = float(HD) ** -0.5
X_SCALE = float(D) ** -0.5
LN_EPS, QK_EPS = 1e-5, 1e-6
MASKED = -1e30
Q_PARTS = [0, 0, 0, 1, 1, 2]
K_PARTS = [0, 1, 2, 0, 1, 0]
SPLIT_ROWS = 96
MAX_ROW = 96


BANKS = {
    "S": (0, 1), "ST": (2, 3), "PV": (4,),
    "mT": (5,), "cT": (5,), "ctxT": (5,), "out": (4,), "x0T": (4,), "x1T": (4,),
    "xk": (2,), "xv": (3,), "xq": (1,), "qkv": (0, 1, 2, 3), "qkT": (0, 1),
    "wT": (6, 7), "wM": (6, 7),
    "x2T": (5,), "gate": (6,), "gT": (5,), "mb": (6,), "ex": (6, 7),
    "x3T": (5,), "lk": (6,), "lq": (7,), "lv": (5,), "kp": (6,), "A": (7,), "KV": (5,),
    "lo": (6, 7), "G": (6, 7), "Vm": (6, 7), "Vr": (6, 7),
    "x4T": (5,), "XS": (6, 7), "PT": (5,), "PR": (5,), "XO": (6, 7), "XOT": (6,),
    "x5T": (5,), "hid": (6, 7), "down": (6,),
}
SELF_PIECES = []
for pair in (0, 2):
    SELF_PIECES += [[(0, pair, 3)], [(0, pair + 1, 3)],
                    [(0, pair, 2), (384, pair, 0)], [(0, pair + 1, 2), (384, pair + 1, 0)],
                    [(0, pair, 1), (256, pair + 1, 1)]]
SELF_T_PIECES = ([[(0, h, 0)] for h in range(4)]
                 + [[(0, h, 1), (384, h, 3)] for h in range(4)]
                 + [[(0, h, 2), (256, h + 1, 2)] for h in (0, 2)])
PV_PARTS = ((0,), (1, 3), (2,))
X_PIECES = [[(0, pair, q), (C, pair + 1, q)] for q in range(NB) for pair in (0, 2)]
PIECES = SELF_PIECES, X_PIECES
T_UNITS = len(SELF_T_PIECES), 5
AHEAD = 4

SETUP_TRANSPOSES = B + 3 * XH // 4 + 1 + 3
SETUP_PRODUCTS = 2 * XH // 4 + 1


def attention_steps(b, a):
    units, t_units = len(PIECES[a]), T_UNITS[a]
    for t in range(NQ + 2):
        for i in range(AHEAD):
            if t < NQ:
                yield b, "S", a, t, i
            if i == 1 and t >= 2:
                yield b, "PV", a, t - 2, 2
                yield b, "PV_out", a, t - 2
        for i in range(max(units - AHEAD, t_units)):
            if t < NQ and AHEAD + i < units:
                yield b, "S", a, t, AHEAD + i
            if 1 <= t <= NQ and i < t_units:
                yield b, "ST", a, t - 1, i
            if i == 3 and t >= 2:
                yield b, "cT", a, t - 2
            if a == 0 and i == 5 and 1 <= t <= NQ:
                yield b, "PV", a, t - 1, 0
            if i == t_units - 2 and t < NQ:
                yield b, "mT", a, t
        if a == 0 and 1 <= t <= NQ:
            yield b, "PV", a, t - 1, 1
    yield b, "ctxT", a
    yield b, "out", a
    yield b, "moments", a
    yield b, "norm", a


def prep_steps(b):
    yield b, "x0T", 0
    for n in range(NB):
        yield b, "qkv", n
    yield b, "qk_moments"
    yield b, "qk_norm"
    for w in range(2):
        yield b, "qkT", w


def attentions(b):
    yield from attention_steps(b, 0)
    yield b, "xk"
    yield b, "xv"
    yield b, "x1T", 1
    if b == 0:
        yield b, "clear_q"
    yield b, "xq"
    if b + 1 < B:
        yield from prep_steps(b + 1)
    yield from attention_steps(b, 1)


def setup_steps():
    for n in range(SETUP_TRANSPOSES):
        yield 0, "wT", n
    for n in range(SETUP_PRODUCTS):
        yield 0, "wM", n


def context_steps(b):
    for n in range(XH // 2):
        yield b, "G", n
    for n in range(2):
        yield b, "Vm", n
    yield b, "Vr"


def rest_steps(b):
    yield b, "x2T", 2
    yield b, "gate"
    yield b, "gate_logits"
    yield b, "ex", 0
    yield b, "gate_exps"
    yield b, "ex", 1
    yield b, "gates"
    for n in range(NB):
        yield b, "combine", n
        if n == 0:
            yield b, "gT"
        if n + 1 < NB:
            yield b, "ex", 2 * n + 2
            yield b, "ex", 2 * n + 3
    yield b, "mb"
    yield b, "moments", 2
    yield b, "norm", 2
    yield b, "x3T", 3
    yield b, "lk"
    yield b, "lq"
    yield b, "lv"
    yield b, "phi", 1
    yield b, "phi", 0
    yield b, "kp"
    yield b, "A"
    yield b, "KV"
    yield b, "lo", 0
    yield b, "lo", 1
    yield b, "moments", 3
    for n, step in enumerate(context_steps(b)):
        if n == 1:
            yield b, "norm", 3
        if n == 5:
            yield b, "x4T", 4
        yield step
    for u in range(2 * NB + 2):
        if u < 2 * NB:
            yield b, "XS", 2 * u
        if 1 <= u <= 2 * NB:
            yield b, "sums", u - 1
        if u < 2 * NB:
            yield b, "XS", 2 * u + 1
        if u >= 2:
            yield b, "PT", u - 2
            yield b, "PR", u - 2
        if u == NB + 1:
            yield b, "XO", 0
    yield b, "XO", 1
    yield b, "XOT"
    yield b, "moments", 4
    yield b, "norm", 4
    yield b, "x5T", 5
    for c in range(HC):
        yield b, "hid", 2 * c
        yield b, "hid", 2 * c + 1
        yield b, "gated", c
    yield b, "down"
    yield b, "moments", 5
    yield b, "norm", 5


def merged(a, b):
    a, b = list(a), list(b)
    at = 0
    for i, step in enumerate(a):
        yield step
        upto = len(b) * (i + 1) // len(a)
        yield from b[at:upto]
        at = upto


def schedule():
    yield from prep_steps(0)
    for b in range(B + 1):
        if b == B:
            yield from rest_steps(b - 1)
        elif b:
            yield from merged(attentions(b), rest_steps(b - 1))
        else:
            first = list(attentions(b))
            cut = first.index((0, "ctxT", 0))
            yield from merged(first[:cut], setup_steps())
            yield from first[cut:]


def plan(steps):
    place, count, turn = {}, [0] * 8, {}
    for step in steps:
        banks = BANKS.get(step[1])
        if banks is None:
            continue
        if step[1] == "PV":
            if step[4] != 2:
                continue
            step = step[:4]
        n = turn.get(step[1], 0)
        turn[step[1]] = n + 1
        bank = banks[n % len(banks)]
        place[step] = bank, count[bank]
        count[bank] += 1
    return place


def build(nc, x, ctx_1024, L0_attn_W_qkv, L0_attn_q_scale, L0_attn_k_scale, L0_attn_W_out,
          L0_xattn_Wq, L0_xattn_bq, L0_xattn_Wk, L0_xattn_bk, L0_xattn_Wv, L0_xattn_bv,
          L0_xattn_Wo, L0_xattn_bo, L0_ffn_gate_w, L0_ffn_gate_b, L0_ffn_expert_w,
          L0_ffn_expert_b, L1_attn_Wq, L1_attn_bq, L1_attn_Wk, L1_attn_bk, L1_attn_Wv,
          L1_attn_bv, L1_attn_Wo, L1_attn_bo, L1_xattn_Wq, L1_xattn_Wkv, L1_xattn_Wproj,
          L1_xattn_b_proj, L1_ffn_w_gate, L1_ffn_w_up, L1_ffn_w_down, out):
    steps = list(schedule())
    place = plan(steps)
    with ExitStack() as stack:
        def sb(name, shape, dt=F32):
            return stack.enter_context(nc.sbuf_tensor(name, shape, dt))

        def sem(name):
            return stack.enter_context(nc.semaphore(name))

        psum = stack.enter_context(nc.psum_tensor("psum", [P, 8, 512], F32))
        bank_filled = [sem(f"bank_filled{n}") for n in range(8)]
        bank_drained = [sem(f"bank_drained{n}") for n in range(8)]

        def bank(key):
            return psum[:, place[key][0], :]

        def filled(eng, key):
            k, n = place[key]
            eng.wait_ge(bank_filled[k], n + 1)
            return psum[:, k, :]

        def drained(eng, key):
            k, n = place[key]
            eng.wait_ge(bank_drained[k], n + 1)

        def drains(ins, key):
            return ins.then_inc(bank_drained[place[key][0]], 1)

        ident = sb("ident", [P, P])
        identb = sb("identb", [P, P], BF16)
        ones = sb("ones", [P, P])
        causal = sb("causal", [P, P])
        maskS = sb("maskS", [P, P], BF16)
        maskT = sb("maskT", [P, P], BF16)
        power = sb("power", [P, 8])

        X0 = sb("X0", [P, 2, NB, D])
        X = {n: sb(name, [P, NB, D]) for n, name in ((1, "X1"), (2, "X2"), (3, "X35"), (4, "X4"))}
        X[5] = X[3]
        XB = [sb("XB_attn", [P, NB, D]), sb("XB_rest", [P, NB, D])]
        Y = [sb("Y_attn", [P, NB, D]), sb("Y_rest", [P, NB, D])]
        xT = {n: sb(name, [P, S]) for n, name in ((0, "xT01"), (2, "xT24"), (3, "xT35"))}
        xT |= {1: xT[0], 4: xT[2], 5: xT[3]}
        stats = [sb(f"stats{n}", [P, NB, 6]) for n in range(2)]
        moments = [sb(f"moments{n}", [P, NB, 2]) for n in range(2)]
        rstd = [sb(f"rstd{n}", [P, NB]) for n in range(2)]
        qkstats = sb("qkstats", [P, NB, 2, 6])
        qkmoments = sb("qkmoments", [P, NB, 2, 2])
        qkrstd = sb("qkrstd", [P, NB, 2])

        wqkv = sb("wqkv", [P, 3 * D])
        wqkv_p = sb("wqkv_p", [P, 3 * D])
        cols = sb("cols", [P, 16])
        COL = {n: i for i, n in enumerate(
            ("q_scale", "k_scale", "xbq", "xbk", "lbq", "lbk", "lbv", "bproj"))}
        QS, XBQ = 8, 9

        def col(i):
            i = COL.get(i, i)
            return cols[:, i:i + 1]

        wout = sb("wout", [P, D])
        Q6 = [sb(f"Q6_{n}", [P, H, S], BF16) for n in range(2)]
        K6 = [sb("K6_0", [P, H, S], BF16), sb("K6_1", [P, H, CP], BF16)]
        EX = sb("EX", [P, 10, 512])
        REST = sb("REST", [P, 8 * S])

        def within(t, at, n, m):
            return t[:, at:at + n * m].rearrange("p (n m) -> p n m", n=n)

        flat_ex = EX[:, :, :].rearrange("p u q -> p (u q)")
        qkf = within(flat_ex, 0, 2, S)
        rest = within(flat_ex, 2 * S, 2, S)
        qkn = within(flat_ex, 4 * S, 2, S).rearrange("p w (n d) -> p w n d", n=NB)
        lexp = within(REST, 0, 2, S)
        lpos = within(REST, 2 * S, 2, S)
        phi = within(REST, 4 * S, 2, S)
        kp = within(REST, 6 * S, NB, D)
        AT = within(REST, 7 * S, NB, P)
        XPT = within(REST, 0, XH, S // 2)
        XPR = within(REST, 4 * S, 2, S // 2)
        XE = within(REST, 5 * S, 8, C).rearrange("p (n h) c -> p n h c", n=2)
        hexp = within(REST, 0, HC, S)
        hT = within(REST, 3 * S, HC, S)
        xoT = xT[5]
        parts = sb("parts", [P, 2, 3, S], BF16)
        xparts = sb("xparts", [P, 2, 3, S], BF16)
        V = sb("V", [P, NB, H, 32])
        VX = sb("VX", [P, H, 32])
        VXR = sb("VXR", [P, NQ, P])
        nmax = sb("nmax", [P, 4, NB])
        nrest = sb("nrest", [P, 16])
        mparts = sb("mparts", [P, 2, 3, 16], BF16)
        mrows = sb("mrows", [48, 2, P], BF16)
        pvraw = sb("pvraw", [P, 512])
        rsum = sb("rsum", [P, NB, 4])
        ctx = sb("ctx", [P, NB, H, HD])
        ctxT = sb("ctxT", [P, S])

        cx = sb("cx", [P, B, D])
        cxr = sb("cxr", [CR, B, D])
        cT = sb("cT", [P, B, CP])
        xwq = sb("xwq", [P, 2, D])
        xwk = sb("xwk", [P, 2, D])
        xwv = sb("xwv", [P, D])
        xwo = sb("xwo", [P, D])
        rows = sb("rows", [P, 4, D])
        BV, BO, LBO, LBV = range(4)

        gw = sb("gw", [P, E])
        gb = sb("gb", [P, E])
        ew = sb("ew", [P, E, D])
        eb = sb("eb", [NB * E, NB, D])
        gl = sb("gl", [P, NB, E])
        ge = sb("ge", [P, NB, E])
        gs = sb("gs", [P, NB])
        gr = sb("gr", [P, NB])
        gT = sb("gT", [NB * E, P])

        lw = sb("lw", [P, 4, D])
        lwT = sb("lwT", [P, 3, D])
        lwv = sb("lwv", [P, D])
        bvb = sb("bvb", [P, P])
        vaug = sb("vaug", [P, NB, D + 2])
        state = sb("state", [P, 3, D + 1])
        den = sb("den", [P, NB])

        aT = sb("aT", [P, XH, D])
        mv = sb("mv", [P, XH, D])
        VM = sb("VM", [P, XH, D])
        VR = sb("VR", [P, 2, D])
        GP = sb("GP", [P, XH * C + 2 * 4 * CP])
        G = GP[:, 0:XH * C].rearrange("p (h c) -> p h c", h=XH)
        XP = GP[:, XH * C:].rearrange("p (n c) -> p n c", n=2)
        nxmax = sb("nxmax", [P, 2, 4])
        xbias = sb("xbias", [P, 2, 4])
        xsum = sb("xsum", [P, 2, 4])
        xrs = sb("xrs", [P, 2, 4])
        fT = sb("fT", [P, 3, HID])
        raw = Q6[1][:, :, :].rearrange("p h t -> p (h t)").bitcast(F32)
        rq = raw[:, 0:XH * D].rearrange("p (h e) -> p h e", h=XH)
        rkv = raw[:, XH * D:3 * XH * D].rearrange("p (h e) -> p h e", h=XH)
        wp = raw[:, 3 * XH * D:4 * XH * D].rearrange("p (h e) -> p h e", h=XH)
        fi = xparts[:, :, :, :].rearrange("p a b t -> p (a b t)")[:, 0:6 * HID].bitcast(
            I32).rearrange("p (w h) -> p w h", w=3)
        whT = [within(GP, 0, XH, D), within(GP, XH * D, XH, D), VM]
        ff = [t[:, :, :].rearrange("p n d -> p (n d)")[:, 0:HID] for t in (X[3], X[4], XB[1])]

        x_loaded = [sem(f"x_loaded{b}") for b in range(B)]
        qkv_loaded = sem("qkv_loaded")
        early_loaded = sem("early_loaded")
        late_loaded = sem("late_loaded")
        consts_ready = sem("consts_ready")
        zeros_ready = sem("zeros_ready")
        wqkv_ready = sem("wqkv_ready")
        x0_weights_ready = sem("x0_weights_ready")
        bias_cols_ready = sem("bias_cols_ready")
        ff_ready = sem("ff_ready")
        bvb_ready = sem("bvb_ready")
        eb_loaded = sem("eb_loaded")
        dve_step = sem("dve_step")
        pool_step = sem("pool_step")
        v_copied = sem("v_copied")
        qk_stats_ready = sem("qk_stats_ready")
        qk_rstd_ready = sem("qk_rstd_ready")
        parts_ready = [sem("parts_ready0"), sem("parts_ready1")]
        qk_placed = [sem("qk_placed0"), sem("qk_placed1")]
        mparts_ready = sem("mparts_ready")
        max_placed = [sem("max_placed0"), sem("max_placed1")]
        ex_used = sem("ex_used")
        stats_ready = [sem(f"stats_ready{n}") for n in range(6)]
        rstd_ready = [sem(f"rstd_ready{n}") for n in range(6)]
        x_ready = [None] + [sem(f"x_ready{n}") for n in range(1, 7)]
        xb_ready = [sem("xb_ready0"), sem("xb_ready1")]
        gate_shifted = sem("gate_shifted")
        gate_exps = sem("gate_exps")
        gates_ready = sem("gates_ready")
        phi_clamped = sem("phi_clamped")
        phi_exps = sem("phi_exps")
        phi_ready = sem("phi_ready")
        vaug_ready = sem("vaug_ready")
        xmax_ready = sem("xmax_ready")
        xrs_ready = sem("xrs_ready")
        xp_ready = sem("xp_ready")
        pads_ready = sem("pads_ready")
        hexp_ready = sem("hexp_ready")
        hsum_ready = sem("hsum_ready")
        q_cleared = sem("q_cleared")
        stored = sem("stored")

        N_EARLY, N_LATE = 16, 13
        QK_DMAS = len(Q_PARTS) + len(K_PARTS)

        block = stack.enter_context(nc.Block())

        @block.sync
        def _(sp):
            def row(vec):
                return vec.rearrange("(o d) -> o d", o=1).partition_broadcast(P)

            def column(vec):
                return vec.rearrange("(d o) -> d o", o=1)

            def head_column(vec):
                return vec.rearrange("(h d) -> d h", d=HD)

            def load_x(b):
                sp.dma_start(X0[:, b % 2, :, :], x[b].rearrange("(n p) d -> p n d", p=P)
                             ).then_inc(x_loaded[b], 16)

            load_x(0)
            sp.dma_start(wqkv[:, :], L0_attn_W_qkv).then_inc(qkv_loaded, 16)
            sp.dma_start(col("q_scale"), head_column(L0_attn_q_scale),
                         allow_slow_non_contiguous=True).then_inc(qkv_loaded, 16)
            sp.dma_start(col("k_scale"), head_column(L0_attn_k_scale),
                         allow_slow_non_contiguous=True).then_inc(qkv_loaded, 16)

            early = [
                (wout[:, :], L0_attn_W_out),
                (cx[:, :, :], ctx_1024[:, 0:P, :].rearrange("b p d -> p b d")),
                (cxr[:, :, :], ctx_1024[:, P:C, :].rearrange("b p d -> p b d")),
                (xwq[:, 0, :], L0_xattn_Wq), (xwk[:, 0, :], L0_xattn_Wk),
                (xwv[:, :], L0_xattn_Wv), (xwo[:, :], L0_xattn_Wo),
                (rows[:, BV:BV + 1, :].rearrange("p o d -> p (o d)"), row(L0_xattn_bv)),
                (rows[:, BO:BO + 1, :].rearrange("p o d -> p (o d)"), row(L0_xattn_bo)),
                (rows[:, LBO:LBO + 1, :].rearrange("p o d -> p (o d)"), row(L1_attn_bo)),
                (col("xbq"), head_column(L0_xattn_bq)), (col("xbk"), head_column(L0_xattn_bk)),
                (col("lbq"), column(L1_attn_bq)), (col("lbk"), column(L1_attn_bk)),
                (col("lbv"), column(L1_attn_bv)), (col("bproj"), column(L1_xattn_b_proj)),
            ]
            assert len(early) == N_EARLY
            late = [
                (gw[:, :], L0_ffn_gate_w), (gb[:, :], row(L0_ffn_gate_b)),
                (ew[:, :, :], L0_ffn_expert_w.rearrange("e d f -> d e f")),
                (lw[:, 0, :], L1_attn_Wq), (lw[:, 1, :], L1_attn_Wk),
                (lw[:, 2, :], L1_attn_Wo), (lw[:, 3, :], L1_attn_Wv),
                (rq, L1_xattn_Wq), (rkv, L1_xattn_Wkv),
                (wp, L1_xattn_Wproj.rearrange("h e o -> e h o")),
                (fi[:, 0, :].rearrange("p (c d) -> p c d", c=HC),
                 L1_ffn_w_gate.rearrange("(c p) d -> p c d", p=P)),
                (fi[:, 1, :].rearrange("p (c d) -> p c d", c=HC),
                 L1_ffn_w_up.rearrange("(c p) d -> p c d", p=P)),
                (fi[:, 2, :], L1_ffn_w_down),
            ]
            assert len(late) == N_LATE
            for dst, src in early:
                sp.dma_start(dst, src, allow_slow_non_contiguous=True).then_inc(early_loaded, 16)
            for dst, src in late:
                sp.dma_start(dst, src).then_inc(late_loaded, 16)

            def place_parts(a, b, w):
                sp.wait_ge(parts_ready[a], 2 * b + 1 + (w if a == 0 else 1 - w))
                if b == 0:
                    sp.wait_ge(zeros_ready, 1)
                    if a == 1 and w == 0:
                        sp.wait_ge(q_cleared, 1)
                n = C if a and w else S
                to = (Q6, K6)[w][a]
                for s, part in enumerate((Q_PARTS, K_PARTS)[w]):
                    sp.dma_start(to[HD * s:HD * s + HD, :, 0:n],
                                 (xparts if a else parts)[:, w, part, 0:n]
                                 ).then_inc(qk_placed[a], 16)

            def mT(b, a, g):
                drained(sp, (b, "mT", a, g))
                for p in range(3):
                    sp.dma_start(
                        Q6[a][MAX_ROW + p:MAX_ROW + p + 1, 4 * g:4 * g + 4, :].rearrange(
                            "o h (n q) -> o (h n) q", q=P),
                        mrows[16 * p:16 * p + 16, g % 2, :]).then_inc(max_placed[a], 16)

            def moments_(b, n):
                if n == 0 and b + 2 < B:
                    drained(sp, (b, "out", 0))
                    load_x(b + 2)

            def norm(b, n):
                if n == 5:
                    sp.wait_ge(x_ready[6], NB * (b + 1))
                    sp.dma_start(out[b].rearrange("(n p) d -> p n d", p=P), XB[1][:, :, :]
                                 ).then_inc(stored, 16)

            def wT(b, n):
                if n == 0:
                    sp.wait_ge(zeros_ready, 1)
                    for m in range(NB):
                        sp.dma_start(eb[E * m:E * m + E, m, :], L0_ffn_expert_b
                                     ).then_inc(eb_loaded, 16)

            load_x(1)
            work = {"qkT": lambda b, w: place_parts(0, b, w), "xk": lambda b: place_parts(1, b, 1),
                    "xq": lambda b: place_parts(1, b, 0), "mT": mT, "moments": moments_,
                    "norm": norm, "wT": wT}
            for b, what, *at in steps:
                if what in work:
                    work[what](b, *at)
            sp.wait_ge(stored, 16 * B)

        @block.gpsimd
        def _(pool):
            done = [0]

            def step(ins):
                ins.then_inc(pool_step, 1)
                done[0] += 1
                pool.wait_ge(pool_step, done[0])

            nc.gpsimd.memset(power[:, :], -0.5)
            step(nc.gpsimd.memset(ones[:, :], 1.0))
            step(nc.gpsimd.affine_select(out=ident[:, :], in_=ones[:, :], pattern=[[-1, P]],
                                         compare_op=ALU.is_equal, fill=0.0, base=0,
                                         channel_multiplier=1))
            nc.gpsimd.tensor_copy(identb[:, :], ident[:, :])
            step(nc.gpsimd.affine_select(out=causal[:, :], in_=ones[:, :], pattern=[[1, P]],
                                         compare_op=ALU.is_ge, fill=0.0, base=0,
                                         channel_multiplier=-1))
            nc.gpsimd.tensor_scalar(maskT[:, :], causal[:, :], -1.0, -MASKED, ALU.add, ALU.mult)
            step(nc.gpsimd.affine_select(out=bvb[:, :], in_=ones[:, :], pattern=[[-1, P]],
                                         compare_op=ALU.is_ge, fill=0.0, base=0,
                                         channel_multiplier=1))
            nc.gpsimd.tensor_scalar(maskS[:, :], bvb[:, :], -1.0, -MASKED, ALU.add, ALU.mult
                                    ).then_inc(consts_ready, 1)
            for t in (Q6[0], K6[0], K6[1]):
                step(nc.gpsimd.memset(t[:, :, :].rearrange("p h t -> p (h t)").bitcast(F32), 0.0))
            for t in (K6[0], K6[1]):
                step(nc.gpsimd.memset(t[MAX_ROW:MAX_ROW + 3, :, :], 1.0))
            step(nc.gpsimd.memset(VXR[:, :, :], 0.0))
            for j in range(4):
                step(nc.gpsimd.memset(VXR[32 * j:32 * j + CR, :, 32 * j + HD:32 * j + HD + 1], 1.0))
            step(nc.gpsimd.memset(eb[:, :, :], 0.0))
            nc.gpsimd.memset(cT[:, :, :], 0.0)
            nc.gpsimd.memset(vaug[:, :, :], 1.0).then_inc(zeros_ready, 1)

            def root(mom, res, half, eps, ready, made, n):
                pool.wait_ge(ready, n)
                step(nc.gpsimd.tensor_scalar(res, mom, eps, None, ALU.add))
                nc.gpsimd.tensor_tensor(res, res, half, ALU.pow).then_inc(made, 1)

            def norm(b, n):
                r = int(n >= 2)
                root(moments[r][:, :, 1], rstd[r][:, :], power[:, 0:NB], LN_EPS, stats_ready[n],
                     rstd_ready[n], b + 1)
                if n in (0, 2):
                    if n == 0 and b == 0:
                        pool.wait_ge(early_loaded, 16 * N_EARLY)
                    if n == 2 and b:
                        pool.wait_ge(stored, 16 * b)
                    pool.wait_ge(x_ready[n + 1], NB * (b + 1))
                    bias = LBO if n else BO
                    nc.gpsimd.tensor_tensor(
                        XB[r][:, :, :], X[n + 1][:, :, :],
                        rows[:, bias:bias + 1, :].to_broadcast([P, NB, D]), ALU.add
                    ).then_inc(xb_ready[r], 1)

            def qk_norm(b):
                root(qkmoments[:, :, :, 1], qkrstd[:, :, :],
                     power[:, :].rearrange("p (n w) -> p n w", n=NB), QK_EPS, qk_stats_ready,
                     qk_rstd_ready, b + 1)

            def wM(b, n):
                if n == SETUP_PRODUCTS - 1:
                    k, m = place[(b, "wM", n)]
                    pool.wait_ge(bank_filled[k], m + 1)
                    nc.gpsimd.memset(XP, 0.0).then_inc(pads_ready, 1)

            def sums(b, u):
                pool.wait_ge(xrs_ready, 2 * NB * b + u + 1)
                if u >= 2 or b:
                    k, n = place[(b, "PR", u - 2) if u >= 2 else (b - 1, "PR", 2 * NB + u - 2)]
                    pool.wait_ge(bank_filled[k], n + 1)
                for at, c0, c1 in ((0, 0, P), (4 * P, P, C)):
                    n = P if c0 == 0 else CP - P
                    last = nc.gpsimd.tensor_tensor(
                        XP[:, u % 2, at:at + 4 * n].rearrange(
                            "p (h c) -> p h c", h=4)[:, :, 0:c1 - c0],
                        XE[:, u % 2, :, c0:c1],
                        xrs[:, u % 2, :].rearrange("p (h o) -> p h o", o=1).to_broadcast(
                            [P, 4, c1 - c0]), ALU.mult)
                last.then_inc(xp_ready, 1)

            def hid(b, i):
                if i % 2 == 1:
                    c = i // 2
                    pool.wait_ge(hexp_ready, HC * b + c + 1)
                    nc.gpsimd.tensor_scalar(hexp[:, c, :], hexp[:, c, :], 1.0, None, ALU.add
                                            ).then_inc(hsum_ready, 1)

            work = {"norm": norm, "qk_norm": qk_norm, "wM": wM, "sums": sums, "hid": hid}
            for b, what, *at in steps:
                if what in work:
                    work[what](b, *at)

        @block.tensor
        def _(pe):
            def fill(key):
                k, n = place[key]
                if n:
                    pe.wait_ge(bank_drained[k], n)
                return psum[:, k, :]

            def fills_(ins, key):
                return ins.then_inc(bank_filled[place[key][0]], 1)

            mm = nc.tensor.matmul

            def transposes(key, pieces):
                to = fill(key)
                for at, src in pieces:
                    m = src.shape[0]
                    n = 1
                    for k in src.shape[1:]:
                        n *= k
                    last = nc.tensor.transpose(to[0:n, at:at + m], src, ident[0:m, 0:m])
                fills_(last, key)

            def to_features(key, src):
                transposes(key, [(P * n, src[:, n, :]) for n in range(NB)])

            def x_T(b, n):
                if n == 0:
                    pe.wait_ge(x_loaded[b], 16)
                    src = X0[:, b % 2, :, :]
                else:
                    pe.wait_ge(x_ready[n], NB * (b + 1))
                    src = X[n]
                to_features((b, f"x{n}T", n), src)

            def qkv(b, n):
                if n == 0:
                    drained(pe, (b, "x0T", 0))
                    if b == 0:
                        pe.wait_ge(wqkv_ready, 1)
                key = (b, "qkv", n)
                fills_(mm(fill(key)[:, 0:3 * D], xT[0][:, P * n:P * n + P], wqkv_p[:, :]), key)

            def qkT(b, w):
                if w == 0:
                    for n in range(NB):
                        drained(pe, (b, "qkv", n))
                to_features((b, "qkT", w), qkn[:, w, :, :])

            def scores(b, a, g, u):
                if g == u == 0:
                    if b == a == 0:
                        pe.wait_ge(zeros_ready, 1)
                    pe.wait_ge(qk_placed[a], 16 * QK_DMAS * (b + 1))
                key = (b, "S", a, g, u)
                to = fill(key)
                for at, h, q in PIECES[a][u]:
                    n = C if a else P * (q + 1)
                    last = mm(to[:, at:at + n], Q6[a][0:SPLIT_ROWS, 4 * g + h, P * q:P * q + P],
                              K6[a][0:SPLIT_ROWS, 4 * g + h, 0:n], start=True, stop=bool(a))
                    if not a:
                        last = mm(to[:, at + n - P:at + n], identb[:, :], maskS[:, :],
                                  start=False, stop=True)
                fills_(last, key)

            def scores_T(b, a, g, u):
                if u == 0:
                    pe.wait_ge(max_placed[a], 48 * (NQ * b + g + 1))
                key = (b, "ST", a, g, u)
                to = fill(key)
                if a and u == 4:
                    for h in range(4):
                        last = mm(to[32 * h:32 * h + 32, :], K6[1][:, 4 * g + h, P:CP],
                                  Q6[1][:, 4 * g + h, :], start=True, stop=True)
                elif a:
                    last = mm(to, K6[1][:, 4 * g + u, 0:P], Q6[1][:, 4 * g + u, :],
                              start=True, stop=True)
                else:
                    for at, h, k in SELF_T_PIECES[u]:
                        n = S - P * k
                        mm(to[:, at:at + n], K6[0][:, 4 * g + h, P * k:P * k + P],
                           Q6[0][:, 4 * g + h, P * k:S], start=True, stop=False)
                        last = mm(to[:, at:at + P], identb[:, :], maskT[:, :],
                                  start=False, stop=True)
                fills_(last, key)

            def values(b, a, g, part):
                key = (b, "PV", a, g)
                if part == 0 or a:
                    fill(key)
                to = bank(key)
                if a:
                    drained(pe, (b, "ST", 1, g, 4))
                    if g == 0:
                        drained(pe, (b, "xv"))
                    at = 5 * (g % 2)
                    for h in range(4):
                        mm(to[32 * h:32 * h + 32, :], VX[:, 4 * g + h, :], EX[:, at + h, :],
                           start=True, stop=False, skip_group_check=True)
                    fills_(mm(to, VXR[:, g, :], EX[:, at + 4, :], start=False, stop=True,
                              skip_group_check=True), key)
                    return
                drained(pe, (b, "ST", 0, g, (3, 7, 9)[part]))
                for k in PV_PARTS[part]:
                    for h in range(4):
                        n = S - P * k
                        u, at = [(u, at) for u, pieces in enumerate(SELF_T_PIECES)
                                 for at, hh, kk in pieces if (hh, kk) == (h, k)][0]
                        last = mm(to[32 * h:32 * h + 32, P * k:S], V[:, k, 4 * g + h, :],
                                  EX[:, u, at:at + n], start=part == 0, stop=part == 2)
                if part == 2:
                    fills_(last, key)
                else:
                    last.then_inc(ex_used, 1)

            def max_T(b, a, g):
                key = (b, "mT", a, g)
                to = fill(key)
                pe.wait_ge(mparts_ready, NQ * (2 * b + a) + g + 1)
                fills_(nc.tensor.transpose(to[0:48, 0:64].bitcast(BF16),
                                           mparts[:, g % 2, :, :].rearrange("p a b -> p (a b)"),
                                           identb[:, :]), key)

            def products_T(b, a, g):
                drained(pe, (b, "PV", a, g))
                transposes((b, "cT", a, g), [(P * n, pvraw[:, P * n:P * n + P])
                                             for n in range(NB)])

            def ctx_T(b, a):
                drained(pe, (b, "cT", a, NQ - 1))
                to_features((b, "ctxT", a), ctx[:, :, :, :].rearrange("p n h d -> p n (h d)"))

            def out_product(b, a):
                drained(pe, (b, "ctxT", a))
                if b == a == 0:
                    pe.wait_ge(early_loaded, 16 * N_EARLY)
                key = (b, "out", a)
                to = fill(key)
                for n in range(NB):
                    last = mm(to[:, P * n:P * n + P], ctxT[:, P * n:P * n + P],
                              (xwo if a else wout)[:, :])
                fills_(last, key)

            def setup_T(b, n):
                key = (b, "wT", n)
                if n == 0:
                    pe.wait_ge(early_loaded, 16 * N_EARLY)
                if n < B:
                    transposes(key, [(0, cx[:, n, :]), (P, cxr[:, n, :])])
                    return
                if n == B:
                    pe.wait_ge(late_loaded, 16 * N_LATE)
                n -= B
                if n < 6:
                    h, src = 4 * (n // 3), (rq, rkv[:, :, 0:D], rkv[:, :, D:2 * D])[n % 3]
                    transposes(key, [(P * i, src[:, h + i, :]) for i in range(4)])
                elif n == 6:
                    transposes(key, [(P * i, lw[:, i, :]) for i in range(3)])
                else:
                    pe.wait_ge(ff_ready, 1)
                    transposes(key, [(P * c, ff[n - 7][:, P * c:P * c + P]) for c in range(HC)])

            def setup_products(b, n):
                if n == 0:
                    for i in range(SETUP_TRANSPOSES):
                        drained(pe, (b, "wT", i))
                key = (b, "wM", n)
                to = fill(key)
                if n == 4:
                    mm(to[:, 0:P], lw[:, 3, :], lwT[:, 2, :])
                    last = mm(to[:, P:2 * P], bvb[:, :], lwT[:, 2, :])
                for i in range(4 if n < 4 else 0):
                    h = 4 * (n // 2) + i
                    last = (mm(to[:, P * i:P * i + P], whT[1][:, h, :], whT[0][:, h, :])
                            if n % 2 == 0 else
                            mm(to[:, P * i:P * i + P], whT[2][:, h, :], wp[:, h, :]))
                fills_(last, key)

            def cross_k(b):
                if b == 0:
                    pe.wait_ge(x0_weights_ready, 1)
                    for n in range(B):
                        drained(pe, (0, "wT", n))
                key = (b, "xk")
                fills_(mm(fill(key)[:, 0:C], xwk[:, 1, :], cT[:, b, 0:C]), key)

            def cross_v(b):
                key = (b, "xv")
                to = fill(key)
                mm(to[:, 0:P], cT[:, b, 0:P], xwv[:, :])
                for j in range(4):
                    last = mm(to[32 * j:32 * j + 32, P:2 * P], cT[:, b, P:CP], xwv[:, :])
                fills_(last, key)

            def cross_q(b):
                drained(pe, (b, "x1T", 1))
                key = (b, "xq")
                fills_(mm(fill(key), xwq[:, 1, :], xT[1][:, :]), key)


            def context_keys(b, n):
                if b == n == 0:
                    for i in range(SETUP_PRODUCTS):
                        drained(pe, (0, "wM", i))
                key = (b, "G", n)
                to = fill(key)
                for i in range(2):
                    last = mm(to[:, C * i:C * i + C], aT[:, 2 * n + i, :], cT[:, b, 0:C])
                fills_(last, key)

            def context_values(b, n):
                key = (b, "Vm", n)
                fills_(mm(fill(key), cT[:, b, 0:P],
                          mv[:, 4 * n:4 * n + 4, :].rearrange("p h o -> p (h o)")), key)

            def context_rest(b):
                key = (b, "Vr")
                to = fill(key)
                for g in range(2):
                    for j in range(4):
                        last = mm(to[32 * j:32 * j + 32, P * g:P * g + P], cT[:, b, P:CP],
                                  mv[:, 4 * g + j, :])
                fills_(last, key)

            def gate(b):
                drained(pe, (b, "x2T", 2))
                if b == 0:
                    pe.wait_ge(late_loaded, 16 * N_LATE)
                key = (b, "gate")
                to = fill(key)
                for n in range(NB):
                    last = mm(to[:, E * n:E * n + E], xT[2][:, P * n:P * n + P], gw[:, :])
                fills_(last, key)

            def expert(b, i):
                n, half = i // 2, i % 2
                key = (b, "ex", i)
                fills_(mm(fill(key), xT[2][:, P * n:P * n + P],
                          ew[:, 4 * half:4 * half + 4, :].rearrange("p e d -> p (e d)")), key)

            def gates_T(b):
                pe.wait_ge(gates_ready, b + 1)
                transposes((b, "gT"), [(0, gl[:, :, :].rearrange("p n e -> p (n e)"))])

            def expert_biases(b):
                drained(pe, (b, "gT"))
                if b == 0:
                    pe.wait_ge(eb_loaded, 16 * NB)
                key = (b, "mb")
                to = fill(key)
                for n in range(NB):
                    last = mm(to[:, P * n:P * n + P], gT[:, :], eb[:, n, :])
                fills_(last, key)

            def linear_qk(b, w):
                if w == 1:
                    drained(pe, (b, "x3T", 3))
                key = (b, ("lq", "lk")[w])
                fills_(mm(fill(key), lwT[:, w, :], xT[3][:, :]), key)

            def linear_v(b):
                key = (b, "lv")
                to = fill(key)
                for n in range(NB):
                    last = mm(to[:, P * n:P * n + P], xT[3][:, P * n:P * n + P], lwv[:, :])
                fills_(last, key)

            def linear_k_T(b):
                pe.wait_ge(phi_ready, 2 * b + 1)
                transposes((b, "kp"), [(P * n, phi[:, 1, P * n:P * n + P]) for n in range(NB)])

            def linear_within(b):
                pe.wait_ge(phi_ready, 2 * b + 2)
                key = (b, "A")
                to = fill(key)
                for n in range(NB):
                    last = mm(to[:, P * n:P * n + P], phi[:, 1, P * n:P * n + P],
                              phi[:, 0, P * n:P * n + P])
                fills_(last, key)

            def linear_states(b):
                drained(pe, (b, "kp"))
                drained(pe, (b, "lv"))
                key = (b, "KV")
                to = fill(key)
                for n in range(NB - 1):
                    last = mm(to[:, (D + 1) * n:(D + 1) * (n + 1)], kp[:, n, :],
                              vaug[:, n, 0:D + 1])
                fills_(last, key)

            def linear_out(b, i):
                drained(pe, (b, "A"))
                drained(pe, (b, "KV"))
                key = (b, "lo", i)
                to = fill(key)
                for n in (2 * i, 2 * i + 1):
                    at = (D + 1) * (n % 2)
                    last = mm(to[:, at:at + D + 1], AT[:, n, :], vaug[:, n, 0:D + 1],
                              start=True, stop=n == 0)
                    if n:
                        last = mm(to[:, at:at + D + 1], phi[:, 0, P * n:P * n + P],
                                  state[:, n - 1, :], start=False, stop=True)
                fills_(last, key)

            def cross_scores(b, i):
                if i == 0:
                    drained(pe, (b, "x4T", 4))
                    for n in range(XH // 2):
                        drained(pe, (b, "G", n))
                q, h = i // 4, 2 * (i % 4)
                key = (b, "XS", i)
                fills_(mm(fill(key)[:, 0:2 * C], xT[4][:, P * q:P * q + P],
                          G[:, h:h + 2, :].rearrange("p h c -> p (h c)")), key)

            def cross_T(b, u):
                pe.wait_ge(xp_ready, 2 * NB * b + u + 1)
                transposes((b, "PT", u), [(P * h, XP[:, u % 2, P * h:P * h + P])
                                          for h in range(4)])

            def cross_rest_T(b, u):
                transposes((b, "PR", u), [(0, XP[:, u % 2, 4 * P:5 * P])])

            def cross_out(b, half):
                for u in range(NB * half, NB * half + NB):
                    drained(pe, (b, "PT", u))
                    drained(pe, (b, "PR", u))
                if half == 0:
                    for n in range(2):
                        drained(pe, (b, "Vm", n))
                    drained(pe, (b, "Vr"))
                key = (b, "XO", half)
                to = fill(key)[:, 0:S // 2]
                for h in range(XH):
                    mm(to, VM[:, h, :], XPT[:, h, :], start=h == 0, stop=False)
                for g in range(2):
                    last = mm(to, VR[:, g, :], XPR[:, g, :], start=False, stop=g == 1)
                fills_(last, key)

            def cross_out_T(b):
                for half in range(2):
                    drained(pe, (b, "XO", half))
                transposes((b, "XOT"), [(P * n, xoT[:, P * n:P * n + P]) for n in range(NB)])

            def hidden(b, i):
                c, w = i // 2, i % 2
                if i == 0:
                    drained(pe, (b, "x5T", 5))
                key = (b, "hid", i)
                fills_(mm(fill(key), fT[:, w, P * c:P * c + P], xT[5][:, :]), key)

            def down(b):
                for c in range(HC):
                    drained(pe, (b, "hid", 2 * c))
                key = (b, "down")
                to = fill(key)
                for n in range(NB):
                    for c in range(HC):
                        last = mm(to[:, P * n:P * n + P], hT[:, c, P * n:P * n + P],
                                  fT[:, 2, P * c:P * c + P], start=c == 0, stop=c == HC - 1)
                fills_(last, key)

            work = {"qkv": qkv, "qkT": qkT, "S": scores, "ST": scores_T, "PV": values,
                    "mT": max_T, "cT": products_T, "ctxT": ctx_T, "out": out_product,
                    "wT": setup_T, "wM": setup_products, "xk": cross_k, "xv": cross_v,
                    "xq": cross_q, "G": context_keys, "Vm": context_values, "Vr": context_rest,
                    "gate": gate, "ex": expert, "gT": gates_T, "mb": expert_biases,
                    "lk": lambda b: linear_qk(b, 1), "lq": lambda b: linear_qk(b, 0),
                    "lv": linear_v, "kp": linear_k_T, "A": linear_within, "KV": linear_states,
                    "lo": linear_out, "XS": cross_scores, "PT": cross_T, "PR": cross_rest_T,
                    "XO": cross_out, "XOT": cross_out_T, "hid": hidden, "down": down}
            work |= {f"x{n}T": x_T for n in range(6)}
            pe.wait_ge(consts_ready, 1)
            for b, what, *at in steps:
                if what in work:
                    work[what](b, *at)

        @block.scalar
        def _(act):
            copy = nc.scalar.copy

            def move(dst, key, n=512, rows_=P):
                src = filled(act, key)[0:rows_, 0:n]
                drains(copy(dst, src), key)

            def flat(t):
                return t.rearrange("p a b -> p (a b)")

            def qkv(b, n):
                src = filled(act, (b, "qkv", n))
                copy(V[:, n, :, 0:HD], src[:, 2 * D:3 * D].rearrange("p (h d) -> p h d", d=HD)
                     ).then_inc(v_copied, 1)

            def qkT(b, w):
                key = (b, "qkT", w)
                src = filled(act, key)
                if b == w == 0:
                    act.wait_ge(bias_cols_ready, 1)
                if b:
                    act.wait_ge(qk_placed[0], 16 * QK_DMAS * b)
                scale = col(QS) if w == 0 else col("k_scale")
                nc.scalar.activation(parts[:, w, 0, :], src, ACT.Copy, scale=scale)
                drains(nc.scalar.activation(qkf[:, w, :], src, ACT.Copy, scale=scale), key)

            def cross_split(b, w):
                key = (b, ("xq", "xk")[w])
                n = (S, C)[w]
                src = filled(act, key)[:, 0:n]
                if b:
                    act.wait_ge(qk_placed[1], 16 * QK_DMAS * b)
                scale = HEAD_SCALE if w == 0 else 1.0
                bias = col(XBQ) if w == 0 else col("xbk")
                nc.scalar.activation(xparts[:, w, 0, 0:n], src, ACT.Identity, bias=bias,
                                     scale=scale)
                drains(nc.scalar.activation(qkf[:, w, 0:n], src, ACT.Identity, bias=bias,
                                            scale=scale), key)

            def exponentials(b, a, g, u):
                key = (b, "ST", a, g, u)
                src = filled(act, key)
                if a == 0 and g == 0:
                    if u == 0 and b:
                        filled(act, (b - 1, "PV", 1, NQ - 1))
                elif a == 0 and u in (0, 4):
                    act.wait_ge(ex_used, 2 * (NQ * b + g - 1) + (1 if u == 0 else 2))
                elif a == 0 and u == 8:
                    filled(act, (b, "PV", 0, g - 1))
                elif a and u == 0 and g != 1:
                    filled(act, (b, "PV", 1, g - 2) if g else (b, "PV", 0, NQ - 1))
                slot = 5 * (g % 2) + u if a else u
                drains(nc.scalar.activation(EX[:, slot, :], src, ACT.Exp), key)

            def max_T(b, a, g):
                key = (b, "mT", a, g)
                src = filled(act, key)
                if g >= 2:
                    act.wait_ge(max_placed[a], 48 * (NQ * b + g - 1))
                drains(copy(mrows[:, g % 2, :], src[0:48, 0:64].bitcast(BF16)), key)

            def setup_T(b, n):
                key = (b, "wT", n)
                if n < B:
                    if n == 0:
                        act.wait_ge(zeros_ready, 1)
                    drains(copy(cT[:, n, 0:C], filled(act, key)[:, 0:C]), key)
                elif n < B + 6:
                    h, w = 4 * ((n - B) // 3), (n - B) % 3
                    move(flat(whT[w][:, h:h + 4, :]), key)
                elif n == B + 6:
                    move(flat(lwT[:, :, :]), key, 3 * D)
                else:
                    move(fT[:, n - B - 7, :], key, HID)

            def setup_products(b, n):
                key = (b, "wM", n)
                if n < 4:
                    move(flat((aT, mv)[n % 2][:, 4 * (n // 2):4 * (n // 2) + 4, :]), key)
                else:
                    src = filled(act, key)
                    copy(lwv[:, :], src[:, 0:D])
                    drains(copy(rows[:, LBV, :], src[:, D:2 * D]), key)

            def gate_exps_(b):
                act.wait_ge(gate_shifted, b + 1)
                nc.scalar.activation(ge[:, :, :], gl[:, :, :], ACT.Exp).then_inc(gate_exps, 1)

            def phi_(b, w):
                act.wait_ge(phi_clamped, 2 * b + 2 - w)
                nc.scalar.activation(lexp[:, w, :], lexp[:, w, :], ACT.Exp).then_inc(phi_exps, 1)

            def cross_exps(b, i):
                u = i // 2
                act.wait_ge(xmax_ready, 4 * NB * b + i + 1)
                if i % 2 == 0 and u >= 2:
                    act.wait_ge(xp_ready, 2 * NB * b + u - 1)
                key = (b, "XS", i)
                src = filled(act, key)
                for j in range(2):
                    h = 2 * (i % 2) + j
                    last = nc.scalar.activation(
                        XE[:, u % 2, h, :], src[:, C * j:C * j + C], ACT.Exp,
                        bias=xbias[:, u % 2, h:h + 1], scale=X_SCALE,
                        accum_out=xsum[:, u % 2, h:h + 1])
                drains(last, key)

            def cross_T(b, u):
                key = (b, "PT", u)
                g, at = u % 2, P * (u // 2 % 2)
                src = filled(act, key).rearrange("p (h q) -> p h q", h=4)
                if u == NB:
                    filled(act, (b, "XO", 0))
                drains(copy(XPT[:, 4 * g:4 * g + 4, at:at + P], src), key)

            def cross_rest_T(b, u):
                g, at = u % 2, P * (u // 2 % 2)
                move(XPR[:, g, at:at + P], (b, "PR", u), P)

            def cross_out(b, half):
                key = (b, "XO", half)
                src = filled(act, key)[:, 0:S // 2]
                drains(nc.scalar.activation(xoT[:, S // 2 * half:S // 2 * (half + 1)], src,
                                            ACT.Identity, bias=col("bproj")), key)

            def hidden(b, i):
                if i % 2 == 0:
                    src = filled(act, (b, "hid", i))
                    nc.scalar.activation(hexp[:, i // 2, :], src, ACT.Exp, scale=-1.0
                                         ).then_inc(hexp_ready, 1)

            work = {"qkv": qkv, "qkT": qkT, "xk": lambda b: cross_split(b, 1),
                    "xq": lambda b: cross_split(b, 0), "ST": exponentials, "mT": max_T,
                    "PV_out": lambda b, a, g: move(pvraw[:, :], (b, "PV", a, g)),
                    "ctxT": lambda b, a: move(ctxT[:, :], (b, "ctxT", a)),
                    "wT": setup_T, "wM": setup_products,
                    "G": lambda b, n: move(flat(G[:, 2 * n:2 * n + 2, :]), (b, "G", n), 2 * C),
                    "Vm": lambda b, n: move(flat(VM[:, 4 * n:4 * n + 4, :]), (b, "Vm", n)),
                    "Vr": lambda b: move(flat(VR[:, :, :]), (b, "Vr"), 2 * D),
                    "gate_exps": gate_exps_,
                    "gT": lambda b: move(gT[:, :], (b, "gT"), P, NB * E), "phi": phi_,
                    "kp": lambda b: move(flat(kp), (b, "kp")), "XS": cross_exps,
                    "PT": cross_T, "PR": cross_rest_T, "XO": cross_out, "hid": hidden}
            work |= {f"x{n}T": lambda b, n: move(xT[n][:, :], (b, f"x{n}T", n))
                     for n in range(6)}
            act.wait_ge(consts_ready, 1)
            for b, what, *at in steps:
                if what in work:
                    work[what](b, *at)

        @block.vector
        def _(dve):
            vec = nc.vector
            done = [0]

            def step(ins):
                ins.then_inc(dve_step, 1)
                done[0] += 1

            def now():
                dve.wait_ge(dve_step, done[0])

            def flat(t):
                return t.rearrange("p n d -> p (n d)")

            def qk_moments(b):
                for n in range(NB):
                    src = filled(dve, (b, "qkv", n))
                    dve.wait_ge(v_copied, NB * b + n + 1)
                    for w in range(2):
                        last = vec.bn_stats(qkstats[:, n, w, :], src[:, D * w:D * w + D])
                step(last)
                now()
                for n in range(NB):
                    for w in range(2):
                        last = vec.bn_aggr(qkmoments[:, n, w, :], qkstats[:, n, w, :])
                last.then_inc(qk_stats_ready, 1)

            def qk_norm(b):
                dve.wait_ge(qk_rstd_ready, b + 1)
                for n in range(NB):
                    key = (b, "qkv", n)
                    for w in range(2):
                        last = vec.tensor_scalar(
                            qkn[:, w, n, :], bank(key)[:, D * w:D * w + D],
                            qkmoments[:, n, w, 0:1], qkrstd[:, n, w:w + 1],
                            ALU.subtract, ALU.mult)
                    drains(last, key)

            def split(whole, left, three, ready):
                step(vec.tensor_tensor(left, whole, three[:, 0, :], ALU.subtract))
                now()
                step(vec.tensor_copy(three[:, 1, :], left))
                now()
                vec.tensor_tensor(three[:, 2, :], left, three[:, 1, :], ALU.subtract
                                  ).then_inc(ready, 1)

            def qkT(b, w):
                drained(dve, (b, "qkT", w))
                split(qkf[:, w, :], rest[:, w, :], parts[:, w, :, :], parts_ready[0])

            def cross_split(b, w):
                n = (S, C)[w]
                drained(dve, (b, ("xq", "xk")[w]))
                split(qkf[:, w, 0:n], rest[:, w, 0:n], xparts[:, w, :, 0:n], parts_ready[1])

            def maxima(b, a, g, u):
                key = (b, "S", a, g, u)
                src = filled(dve, key)
                pieces = PIECES[a][u]
                if len(pieces) == 2 and pieces[0][2] == pieces[1][2]:
                    (_, h, q), (w, _, _) = pieces
                    drains(vec.tensor_reduce(
                        nmax[:, h:h + 2, q:q + 1],
                        src[:, 0:2 * w].rearrange("p (h k) -> p h k", h=2),
                        AX.X, ALU.max, negate=True), key)
                else:
                    for at, h, q in pieces:
                        last = vec.tensor_reduce(nmax[:, h, q:q + 1], src[:, at:at + P * (q + 1)],
                                                 AX.X, ALU.max, negate=True)
                    drains(last, key)
                if u == len(PIECES[a]) - 1:
                    drained(dve, key)
                    if g >= 2:
                        filled(dve, (b, "mT", a, g - 2))
                    m = nmax[:, :, :].rearrange("p h q -> p (h q)")
                    three = mparts[:, g % 2, :, :]
                    step(vec.tensor_copy(three[:, 0, :], m))
                    now()
                    step(vec.tensor_tensor(nrest[:, :], m, three[:, 0, :], ALU.subtract))
                    now()
                    step(vec.tensor_copy(three[:, 1, :], nrest[:, :]))
                    now()
                    vec.tensor_tensor(three[:, 2, :], nrest[:, :], three[:, 1, :],
                                      ALU.subtract).then_inc(mparts_ready, 1)

            def divided(b, a, g):
                key = (b, "cT", a, g)
                src = filled(dve, key).rearrange("p (n h d) -> p n h d", n=NB, h=4)
                step(vec.reciprocal(rsum[:, :, :], src[:, :, :, HD]))
                now()
                drains(vec.tensor_tensor(
                    ctx[:, :, 4 * g:4 * g + 4, :], src[:, :, :, 0:HD],
                    rsum[:, :, :].rearrange("p n (h o) -> p n h o", o=1).to_broadcast(
                        [P, NB, 4, HD]), ALU.mult), key)

            def moments_(b, n):
                r = int(n >= 2)
                y = Y[r]
                if n == 3:
                    linear_sum(b)
                else:
                    key = (b, "out", n) if n < 2 else (b, {2: "mb", 4: "XOT", 5: "down"}[n])
                    src = filled(dve, key)
                    if n == 1:
                        dve.wait_ge(xb_ready[0], b + 1)
                    if n == 2:
                        for i in range(NB):
                            drained(dve, (b, "ex", 2 * i + 1))
                    res = {0: X0[:, b % 2, :, :], 1: XB[0][:, :, :], 2: y[:, :, :]}.get(n)
                    if res is None:
                        res = X[n][:, :, :]
                    drains(vec.tensor_tensor(flat(y[:, :, :]), src, flat(res), ALU.add), key)
                    drained(dve, key)
                for i in range(NB):
                    last = vec.bn_stats(stats[r][:, i, :], y[:, i, :])
                step(last)
                now()
                for i in range(NB):
                    last = vec.bn_aggr(moments[r][:, i, :], stats[r][:, i, :])
                last.then_inc(stats_ready[n], 1)

            def norm(b, n):
                r = int(n >= 2)
                dst = XB[1] if n == 5 else X[n + 1]
                dve.wait_ge(rstd_ready[n], b + 1)
                for i in range(NB):
                    vec.tensor_scalar(dst[:, i, :], Y[r][:, i, :], moments[r][:, i, 0:1],
                                      rstd[r][:, i:i + 1], ALU.subtract, ALU.mult
                                      ).then_inc(x_ready[n + 1], 1)

            def setup_T(b, n):
                if n == SETUP_TRANSPOSES - 4:
                    dve.wait_ge(late_loaded, 16 * N_LATE)
                    for i in range(3):
                        vec.tensor_scalar(ff[i], fi[:, i, :], 1.0 / 127.0, None, ALU.mult)
                    vec.tensor_copy(bvb[:, :], col("lbv").to_broadcast([P, P])
                                    ).then_inc(ff_ready, 1)

            def clear_q(b):
                filled(dve, (b, "wM", SETUP_PRODUCTS - 1))
                vec.memset(raw, 0.0).then_inc(q_cleared, 1)

            def cross_v(b):
                key = (b, "xv")
                src = filled(dve, key)
                for j in range(4):
                    at = slice(32 * j, 32 * j + CR)
                    vec.tensor_tensor(
                        VXR[at, :, 32 * j:32 * j + HD],
                        src[at, P:2 * P].rearrange("p (g h d) -> p g h d", g=NQ, h=4)[:, :, j, :],
                        rows[at, BV, :].rearrange("p (g h d) -> p g h d", g=NQ, h=4)[:, :, j, :],
                        ALU.add)
                drains(vec.tensor_tensor(VX[:, :, 0:HD],
                                         src[:, 0:P].rearrange("p (h d) -> p h d", d=HD),
                                         rows[:, BV, :].rearrange("p (h d) -> p h d", d=HD),
                                         ALU.add), key)

            def over(t):
                return t[:, :].rearrange("p (n o) -> p n o", o=1).to_broadcast([P, NB, E])

            def gate_logits(b):
                key = (b, "gate")
                src = filled(dve, key)[:, 0:NB * E].rearrange("p (n e) -> p n e", n=NB)
                bias = gb[:, :].rearrange("p (o e) -> p o e", o=1).to_broadcast([P, NB, E])
                drains(vec.tensor_tensor(gl[:, :, :], src, bias, ALU.add), key)
                drained(dve, key)
                step(vec.tensor_reduce(gs[:, :], gl[:, :, :], AX.X, ALU.max))
                now()
                vec.tensor_tensor(gl[:, :, :], gl[:, :, :], over(gs), ALU.subtract
                                  ).then_inc(gate_shifted, 1)

            def gates(b):
                dve.wait_ge(gate_exps, b + 1)
                step(vec.tensor_reduce(gs[:, :], ge[:, :, :], AX.X, ALU.add))
                now()
                step(vec.reciprocal(gr[:, :], gs[:, :]))
                now()
                step(vec.tensor_tensor(ge[:, :, :], ge[:, :, :], over(gr), ALU.mult))
                now()
                step(vec.scalar_tensor_tensor(gl[:, :, :], ge[:, :, :], 0.1, ge[:, :, :],
                                              ALU.is_ge, ALU.mult))
                now()
                step(vec.tensor_reduce(gs[:, :], gl[:, :, :], AX.X, ALU.add))
                now()
                step(vec.scalar_tensor_tensor(gr[:, :], gs[:, :], 0.0, gs[:, :],
                                              ALU.is_equal, ALU.add))
                now()
                step(vec.reciprocal(gs[:, :], gr[:, :]))
                now()
                vec.tensor_tensor(gl[:, :, :], gl[:, :, :], over(gs), ALU.mult
                                  ).then_inc(gates_ready, 1)

            def combine(b, n):
                if n == 0:
                    dve.wait_ge(gates_ready, b + 1)
                y = Y[1][:, n, :]
                for e in range(E):
                    key = (b, "ex", 2 * n + e // 4)
                    src = filled(dve, key)
                    if e == 4:
                        drained(dve, (b, "ex", 2 * n))
                    elif e:
                        now()
                    at = P * (e % 4)
                    last = vec.scalar_tensor_tensor(y, src[:, at:at + P], gl[:, n, e:e + 1],
                                                    y if e else X[2][:, n, :],
                                                    ALU.mult, ALU.add)
                    if e % 4 == 3:
                        drains(last, key)
                    else:
                        step(last)

            def clamp(b, w):
                key = (b, ("lq", "lk")[w])
                src = filled(dve, key)
                bias = col("lbk" if w else "lbq")
                vec.tensor_scalar(lexp[:, w, :], src, bias, 0.0, ALU.add, ALU.min
                                  ).then_inc(phi_clamped, 1)
                drains(vec.tensor_scalar(lpos[:, w, :], src, bias, 0.0, ALU.add, ALU.max), key)

            def phi_(b, w):
                dve.wait_ge(phi_exps, 2 * b + 2 - w)
                drained(dve, (b, ("lq", "lk")[w]))
                vec.tensor_tensor(phi[:, w, :], lexp[:, w, :], lpos[:, w, :], ALU.add
                                  ).then_inc(phi_ready, 1)

            def linear_v(b):
                key = (b, "lv")
                src = filled(dve, key).rearrange("p (n d) -> p n d", n=NB)
                drains(vec.tensor_tensor(vaug[:, :, 0:D], src,
                                         rows[:, LBV:LBV + 1, :].to_broadcast([P, NB, D]),
                                         ALU.add), key)

            def linear_mask(b):
                key = (b, "A")
                src = filled(dve, key).rearrange("p (n d) -> p n d", n=NB)
                drains(vec.tensor_tensor(
                    AT, src, causal[:, :].rearrange("p (o q) -> p o q", o=1).to_broadcast(
                        [P, NB, P]), ALU.mult), key)

            def linear_states(b):
                key = (b, "KV")
                src = filled(dve, key)[:, 0:3 * (D + 1)].rearrange("p (n d) -> p n d", n=3)
                step(vec.tensor_copy(state[:, 0, :], src[:, 0, :]))
                now()
                step(vec.tensor_tensor(state[:, 1, :], src[:, 1, :], state[:, 0, :], ALU.add))
                now()
                drains(vec.tensor_tensor(state[:, 2, :], src[:, 2, :], state[:, 1, :], ALU.add),
                       key)

            def linear_sum(b):
                dve.wait_ge(xb_ready[1], b + 1)
                for i in range(2):
                    key = (b, "lo", i)
                    src = filled(dve, key)[:, 0:2 * (D + 1)].rearrange("p (n d) -> p n d", n=2)
                    step(vec.tensor_scalar(den[:, 2 * i:2 * i + 2], src[:, :, D], 1e-6, None,
                                           ALU.add))
                    now()
                    step(vec.reciprocal(den[:, 2 * i:2 * i + 2], den[:, 2 * i:2 * i + 2]))
                    now()
                    for n in range(2):
                        m = 2 * i + n
                        last = vec.scalar_tensor_tensor(Y[1][:, m, :], src[:, n, 0:D],
                                                        den[:, m:m + 1], XB[1][:, m, :],
                                                        ALU.mult, ALU.add)
                    drains(last, key)
                drained(dve, key)

            def cross_maxima(b, i):
                u, at = i // 2, 2 * (i % 2)
                src = filled(dve, (b, "XS", i))[:, 0:2 * C].rearrange("p (h c) -> p h c", h=2)
                step(vec.tensor_reduce(nxmax[:, u % 2, at:at + 2], src, AX.X, ALU.max,
                                       negate=True))
                now()
                vec.tensor_scalar(xbias[:, u % 2, at:at + 2], nxmax[:, u % 2, at:at + 2], X_SCALE,
                                  None, ALU.mult).then_inc(xmax_ready, 1)

            def sums(b, u):
                drained(dve, (b, "XS", 2 * u + 1))
                vec.reciprocal(xrs[:, u % 2, :], xsum[:, u % 2, :]).then_inc(xrs_ready, 1)

            def gated(b, c):
                gate, up = (b, "hid", 2 * c), (b, "hid", 2 * c + 1)
                dve.wait_ge(hsum_ready, HC * b + c + 1)
                step(vec.reciprocal(hT[:, c, :], hexp[:, c, :]))
                now()
                src = filled(dve, up)
                drains(vec.tensor_tensor(hT[:, c, :], src, hT[:, c, :], ALU.mult), up)
                drained(dve, up)
                drains(vec.tensor_tensor(hT[:, c, :], bank(gate), hT[:, c, :], ALU.mult), gate)

            def by_feature(w):
                return w.rearrange("p (h d) -> p d h", d=HD)

            def by_head(w):
                return w.rearrange("p (d h) -> p d h", d=HD)

            dve.wait_ge(qkv_loaded, 48)
            for w in range(2):
                vec.tensor_copy(by_head(wqkv_p[:, D * w:D * w + D]),
                                by_feature(wqkv[:, D * w:D * w + D]))
            vec.tensor_copy(wqkv_p[:, 2 * D:3 * D], wqkv[:, 2 * D:3 * D]).then_inc(wqkv_ready, 1)
            vec.tensor_scalar(col(QS), col("q_scale"), HEAD_SCALE, None, ALU.mult
                              ).then_inc(bias_cols_ready, 1)
            vec.memset(V[:, :, :, HD:32], 0.0)
            step(vec.memset(VX[:, :, HD:32], 0.0))
            now()
            vec.memset(V[:, :, :, HD:HD + 1], 1.0)
            vec.memset(VX[:, :, HD:HD + 1], 1.0)

            def cross_weights():
                dve.wait_ge(early_loaded, 16 * N_EARLY)
                vec.tensor_scalar(col(XBQ), col("xbq"), HEAD_SCALE, None, ALU.mult)
                vec.tensor_copy(by_head(xwq[:, 1, :]), by_feature(xwq[:, 0, :]))
                vec.tensor_copy(by_head(xwk[:, 1, :]), by_feature(xwk[:, 0, :])
                                ).then_inc(x0_weights_ready, 1)

            work = {"qk_moments": qk_moments, "qk_norm": qk_norm, "qkT": qkT,
                    "xk": lambda b: cross_split(b, 1), "xq": lambda b: cross_split(b, 0),
                    "xv": cross_v, "S": maxima, "cT": divided, "moments": moments_,
                    "norm": norm, "wT": setup_T, "clear_q": clear_q,
                    "gate_logits": gate_logits, "gates": gates, "combine": combine,
                    "lk": lambda b: clamp(b, 1), "lq": lambda b: clamp(b, 0), "phi": phi_,
                    "lv": linear_v, "A": linear_mask, "KV": linear_states,
                    "XS": cross_maxima, "sums": sums, "gated": gated}
            for b, what, *at in steps:
                if (b, what, *at) == (0, "xk"):
                    cross_weights()
                if what in work:
                    work[what](b, *at)


_INS = ["x", "ctx_1024", "L0_attn_W_qkv", "L0_attn_q_scale", "L0_attn_k_scale", "L0_attn_W_out",
        "L0_xattn_Wq", "L0_xattn_bq", "L0_xattn_Wk", "L0_xattn_bk", "L0_xattn_Wv", "L0_xattn_bv",
        "L0_xattn_Wo", "L0_xattn_bo", "L0_ffn_gate_w", "L0_ffn_gate_b", "L0_ffn_expert_w",
        "L0_ffn_expert_b", "L1_attn_Wq", "L1_attn_bq", "L1_attn_Wk", "L1_attn_bk", "L1_attn_Wv",
        "L1_attn_bv", "L1_attn_Wo", "L1_attn_bo", "L1_xattn_Wq", "L1_xattn_Wkv", "L1_xattn_Wproj",
        "L1_xattn_b_proj", "L1_ffn_w_gate", "L1_ffn_w_up", "L1_ffn_w_down"]


def kernel(**inputs):
    import numpy as np
    import concourse.bacc as bacc
    from concourse.bass_utils import run_bass_kernel_spmd

    nc = bacc.Bacc("TRN2", target_bir_lowering=False, num_devices=1)
    arrays, args = {}, []
    for name in _INS:
        a = np.ascontiguousarray(inputs[name])
        arrays[f"in_{name}"] = a
        args.append(nc.dram_tensor(f"in_{name}", a.shape, mybir.dt.from_np(a.dtype),
                                   kind="ExternalInput").ap())
    out = nc.dram_tensor("out", (B, S, D), F32, kind="ExternalOutput").ap()
    build(nc, *args, out)
    return run_bass_kernel_spmd(nc, [arrays], core_ids=[0]).results[0]["out"]
```

```python
from contextlib import ExitStack

import numpy as np

import concourse.bass as bass
from concourse import mybir

F32 = mybir.dt.float32
BF16 = mybir.dt.bfloat16
I32 = mybir.dt.int32
ALU = mybir.AluOpType
ACT = mybir.ActivationFunctionType
AX = mybir.AxisListType

P = 128
B, S, D = 4, 512, 128
NB = S // P
H, HD = 16, 8
NQ = H // 4
C = 154
CR = C - P
CP = P + 32
XH = 8
E = 8
HID = 384
HC = HID // P
HEAD_SCALE = float(HD) ** -0.5
X_SCALE = float(D) ** -0.5
LN_EPS, QK_EPS = 1e-5, 1e-6
MASKED = -1e30
Q_PARTS = [0, 0, 0, 1, 1, 2]
K_PARTS = [0, 1, 2, 0, 1, 0]
SPLIT_ROWS = 96
MAX_ROW = 96

DVE_BLOCKS, ACT_BLOCKS = (0, 1), (2, 3)

TWO_ONES = float(np.array([0x3F803F80], np.uint32).view(np.float32)[0])


BANKS = {
    "S": (0, 1), "ST": (2, 3), "PV": (4,),
    "mT": (0, 1), "cT": (4,), "ctxT": (4, 5), "out": (5, 6, 7), "x0T": (6, 7), "x1T": (6,),
    "xk": (0, 1, 2), "xv": (5,), "xq": (5, 6, 7), "qkv": (0, 1, 2, 3), "qkT": (0, 1),
    "wT": (7,), "wM": (6, 7),
    "x2T": (5, 6, 7), "gate": (5,), "gT": (2, 3), "mb": (3,), "ex": (6, 7),
    "x3T": (1,), "lk": (6,), "lq": (1,), "lv": (5,), "kp": (5,), "A": (2,), "KV": (0, 1, 2, 3),
    "lo": (6, 7), "G": (6, 7), "Vm": (6, 7), "Vr": (0, 1, 2),
    "x4T": (0,), "XS": (6, 7), "PT": (5,), "PR": (6, 7), "XO": (5, 6, 7), "XOT": (6, 7),
    "x5T": (0,), "hid": (6, 7), "down": (5,),
}
WEIGHT = {
    "A": 0.85, "KV": 1.2, "PR 5": 0.5, "PT 0": 1.4, "PT 1": 0.85, "PT 7": 0.72, "PV": 0.5,
    "Vm 1": 1.4, "XO": 0.5, "XOT": 1.2, "XS": 0.5, "XS 15": 0.35, "XS 5": 0.3, "XS 6": 0.25,
    "XS 9": 0.6, "cT": 0.85, "clear_q": 0.84, "gate_exps": 1.2, "gated": 2, "gates": 0.26,
    "lv": 1.2, "mT": 2.77, "mb": 1.39, "moments": 0.7, "moments 1": 0.59, "moments 3": 0.41,
    "norm 0": 1.2, "norm 2": 1.2, "placing": 1.4, "qkT": 0.7, "qkT 1": 0.42,
    "qk_moments": 0.41, "qk_norm": 1.2, "sums 2": 1.4, "sums 7": 0.59, "wM": 0.99,
    "wM 0": 0.11, "wM 1": 0.15, "wM 2": 1.21, "wM 3": 0.21, "wM 4": 0.42, "wT": 2.8,
    "wT 1": 2.35, "wT 10": 4, "wT 12": 7.85, "wT 13": 2.77, "wT 2": 2.38, "wT 3": 2.35,
    "wT 4": 2.86, "wT 5": 2.38, "wT 6": 9.24, "wT 7": 1.4, "wT 8": 6.47, "wT 9": 0.69,
    "x0T": 0.3, "x0T 0": 0.49, "x1T": 0.42, "x2T": 0.5, "x2T 2": 0.85, "x3T": 0.5, "x4T": 0.42,
    "xq": 1.2, "xv": 0.7,
}
SELF_PIECES = []
for pair in (0, 2):
    SELF_PIECES += [[(0, pair, 3)], [(0, pair + 1, 3)],
                    [(0, pair, 2), (384, pair, 0)], [(0, pair + 1, 2), (384, pair + 1, 0)],
                    [(0, pair, 1), (256, pair + 1, 1)]]
SELF_T_PIECES = ([[(0, h, 0)] for h in range(4)]
                 + [[(0, h, 1), (384, h, 3)] for h in range(4)]
                 + [[(0, h, 2), (256, h + 1, 2)] for h in (0, 2)])
PV_PARTS = ((0,), (1, 3), (2,))
X_PIECES = [[(0, pair, q), (C, pair + 1, q)] for q in range(NB) for pair in (0, 2)]
PIECES = SELF_PIECES, X_PIECES
T_UNITS = len(SELF_T_PIECES), 5
AHEAD = 4

SETUP_TRANSPOSES = B + 3 * XH // 4 + 1 + 3
SETUP_PRODUCTS = 2 * XH // 4 + 1


def attention_steps(b, a, turns):
    units, t_units = len(PIECES[a]), T_UNITS[a]
    for t in turns:
        for i in range(AHEAD):
            if t < NQ:
                yield b, "S", a, t, i
            if i == 1 and t >= 2:
                yield b, "PV", a, t - 2, 2
                yield b, "PV_out", a, t - 2
        for i in range(max(units - AHEAD, t_units)):
            if t < NQ and AHEAD + i < units:
                yield b, "S", a, t, AHEAD + i
            if 1 <= t <= NQ and i < t_units:
                yield b, "ST", a, t - 1, i
            if i == 3 and t >= 2:
                yield b, "cT", a, t - 2
            if a == 0 and i == 5 and 1 <= t <= NQ:
                yield b, "PV", a, t - 1, 0
            if i == t_units - 2 and t < NQ:
                yield b, "mT", a, t
        if a == 0 and 1 <= t <= NQ:
            yield b, "PV", a, t - 1, 1


def finish_steps(b, a):
    yield b, "ctxT", a
    yield b, "out", a
    yield b, "moments", a
    yield b, "norm", a


def prep_steps(b):
    yield b, "x0T", 0
    for n in range(NB):
        yield b, "qkv", n
    yield b, "qk_moments"
    yield b, "qk_norm"
    for w in range(2):
        yield b, "qkT", w


def between_steps(b):
    own = list(attention_steps(b, 0, [NQ + 1])) + list(finish_steps(b, 0))
    if b == 0:
        own.append((b, "clear_q"))
    own += [(b, "x1T", 1), (b, "xq"),
            (b, "placing")]
    yield from merged(own, prep_steps(b + 1) if b + 1 < B else [])


def attentions(b):
    yield from attention_steps(b, 0, [1])
    yield b, "xk"
    yield b, "xv"
    yield from attention_steps(b, 0, range(2, NQ + 1))
    yield from between_steps(b)
    yield from attention_steps(b, 1, range(NQ))
    end = list(attention_steps(b, 1, range(NQ, NQ + 2))) + list(finish_steps(b, 1))
    yield from merged(end, attention_steps(b + 1, 0, [0]) if b + 1 < B else [])


def setup_steps():
    for n in range(SETUP_TRANSPOSES):
        yield 0, "wT", n
    for n in range(SETUP_PRODUCTS):
        yield 0, "wM", n


def context_steps(b):
    for n in range(XH // 2):
        yield b, "G", n
    for n in range(2):
        yield b, "Vm", n
    yield b, "Vr"


def rest_steps(b):
    yield b, "x2T", 2
    yield b, "gate"
    yield b, "gate_logits"
    yield b, "ex", 0
    yield b, "gate_exps"
    yield b, "ex", 1
    yield b, "gates"
    for n in range(NB):
        yield b, "combine", n
        if n == 0:
            yield b, "gT"
        if n + 1 < NB:
            yield b, "ex", 2 * n + 2
            yield b, "ex", 2 * n + 3
    yield b, "mb"
    yield b, "moments", 2
    yield b, "norm", 2
    yield b, "x3T", 3
    yield b, "lk"
    yield b, "lq"
    yield b, "lv"
    yield b, "phi", 1
    yield b, "phi", 0
    yield b, "kp"
    yield b, "A"
    yield b, "KV"
    yield b, "lo", 0
    yield b, "lo", 1
    yield b, "moments", 3
    for n, step in enumerate(context_steps(b)):
        if n == 1:
            yield b, "norm", 3
        if n == 5:
            yield b, "x4T", 4
        yield step
    for u in range(2 * NB + 2):
        if u < 2 * NB:
            yield b, "XS", 2 * u
        if 1 <= u <= 2 * NB:
            yield b, "sums", u - 1
        if u < 2 * NB:
            yield b, "XS", 2 * u + 1
        if u >= 2:
            yield b, "PT", u - 2
            yield b, "PR", u - 2
        if u == NB + 1:
            yield b, "XO", 0
    yield b, "XO", 1
    yield b, "XOT"
    yield b, "moments", 4
    yield b, "norm", 4
    yield b, "x5T", 5
    for c in range(HC):
        yield b, "hid", 2 * c
        yield b, "hid", 2 * c + 1
        yield b, "gated", c
    yield b, "down"
    yield b, "moments", 5
    yield b, "norm", 5


def places(steps):
    ends, at = [], 0.0
    for step in steps:
        at += WEIGHT.get(f"{step[1]} {step[2]}" if len(step) > 2 else step[1],
                         WEIGHT.get(step[1], 1.0))
        ends.append(at)
    return [end / at for end in ends] if ends else []


def merged(a, b):
    a, b = list(a), list(b)
    row = [(at, 0, step) for at, step in zip(places(a), a)]
    row += [(at, 1, step) for at, step in zip(places(b), b)]
    row.sort(key=lambda entry: entry[:2])
    yield from (step for _, _, step in row)


def schedule():
    yield from prep_steps(0)
    yield from attention_steps(0, 0, [0])
    for b in range(B + 1):
        if b == B:
            yield from rest_steps(b - 1)
        elif b:
            yield from merged(attentions(b), rest_steps(b - 1))
        else:
            first = list(attentions(b))
            cut = first.index((0, "PV", 0, NQ - 1, 2))
            yield from merged(first[:cut], setup_steps())
            yield from first[cut:]


def plan(steps):
    place, count, turn = {}, [0] * 8, {}
    for step in steps:
        banks = BANKS.get(step[1])
        if banks is None:
            continue
        if step[1] == "PV":
            if step[4] != 2:
                continue
            step = step[:4]
        n = turn.get(banks, 0)
        turn[banks] = n + 1
        bank = banks[n % len(banks)]
        place[step] = bank, count[bank]
        count[bank] += 1
    return place


def build(nc, x, ctx_1024, L0_attn_W_qkv, L0_attn_q_scale, L0_attn_k_scale, L0_attn_W_out,
          L0_xattn_Wq, L0_xattn_bq, L0_xattn_Wk, L0_xattn_bk, L0_xattn_Wv, L0_xattn_bv,
          L0_xattn_Wo, L0_xattn_bo, L0_ffn_gate_w, L0_ffn_gate_b, L0_ffn_expert_w,
          L0_ffn_expert_b, L1_attn_Wq, L1_attn_bq, L1_attn_Wk, L1_attn_bk, L1_attn_Wv,
          L1_attn_bv, L1_attn_Wo, L1_attn_bo, L1_xattn_Wq, L1_xattn_Wkv, L1_xattn_Wproj,
          L1_xattn_b_proj, L1_ffn_w_gate, L1_ffn_w_up, L1_ffn_w_down, out):
    steps = list(schedule())
    place = plan(steps)
    with ExitStack() as stack:
        def sb(name, shape, dt=F32):
            return stack.enter_context(nc.sbuf_tensor(name, shape, dt))

        def sem(name):
            return stack.enter_context(nc.semaphore(name))

        psum = stack.enter_context(nc.psum_tensor("psum", [P, 8, 512], F32))
        bank_filled = [sem(f"bank_filled{n}") for n in range(8)]
        bank_drained = [sem(f"bank_drained{n}") for n in range(8)]

        def bank(key):
            return psum[:, place[key][0], :]

        def filled(eng, key):
            k, n = place[key]
            eng.wait_ge(bank_filled[k], n + 1)
            return psum[:, k, :]

        def drained(eng, key):
            k, n = place[key]
            eng.wait_ge(bank_drained[k], n + 1)

        def drains(ins, key):
            return ins.then_inc(bank_drained[place[key][0]], 1)

        def before(b, a, g):
            n = NQ * (2 * b + a) + g - 2
            return (n // (2 * NQ), n // NQ % 2, n % NQ) if n >= 0 else None

        REST = sb("REST", [P, 8 * S])

        def within(t, at, n, m):
            return t[:, at:at + n * m].rearrange("p (n m) -> p n m", n=n)

        wqkv = REST[:, 0:3 * D]
        xw_raw = within(REST, 3 * D, 2, D)
        ones, bvb = within(REST, 5 * D, 2, P)[:, 0, :], within(REST, 5 * D, 2, P)[:, 1, :]
        ident = sb("ident", [P, P])
        identb = sb("identb", [P, P], BF16)
        power = sb("power", [P, 8])
        zero = sb("zero", [P, 1])
        causal = sb("causal", [P, P])
        maskS = sb("maskS", [P, P], BF16)
        maskT = sb("maskT", [P, P], BF16)

        X0 = sb("X0", [P, 2, NB, D])
        X = {n: sb(name, [P, NB, D]) for n, name in ((1, "X1"), (2, "X2"), (3, "X35"), (4, "X4"))}
        X[5] = X[3]
        XB = [sb("XB_attn", [P, NB, D]), sb("XB_rest", [P, NB, D])]
        Y = [sb("Y_attn", [P, NB, D]), sb("Y_rest", [P, NB, D])]
        xT = {n: sb(name, [P, S]) for n, name in ((0, "xT01"), (2, "xT24"), (3, "xT35"))}
        xT |= {1: xT[0], 4: xT[2], 5: xT[3]}
        stats = [sb(f"stats{n}", [P, NB, 6]) for n in range(2)]
        moments = [sb(f"moments{n}", [P, NB, 2]) for n in range(2)]
        rstd = [sb(f"rstd{n}", [P, NB]) for n in range(2)]
        shift = [sb(f"shift{n}", [P, NB]) for n in range(2)]
        qkstats = sb("qkstats", [P, NB, 2, 6])
        qkmoments = sb("qkmoments", [P, NB, 2, 2])
        qkrstd = sb("qkrstd", [P, NB, 2])
        qkshift = sb("qkshift", [P, NB, 2])

        wqkv_p = sb("wqkv_p", [P, 3 * D])
        cols = sb("cols", [P, 16])
        COL = {n: i for i, n in enumerate(
            ("q_scale", "k_scale", "xbq", "xbk", "lbq", "lbk", "lbv", "bproj"))}
        QS, XBQ = 8, 9

        def col(i):
            i = COL.get(i, i)
            return cols[:, i:i + 1]

        wout = sb("wout", [P, D])
        Q6 = [sb(f"Q6_{n}", [P, H, S], BF16) for n in range(2)]
        K6 = [sb("K6_0", [P, H, S], BF16), sb("K6_1", [P, H, CP], BF16)]
        EX = sb("EX", [P, 10, 512])

        flat_ex = EX[:, :, :].rearrange("p u q -> p (u q)")
        xqf = flat_ex[:, 0:S]
        lexp = within(REST, 0, 2, S)
        lpos = within(REST, 2 * S, 2, S)
        phi = within(REST, 4 * S, 2, S)
        kp = within(REST, 6 * S, NB, D)
        AT = within(REST, 7 * S, NB, P)
        XPT = within(REST, 0, XH, S // 2)
        XPR = within(REST, 4 * S, 2, S // 2)
        XE = within(REST, 5 * S, 8, C).rearrange("p (n h) c -> p n h c", n=2)
        htanh = within(REST, 0, HC, S)
        hT = within(REST, 3 * S, HC, S)
        xoT = xT[5]
        parts = sb("parts", [P, 2, 3, S], BF16)
        fi = sb("fi", [P, 3, HID], I32)
        flat_fi = fi[:, :, :].rearrange("p w h -> p (w h)")
        xparts = sb("xparts", [P, 3, S], BF16)
        xkparts = sb("xkparts", [P, 3, C], BF16)
        xkf = sb("xkf", [P, C])
        left = sb("left", [P, S])
        qkn = flat_fi.bitcast(F32)[:, 0:2 * S].rearrange("p (w n d) -> p w n d", w=2, n=NB)
        V = sb("V", [P, NB, H, 32])
        VX = sb("VX", [P, H, 32])
        VXR = sb("VXR", [P, NQ, P])
        nmax = sb("nmax", [P, 4, NB])
        nrest = sb("nrest", [P, 16])
        mparts = sb("mparts", [P, 2, 3, 16], BF16)
        mrows = sb("mrows", [48, 2, P], BF16)
        pvraw = sb("pvraw", [P, 512])
        rsum = sb("rsum", [P, NB, 4])
        ctx = sb("ctx", [P, NB, H, HD])
        ctxT = sb("ctxT", [P, S])

        cx = sb("cx", [P, B, D])
        cxr = sb("cxr", [CR, B, D])
        cT = sb("cT", [P, B, CP])
        xwq = sb("xwq", [P, D])
        xwk = sb("xwk", [P, D])
        xwv = sb("xwv", [P, D])
        xwo = sb("xwo", [P, D])
        rows = sb("rows", [P, 4, D])
        BV, BO, LBO, LBV = range(4)

        gw = sb("gw", [P, E])
        gb = sb("gb", [P, E])
        ew = sb("ew", [P, E, D])
        eb = sb("eb", [NB * E, NB, D])
        gl = sb("gl", [P, NB, E])
        ge = sb("ge", [P, NB, E])
        gs = sb("gs", [P, NB])
        gr = sb("gr", [P, NB])
        gT = sb("gT", [NB * E, P])

        lw = sb("lw", [P, 4, D])
        lwT = sb("lwT", [P, 3, D])
        lwv = sb("lwv", [P, D])
        vaug = sb("vaug", [P, NB, D + 2])
        state = sb("state", [P, 3, D + 1])
        den = sb("den", [P, NB])

        aT = sb("aT", [P, XH, D])
        mv = sb("mv", [P, XH, D])
        VM = sb("VM", [P, XH, D])
        VR = sb("VR", [P, 2, D])
        GP = sb("GP", [P, XH * C + 2 * 4 * CP])
        G = GP[:, 0:XH * C].rearrange("p (h c) -> p h c", h=XH)
        XP = GP[:, XH * C:].rearrange("p (n c) -> p n c", n=2)
        nxmax = sb("nxmax", [P, 2, 4])
        xsum = sb("xsum", [P, 2, 4])
        xrs = sb("xrs", [P, 2, 4])
        fT = sb("fT", [P, 3, HID])
        raw = Q6[1][:, :, :].rearrange("p h t -> p (h t)").bitcast(F32)
        rq = raw[:, 0:XH * D].rearrange("p (h e) -> p h e", h=XH)
        rkv = raw[:, XH * D:3 * XH * D].rearrange("p (h e) -> p h e", h=XH)
        wp = raw[:, 3 * XH * D:4 * XH * D].rearrange("p (h e) -> p h e", h=XH)
        whT = [within(GP, 0, XH, D), within(GP, XH * D, XH, D), VM]
        ff = [t[:, :, :].rearrange("p n d -> p (n d)")[:, 0:HID] for t in (X[3], X[4], XB[1])]

        def words(t):
            return t.rearrange("p h t -> p (h t)").bitcast(F32)

        x_loaded = [sem(f"x_loaded{b}") for b in range(B)]
        qkv_loaded = sem("qkv_loaded")
        early_loaded = sem("early_loaded")
        late_loaded = sem("late_loaded")
        zero_ready = sem("zero_ready")
        consts_ready = sem("consts_ready")
        zeros_ready = sem("zeros_ready")
        key_zeros_ready = sem("key_zeros_ready")
        late_zeros_ready = sem("late_zeros_ready")
        wqkv_ready = sem("wqkv_ready")
        x0_weights_ready = sem("x0_weights_ready")
        bias_cols_ready = sem("bias_cols_ready")
        ff_ready = sem("ff_ready")
        bvb_ready = sem("bvb_ready")
        eb_loaded = sem("eb_loaded")
        dve_step = sem("dve_step")
        pool_step = sem("pool_step")
        v_copied = sem("v_copied")
        qk_stats_ready = sem("qk_stats_ready")
        qk_rstd_ready = sem("qk_rstd_ready")
        qk_shift_ready = sem("qk_shift_ready")
        part_ready = [[sem(f"part{n}_ready{a}") for n in range(3)] for a in range(2)]
        qk_placed = [sem("qk_placed0"), sem("qk_placed1")]
        mparts_ready = sem("mparts_ready")
        max_placed = [sem("max_placed0"), sem("max_placed1")]
        ex_used = sem("ex_used")
        stats_ready = [sem(f"stats_ready{n}") for n in range(6)]
        shift_ready = [sem(f"shift_ready{n}") for n in range(6)]
        rstd_ready = [sem(f"rstd_ready{n}") for n in range(6)]
        x_ready = [None] + [sem(f"x_ready{n}") for n in range(1, 7)]
        xb_ready = [sem("xb_ready0"), sem("xb_ready1")]
        gate_shifted = sem("gate_shifted")
        gate_exps = sem("gate_exps")
        gates_ready = sem("gates_ready")
        phi_clamped = sem("phi_clamped")
        phi_exps = sem("phi_exps")
        phi_ready = sem("phi_ready")
        vaug_ready = sem("vaug_ready")
        xmax_ready = sem("xmax_ready")
        xrs_ready = sem("xrs_ready")
        xp_ready = sem("xp_ready")
        pads_ready = sem("pads_ready")
        htanh_ready = sem("htanh_ready")
        q_cleared = sem("q_cleared")
        stored = sem("stored")

        N_EARLY, N_LATE = 16, 13
        QK_DMAS = len(Q_PARTS) + len(K_PARTS)

        def qkn_free(eng, b):
            if b == 1:
                eng.wait_ge(ff_ready, 1)
            elif b:
                filled(eng, (b - 1, "qkT", 1))

        block = stack.enter_context(nc.Block())

        @block.sync
        def _(sp):
            def row(vec):
                return vec.rearrange("(o d) -> o d", o=1).partition_broadcast(P)

            def column(vec):
                return vec.rearrange("(d o) -> d o", o=1)

            def head_column(vec):
                return vec.rearrange("(h d) -> d h", d=HD)

            def load_x(b):
                sp.dma_start(X0[:, b % 2, :, :], x[b].rearrange("(n p) d -> p n d", p=P)
                             ).then_inc(x_loaded[b], 16)

            load_x(0)
            sp.dma_start(wqkv, L0_attn_W_qkv).then_inc(qkv_loaded, 16)
            sp.dma_start(col("q_scale"), head_column(L0_attn_q_scale),
                         allow_slow_non_contiguous=True).then_inc(qkv_loaded, 16)
            sp.dma_start(col("k_scale"), head_column(L0_attn_k_scale),
                         allow_slow_non_contiguous=True).then_inc(qkv_loaded, 16)

            early = [
                (wout[:, :], L0_attn_W_out),
                (cx[:, :, :], ctx_1024[:, 0:P, :].rearrange("b p d -> p b d")),
                (cxr[:, :, :], ctx_1024[:, P:C, :].rearrange("b p d -> p b d")),
                (xw_raw[:, 0, :], L0_xattn_Wq), (xw_raw[:, 1, :], L0_xattn_Wk),
                (xwv[:, :], L0_xattn_Wv), (xwo[:, :], L0_xattn_Wo),
                (rows[:, BV:BV + 1, :].rearrange("p o d -> p (o d)"), row(L0_xattn_bv)),
                (rows[:, BO:BO + 1, :].rearrange("p o d -> p (o d)"), row(L0_xattn_bo)),
                (rows[:, LBO:LBO + 1, :].rearrange("p o d -> p (o d)"), row(L1_attn_bo)),
                (col("xbq"), head_column(L0_xattn_bq)), (col("xbk"), head_column(L0_xattn_bk)),
                (col("lbq"), column(L1_attn_bq)), (col("lbk"), column(L1_attn_bk)),
                (col("lbv"), column(L1_attn_bv)), (col("bproj"), column(L1_xattn_b_proj)),
            ]
            assert len(early) == N_EARLY
            late = [
                (gw[:, :], L0_ffn_gate_w), (gb[:, :], row(L0_ffn_gate_b)),
                (ew[:, :, :], L0_ffn_expert_w.rearrange("e d f -> d e f")),
                (lw[:, 0, :], L1_attn_Wq), (lw[:, 1, :], L1_attn_Wk),
                (lw[:, 2, :], L1_attn_Wo), (lw[:, 3, :], L1_attn_Wv),
                (rq, L1_xattn_Wq), (rkv, L1_xattn_Wkv),
                (wp, L1_xattn_Wproj.rearrange("h e o -> e h o")),
                (fi[:, 0, :].rearrange("p (c d) -> p c d", c=HC),
                 L1_ffn_w_gate.rearrange("(c p) d -> p c d", p=P)),
                (fi[:, 1, :].rearrange("p (c d) -> p c d", c=HC),
                 L1_ffn_w_up.rearrange("(c p) d -> p c d", p=P)),
                (fi[:, 2, :], L1_ffn_w_down),
            ]
            assert len(late) == N_LATE
            for dst, src in early:
                sp.dma_start(dst, src, allow_slow_non_contiguous=True).then_inc(early_loaded, 16)
            def load(those):
                for dst, src in those:
                    sp.dma_start(dst, src).then_inc(late_loaded, 16)

            load(late[:-3])

            def place_parts(a, b, w):
                if b == 0:
                    if w == 0:
                        sp.wait_ge(q_cleared if a else zeros_ready, 1)
                    else:
                        sp.wait_ge(late_zeros_ready if a else key_zeros_ready, 1)
                n = C if a and w else S
                if b:
                    filled(sp, (b - 1, "ST", a, NQ - 1, T_UNITS[a] - 1))
                to = (Q6, K6)[w][a]
                for part in range(3):
                    sp.wait_ge(part_ready[a][part], 2 * b + 1 + (w if a == 0 else 1 - w))
                    for s, slot_part in enumerate((Q_PARTS, K_PARTS)[w]):
                        if slot_part == part:
                            sp.dma_start(to[HD * s:HD * s + HD, :, 0:n],
                                         ((xkparts if w else xparts)[:, part, 0:n] if a else
                                          parts[:, w, part, 0:n])
                                         ).then_inc(qk_placed[a], 16)

            def qkT(b, w):
                place_parts(0, b, w)
                if b == 0 and w == 1:
                    drained(sp, (0, "qkT", 1))
                    load(late[-3:])

            def mT(b, a, g):
                drained(sp, (b, "mT", a, g))
                for p in range(3):
                    sp.dma_start(
                        Q6[a][MAX_ROW + p:MAX_ROW + p + 1, 4 * g:4 * g + 4, :].rearrange(
                            "o h (n q) -> o (h n) q", q=P),
                        mrows[16 * p:16 * p + 16, g % 2, :]).then_inc(max_placed[a], 16)

            def moments_(b, n):
                if n == 0 and b + 2 < B:
                    drained(sp, (b, "out", 0))
                    load_x(b + 2)

            def norm(b, n):
                if n == 5:
                    sp.wait_ge(x_ready[6], NB * (b + 1))
                    sp.dma_start(out[b].rearrange("(n p) d -> p n d", p=P), XB[1][:, :, :]
                                 ).then_inc(stored, 16)

            def wT(b, n):
                if n == 0:
                    sp.wait_ge(late_zeros_ready, 1)
                    for m in range(NB):
                        sp.dma_start(eb[E * m:E * m + E, m, :], L0_ffn_expert_b
                                     ).then_inc(eb_loaded, 16)

            load_x(1)
            work = {"qkT": qkT, "xk": lambda b: place_parts(1, b, 1),
                    "xq": lambda b: place_parts(1, b, 0), "mT": mT, "moments": moments_,
                    "norm": norm, "wT": wT}
            for b, what, *at in steps:
                if what in work:
                    work[what](b, *at)
            sp.wait_ge(stored, 16 * B)

        @block.gpsimd
        def _(pool):
            done = [0]

            def step(ins):
                ins.then_inc(pool_step, 1)
                done[0] += 1
                pool.wait_ge(pool_step, done[0])

            nc.gpsimd.memset(zero[:, :], 0.0).then_inc(zero_ready, 1)
            nc.gpsimd.memset(power[:, :], -0.5)
            step(nc.gpsimd.memset(ones, 1.0))
            step(nc.gpsimd.affine_select(out=ident[:, :], in_=ones, pattern=[[-1, P]],
                                         compare_op=ALU.is_equal, fill=0.0, base=0,
                                         channel_multiplier=1))
            nc.gpsimd.tensor_copy(identb[:, :], ident[:, :])
            step(nc.gpsimd.affine_select(out=causal[:, :], in_=ones, pattern=[[1, P]],
                                         compare_op=ALU.is_ge, fill=0.0, base=0,
                                         channel_multiplier=-1))
            nc.gpsimd.tensor_scalar(maskT[:, :], causal[:, :], -1.0, -MASKED, ALU.add, ALU.mult)
            step(nc.gpsimd.affine_select(out=bvb, in_=ones, pattern=[[-1, P]],
                                         compare_op=ALU.is_ge, fill=0.0, base=0,
                                         channel_multiplier=1))
            nc.gpsimd.tensor_scalar(maskS[:, :], bvb, -1.0, -MASKED, ALU.add, ALU.mult
                                    ).then_inc(consts_ready, 1)
            step(nc.gpsimd.memset(words(Q6[0][:, :, :]), 0.0))
            nc.gpsimd.memset(words(K6[0][MAX_ROW:P, :, :]), TWO_ONES).then_inc(zeros_ready, 1)
            pool.wait_ge(zeros_ready, 1)

            def late_zeros():
                step(nc.gpsimd.memset(cT[:, :, :], 0.0))
                step(nc.gpsimd.memset(eb[:, :, :], 0.0))
                step(nc.gpsimd.memset(words(K6[1][0:MAX_ROW, :, :]), 0.0))
                step(nc.gpsimd.memset(words(K6[1][MAX_ROW:P, :, :]), TWO_ONES))
                step(nc.gpsimd.memset(VXR[:, :, :], 0.0))
                for j in range(4):
                    step(nc.gpsimd.memset(
                        VXR[32 * j:32 * j + CR, :, 32 * j + HD:32 * j + HD + 1], 1.0))
                nc.gpsimd.memset(vaug[:, :, :], 1.0).then_inc(late_zeros_ready, 1)

            def roots(mom, root, half, shift_, eps, ready, rooted, shifted, n):
                pool.wait_ge(ready, n)
                step(nc.gpsimd.tensor_scalar(root, mom[..., 1], eps, None, ALU.add))
                nc.gpsimd.tensor_tensor(root, root, half, ALU.pow).then_inc(rooted, 1)
                step(nc.gpsimd.tensor_scalar(shift_, mom[..., 0], -1.0, None, ALU.mult))
                pool.wait_ge(rooted, n)
                nc.gpsimd.tensor_tensor(shift_, shift_, root, ALU.mult).then_inc(shifted, 1)

            def qk_norm(b):
                roots(qkmoments[:, :, :, :], qkrstd[:, :, :],
                      power[:, :].rearrange("p (n w) -> p n w", n=NB), qkshift[:, :, :],
                      QK_EPS, qk_stats_ready, qk_rstd_ready, qk_shift_ready, b + 1)
                if b == 0:
                    late_zeros()

            def norm(b, n):
                r = int(n >= 2)
                roots(moments[r][:, :, :], rstd[r][:, :], power[:, 0:NB], shift[r][:, :],
                      LN_EPS, stats_ready[n], rstd_ready[n], shift_ready[n], b + 1)
                if n in (0, 2):
                    if n == 0 and b == 0:
                        pool.wait_ge(early_loaded, 16 * N_EARLY)
                    if n == 2 and b:
                        pool.wait_ge(stored, 16 * b)
                    pool.wait_ge(x_ready[n + 1], NB * (b + 1))
                    bias = LBO if n else BO
                    nc.gpsimd.tensor_tensor(
                        XB[r][:, :, :], X[n + 1][:, :, :],
                        rows[:, bias:bias + 1, :].to_broadcast([P, NB, D]), ALU.add
                    ).then_inc(xb_ready[r], 1)

            def wM(b, n):
                if n == SETUP_PRODUCTS - 1:
                    k, m = place[(b, "wM", n)]
                    pool.wait_ge(bank_filled[k], m + 1)
                    nc.gpsimd.memset(XP, 0.0).then_inc(pads_ready, 1)

            def sums(b, u):
                pool.wait_ge(xrs_ready, 2 * NB * b + u + 1)
                if u >= 2 or b:
                    k, n = place[(b, "PR", u - 2) if u >= 2 else (b - 1, "PR", 2 * NB + u - 2)]
                    pool.wait_ge(bank_filled[k], n + 1)
                for at, c0, c1 in ((0, 0, P), (4 * P, P, C)):
                    n = P if c0 == 0 else CP - P
                    last = nc.gpsimd.tensor_tensor(
                        XP[:, u % 2, at:at + 4 * n].rearrange(
                            "p (h c) -> p h c", h=4)[:, :, 0:c1 - c0],
                        XE[:, u % 2, :, c0:c1],
                        xrs[:, u % 2, :].rearrange("p (h o) -> p h o", o=1).to_broadcast(
                            [P, 4, c1 - c0]), ALU.mult)
                last.then_inc(xp_ready, 1)

            work = {"norm": norm, "qk_norm": qk_norm, "wM": wM, "sums": sums}
            for b, what, *at in steps:
                if what in work:
                    work[what](b, *at)

        @block.tensor
        def _(pe):
            def fill(key):
                k, n = place[key]
                if n:
                    pe.wait_ge(bank_drained[k], n)
                return psum[:, k, :]

            def fills_(ins, key):
                return ins.then_inc(bank_filled[place[key][0]], 1)

            mm = nc.tensor.matmul

            def transposes(key, pieces):
                to = fill(key)
                for at, src in pieces:
                    m = src.shape[0]
                    n = 1
                    for k in src.shape[1:]:
                        n *= k
                    last = nc.tensor.transpose(to[0:n, at:at + m], src, ident[0:m, 0:m])
                fills_(last, key)

            def to_features(key, src):
                transposes(key, [(P * n, src[:, n, :]) for n in range(NB)])

            def x_T(b, n):
                if n == 0:
                    pe.wait_ge(x_loaded[b], 16)
                    src = X0[:, b % 2, :, :]
                else:
                    pe.wait_ge(x_ready[n], NB * (b + 1))
                    src = X[n]
                to_features((b, f"x{n}T", n), src)

            def qkv(b, n):
                if n == 0:
                    drained(pe, (b, "x0T", 0))
                    if b == 0:
                        pe.wait_ge(wqkv_ready, 1)
                key = (b, "qkv", n)
                fills_(mm(fill(key)[:, 0:3 * D], xT[0][:, P * n:P * n + P], wqkv_p[:, :]), key)

            def qkT(b, w):
                if w == 0:
                    for n in range(NB):
                        drained(pe, (b, "qkv", n))
                to_features((b, "qkT", w), qkn[:, w, :, :])

            def scores(b, a, g, u):
                if g == u == 0:
                    if b == a == 0:
                        pe.wait_ge(zeros_ready, 1)
                    pe.wait_ge(qk_placed[a], 16 * QK_DMAS * (b + 1))
                key = (b, "S", a, g, u)
                to = fill(key)
                for at, h, q in PIECES[a][u]:
                    n = C if a else P * (q + 1)
                    last = mm(to[:, at:at + n], Q6[a][0:SPLIT_ROWS, 4 * g + h, P * q:P * q + P],
                              K6[a][0:SPLIT_ROWS, 4 * g + h, 0:n], start=True, stop=bool(a))
                    if not a:
                        last = mm(to[:, at + n - P:at + n], identb[:, :], maskS[:, :],
                                  start=False, stop=True)
                fills_(last, key)

            def scores_T(b, a, g, u):
                if u == 0:
                    pe.wait_ge(max_placed[a], 48 * (NQ * b + g + 1))
                key = (b, "ST", a, g, u)
                to = fill(key)
                if a and u == 4:
                    for h in range(4):
                        last = mm(to[32 * h:32 * h + 32, :], K6[1][:, 4 * g + h, P:CP],
                                  Q6[1][:, 4 * g + h, :], start=True, stop=True)
                elif a:
                    last = mm(to, K6[1][:, 4 * g + u, 0:P], Q6[1][:, 4 * g + u, :],
                              start=True, stop=True)
                else:
                    for at, h, k in SELF_T_PIECES[u]:
                        n = S - P * k
                        mm(to[:, at:at + n], K6[0][:, 4 * g + h, P * k:P * k + P],
                           Q6[0][:, 4 * g + h, P * k:S], start=True, stop=False)
                        last = mm(to[:, at:at + P], identb[:, :], maskT[:, :],
                                  start=False, stop=True)
                fills_(last, key)

            def values(b, a, g, part):
                key = (b, "PV", a, g)
                if part == 0 or a:
                    fill(key)
                to = bank(key)
                if a:
                    drained(pe, (b, "ST", 1, g, 4))
                    if g == 0:
                        drained(pe, (b, "xv"))
                    at = 5 * (g % 2)
                    for h in range(4):
                        mm(to[32 * h:32 * h + 32, :], VX[:, 4 * g + h, :], EX[:, at + h, :],
                           start=True, stop=False, skip_group_check=True)
                    fills_(mm(to, VXR[:, g, :], EX[:, at + 4, :], start=False, stop=True,
                              skip_group_check=True), key)
                    return
                drained(pe, (b, "ST", 0, g, (3, 7, 9)[part]))
                for k in PV_PARTS[part]:
                    for h in range(4):
                        n = S - P * k
                        u, at = [(u, at) for u, pieces in enumerate(SELF_T_PIECES)
                                 for at, hh, kk in pieces if (hh, kk) == (h, k)][0]
                        last = mm(to[32 * h:32 * h + 32, P * k:S], V[:, k, 4 * g + h, :],
                                  EX[:, u, at:at + n], start=part == 0, stop=part == 2)
                if part == 2:
                    fills_(last, key)
                else:
                    last.then_inc(ex_used, 1)

            def max_T(b, a, g):
                key = (b, "mT", a, g)
                to = fill(key)
                pe.wait_ge(mparts_ready, NQ * (2 * b + a) + g + 1)
                fills_(nc.tensor.transpose(to[0:48, 0:64].bitcast(BF16),
                                           mparts[:, g % 2, :, :].rearrange("p a b -> p (a b)"),
                                           identb[:, :]), key)

            def products_T(b, a, g):
                drained(pe, (b, "PV", a, g))
                transposes((b, "cT", a, g), [(P * n, pvraw[:, P * n:P * n + P])
                                             for n in range(NB)])

            def ctx_T(b, a):
                drained(pe, (b, "cT", a, NQ - 1))
                to_features((b, "ctxT", a), ctx[:, :, :, :].rearrange("p n h d -> p n (h d)"))

            def out_product(b, a):
                drained(pe, (b, "ctxT", a))
                if b == a == 0:
                    pe.wait_ge(early_loaded, 16 * N_EARLY)
                key = (b, "out", a)
                to = fill(key)
                for n in range(NB):
                    last = mm(to[:, P * n:P * n + P], ctxT[:, P * n:P * n + P],
                              (xwo if a else wout)[:, :])
                fills_(last, key)

            def setup_T(b, n):
                key = (b, "wT", n)
                if n == 0:
                    pe.wait_ge(early_loaded, 16 * N_EARLY)
                    pe.wait_ge(late_zeros_ready, 1)
                if n < B:
                    transposes(key, [(0, cx[:, n, :]), (P, cxr[:, n, :])])
                    return
                if n == B:
                    pe.wait_ge(late_loaded, 16 * N_LATE)
                n -= B
                if n < 6:
                    h, src = 4 * (n // 3), (rq, rkv[:, :, 0:D], rkv[:, :, D:2 * D])[n % 3]
                    transposes(key, [(P * i, src[:, h + i, :]) for i in range(4)])
                elif n == 6:
                    transposes(key, [(P * i, lw[:, i, :]) for i in range(3)])
                else:
                    pe.wait_ge(ff_ready, 1)
                    transposes(key, [(P * c, ff[n - 7][:, P * c:P * c + P]) for c in range(HC)])

            def setup_products(b, n):
                if n == 0:
                    for i in range(SETUP_TRANSPOSES):
                        drained(pe, (b, "wT", i))
                key = (b, "wM", n)
                to = fill(key)
                if n == 4:
                    mm(to[:, 0:P], lw[:, 3, :], lwT[:, 2, :])
                    last = mm(to[:, P:2 * P], bvb, lwT[:, 2, :])
                for i in range(4 if n < 4 else 0):
                    h = 4 * (n // 2) + i
                    last = (mm(to[:, P * i:P * i + P], whT[1][:, h, :], whT[0][:, h, :])
                            if n % 2 == 0 else
                            mm(to[:, P * i:P * i + P], whT[2][:, h, :], wp[:, h, :]))
                fills_(last, key)

            def cross_k(b):
                if b == 0:
                    pe.wait_ge(x0_weights_ready, 1)
                    for n in range(B):
                        drained(pe, (0, "wT", n))
                key = (b, "xk")
                fills_(mm(fill(key)[:, 0:C], xwk[:, :], cT[:, b, 0:C]), key)

            def cross_v(b):
                key = (b, "xv")
                to = fill(key)
                mm(to[:, 0:P], cT[:, b, 0:P], xwv[:, :])
                for j in range(4):
                    last = mm(to[32 * j:32 * j + 32, P:2 * P], cT[:, b, P:CP], xwv[:, :])
                fills_(last, key)

            def cross_q(b):
                drained(pe, (b, "x1T", 1))
                key = (b, "xq")
                fills_(mm(fill(key), xwq[:, :], xT[1][:, :]), key)


            def context_keys(b, n):
                if b == n == 0:
                    for i in range(SETUP_PRODUCTS):
                        drained(pe, (0, "wM", i))
                key = (b, "G", n)
                to = fill(key)
                for i in range(2):
                    last = mm(to[:, C * i:C * i + C], aT[:, 2 * n + i, :], cT[:, b, 0:C])
                fills_(last, key)

            def context_values(b, n):
                key = (b, "Vm", n)
                fills_(mm(fill(key), cT[:, b, 0:P],
                          mv[:, 4 * n:4 * n + 4, :].rearrange("p h o -> p (h o)")), key)

            def context_rest(b):
                key = (b, "Vr")
                to = fill(key)
                for g in range(2):
                    for j in range(4):
                        last = mm(to[32 * j:32 * j + 32, P * g:P * g + P], cT[:, b, P:CP],
                                  mv[:, 4 * g + j, :])
                fills_(last, key)

            def gate(b):
                drained(pe, (b, "x2T", 2))
                if b == 0:
                    pe.wait_ge(late_loaded, 16 * N_LATE)
                key = (b, "gate")
                to = fill(key)
                for n in range(NB):
                    last = mm(to[:, E * n:E * n + E], xT[2][:, P * n:P * n + P], gw[:, :])
                fills_(last, key)

            def expert(b, i):
                n, half = i // 2, i % 2
                key = (b, "ex", i)
                fills_(mm(fill(key), xT[2][:, P * n:P * n + P],
                          ew[:, 4 * half:4 * half + 4, :].rearrange("p e d -> p (e d)")), key)

            def gates_T(b):
                pe.wait_ge(gates_ready, b + 1)
                transposes((b, "gT"), [(0, gl[:, :, :].rearrange("p n e -> p (n e)"))])

            def expert_biases(b):
                drained(pe, (b, "gT"))
                if b == 0:
                    pe.wait_ge(eb_loaded, 16 * NB)
                key = (b, "mb")
                to = fill(key)
                for n in range(NB):
                    last = mm(to[:, P * n:P * n + P], gT[:, :], eb[:, n, :])
                fills_(last, key)

            def linear_qk(b, w):
                if w == 1:
                    drained(pe, (b, "x3T", 3))
                key = (b, ("lq", "lk")[w])
                fills_(mm(fill(key), lwT[:, w, :], xT[3][:, :]), key)

            def linear_v(b):
                key = (b, "lv")
                to = fill(key)
                for n in range(NB):
                    last = mm(to[:, P * n:P * n + P], xT[3][:, P * n:P * n + P], lwv[:, :])
                fills_(last, key)

            def linear_k_T(b):
                pe.wait_ge(phi_ready, 2 * b + 1)
                transposes((b, "kp"), [(P * n, phi[:, 1, P * n:P * n + P]) for n in range(NB)])

            def linear_within(b):
                pe.wait_ge(phi_ready, 2 * b + 2)
                key = (b, "A")
                to = fill(key)
                for n in range(NB):
                    last = mm(to[:, P * n:P * n + P], phi[:, 1, P * n:P * n + P],
                              phi[:, 0, P * n:P * n + P])
                fills_(last, key)

            def linear_states(b):
                drained(pe, (b, "kp"))
                drained(pe, (b, "lv"))
                key = (b, "KV")
                to = fill(key)
                for n in range(NB - 1):
                    last = mm(to[:, (D + 1) * n:(D + 1) * (n + 1)], kp[:, n, :],
                              vaug[:, n, 0:D + 1])
                fills_(last, key)

            def linear_out(b, i):
                drained(pe, (b, "A"))
                drained(pe, (b, "KV"))
                key = (b, "lo", i)
                to = fill(key)
                for n in (2 * i, 2 * i + 1):
                    at = (D + 1) * (n % 2)
                    last = mm(to[:, at:at + D + 1], AT[:, n, :], vaug[:, n, 0:D + 1],
                              start=True, stop=n == 0)
                    if n:
                        last = mm(to[:, at:at + D + 1], phi[:, 0, P * n:P * n + P],
                                  state[:, n - 1, :], start=False, stop=True)
                fills_(last, key)

            def cross_scores(b, i):
                if i == 0:
                    drained(pe, (b, "x4T", 4))
                    for n in range(XH // 2):
                        drained(pe, (b, "G", n))
                q, h = i // 4, 2 * (i % 4)
                key = (b, "XS", i)
                fills_(mm(fill(key)[:, 0:2 * C], xT[4][:, P * q:P * q + P],
                          G[:, h:h + 2, :].rearrange("p h c -> p (h c)")), key)

            def cross_T(b, u):
                pe.wait_ge(xp_ready, 2 * NB * b + u + 1)
                transposes((b, "PT", u), [(P * h, XP[:, u % 2, P * h:P * h + P])
                                          for h in range(4)])

            def cross_rest_T(b, u):
                transposes((b, "PR", u), [(0, XP[:, u % 2, 4 * P:5 * P])])

            def cross_out(b, half):
                for u in range(NB * half, NB * half + NB):
                    drained(pe, (b, "PT", u))
                    drained(pe, (b, "PR", u))
                if half == 0:
                    for n in range(2):
                        drained(pe, (b, "Vm", n))
                    drained(pe, (b, "Vr"))
                key = (b, "XO", half)
                to = fill(key)[:, 0:S // 2]
                for h in range(XH):
                    mm(to, VM[:, h, :], XPT[:, h, :], start=h == 0, stop=False)
                for g in range(2):
                    last = mm(to, VR[:, g, :], XPR[:, g, :], start=False, stop=g == 1)
                fills_(last, key)

            def cross_out_T(b):
                for half in range(2):
                    drained(pe, (b, "XO", half))
                transposes((b, "XOT"), [(P * n, xoT[:, P * n:P * n + P]) for n in range(NB)])

            def hidden(b, i):
                c, w = i // 2, i % 2
                if i == 0:
                    drained(pe, (b, "x5T", 5))
                key = (b, "hid", i)
                fills_(mm(fill(key), fT[:, w, P * c:P * c + P], xT[5][:, :]), key)

            def down(b):
                for c in range(HC):
                    drained(pe, (b, "hid", 2 * c + 1))
                key = (b, "down")
                to = fill(key)
                for n in range(NB):
                    for c in range(HC):
                        last = mm(to[:, P * n:P * n + P], hT[:, c, P * n:P * n + P],
                                  fT[:, 2, P * c:P * c + P], start=c == 0, stop=c == HC - 1)
                fills_(last, key)

            work = {"qkv": qkv, "qkT": qkT, "S": scores, "ST": scores_T, "PV": values,
                    "mT": max_T, "cT": products_T, "ctxT": ctx_T, "out": out_product,
                    "wT": setup_T, "wM": setup_products, "xk": cross_k, "xv": cross_v,
                    "xq": cross_q, "G": context_keys, "Vm": context_values, "Vr": context_rest,
                    "gate": gate, "ex": expert, "gT": gates_T, "mb": expert_biases,
                    "lk": lambda b: linear_qk(b, 1), "lq": lambda b: linear_qk(b, 0),
                    "lv": linear_v, "kp": linear_k_T, "A": linear_within, "KV": linear_states,
                    "lo": linear_out, "XS": cross_scores, "PT": cross_T, "PR": cross_rest_T,
                    "XO": cross_out, "XOT": cross_out_T, "hid": hidden, "down": down}
            work |= {f"x{n}T": x_T for n in range(6)}
            pe.wait_ge(consts_ready, 1)
            for b, what, *at in steps:
                if what in work:
                    work[what](b, *at)

        @block.scalar
        def _(act):
            copy = nc.scalar.copy

            def move(dst, key, n=512, rows_=P):
                src = filled(act, key)[0:rows_, 0:n]
                drains(copy(dst, src), key)

            def flat(t):
                return t.rearrange("p a b -> p (a b)")

            def qkv(b, n):
                src = filled(act, (b, "qkv", n))
                copy(V[:, n, :, 0:HD], src[:, 2 * D:3 * D].rearrange("p (h d) -> p h d", d=HD)
                     ).then_inc(v_copied, 1)

            def qkT(b, w):
                key = (b, "qkT", w)
                src = filled(act, key)
                if b == w == 0:
                    act.wait_ge(bias_cols_ready, 1)
                if b:
                    act.wait_ge(qk_placed[0], 16 * QK_DMAS * b)
                scale = col(QS) if w == 0 else col("k_scale")
                nc.scalar.activation(parts[:, w, 0, :], src, ACT.Copy, scale=scale
                                     ).then_inc(part_ready[0][0], 1)

            def cross_split(b, w):
                key = (b, ("xq", "xk")[w])
                n = (S, C)[w]
                src = filled(act, key)[:, 0:n]
                if b:
                    act.wait_ge(qk_placed[1], 16 * QK_DMAS * b)
                scale = HEAD_SCALE if w == 0 else 1.0
                bias = col(XBQ) if w == 0 else col("xbk")
                three, whole = (xkparts, xkf[:, :]) if w else (xparts, xqf)
                nc.scalar.activation(three[:, 0, :], src, ACT.Identity, bias=bias,
                                     scale=scale).then_inc(part_ready[1][0], 1)
                drains(nc.scalar.activation(whole, src, ACT.Identity, bias=bias,
                                            scale=scale), key)

            def qk_norm(b):
                act.wait_ge(qk_shift_ready, b + 1)
                qkn_free(act, b)
                for n in ACT_BLOCKS:
                    key = (b, "qkv", n)
                    for w in range(2):
                        last = nc.scalar.activation(
                            qkn[:, w, n, :], bank(key)[:, D * w:D * w + D], ACT.Identity,
                            bias=qkshift[:, n, w:w + 1], scale=qkrstd[:, n, w:w + 1])
                    drains(last, key)

            def norm(b, n):
                r = int(n >= 2)
                dst = XB[1] if n == 5 else X[n + 1]
                act.wait_ge(shift_ready[n], b + 1)
                for i in ACT_BLOCKS:
                    nc.scalar.activation(dst[:, i, :], Y[r][:, i, :], ACT.Identity,
                                         bias=shift[r][:, i:i + 1], scale=rstd[r][:, i:i + 1]
                                         ).then_inc(x_ready[n + 1], 1)

            def exponentials(b, a, g, u):
                key = (b, "ST", a, g, u)
                src = filled(act, key)
                if a == 0 and g == 0:
                    if u == 0 and b:
                        filled(act, (b - 1, "PV", 1, NQ - 1))
                elif a == 0 and u in (0, 4):
                    act.wait_ge(ex_used, 2 * (NQ * b + g - 1) + (1 if u == 0 else 2))
                elif a == 0 and u == 8:
                    filled(act, (b, "PV", 0, g - 1))
                elif a and u == 0 and g != 1:
                    filled(act, (b, "PV", 1, g - 2) if g else (b, "PV", 0, NQ - 1))
                slot = 5 * (g % 2) + u if a else u
                drains(nc.scalar.activation(EX[:, slot, :], src, ACT.Exp), key)

            def max_T(b, a, g):
                key = (b, "mT", a, g)
                src = filled(act, key)
                if before(b, a, g):
                    b0, a0, g0 = before(b, a, g)
                    act.wait_ge(max_placed[a0], 48 * (NQ * b0 + g0 + 1))
                drains(copy(mrows[:, g % 2, :], src[0:48, 0:64].bitcast(BF16)), key)

            def setup_T(b, n):
                key = (b, "wT", n)
                if n < B:
                    if n == 0:
                        act.wait_ge(late_zeros_ready, 1)
                    drains(copy(cT[:, n, 0:C], filled(act, key)[:, 0:C]), key)
                elif n < B + 6:
                    h, w = 4 * ((n - B) // 3), (n - B) % 3
                    move(flat(whT[w][:, h:h + 4, :]), key)
                elif n == B + 6:
                    move(flat(lwT[:, :, :]), key, 3 * D)
                else:
                    move(fT[:, n - B - 7, :], key, HID)

            def setup_products(b, n):
                key = (b, "wM", n)
                if n < 4:
                    drains(nc.scalar.activation(
                        flat((aT, mv)[n % 2][:, 4 * (n // 2):4 * (n // 2) + 4, :]),
                        filled(act, key), ACT.Copy, scale=1.0 if n % 2 else X_SCALE), key)
                else:
                    src = filled(act, key)
                    copy(lwv[:, :], src[:, 0:D])
                    drains(copy(rows[:, LBV, :], src[:, D:2 * D]), key)

            def gate_exps_(b):
                act.wait_ge(gate_shifted, b + 1)
                nc.scalar.activation(ge[:, :, :], gl[:, :, :], ACT.Exp).then_inc(gate_exps, 1)

            def phi_(b, w):
                act.wait_ge(phi_clamped, 2 * b + 2 - w)
                nc.scalar.activation(lexp[:, w, :], lexp[:, w, :], ACT.Exp).then_inc(phi_exps, 1)

            def cross_exps(b, i):
                u = i // 2
                act.wait_ge(xmax_ready, 4 * NB * b + i + 1)
                if i % 2 == 0 and u >= 2:
                    act.wait_ge(xp_ready, 2 * NB * b + u - 1)
                key = (b, "XS", i)
                src = filled(act, key)
                for j in range(2):
                    h = 2 * (i % 2) + j
                    last = nc.scalar.activation(
                        XE[:, u % 2, h, :], src[:, C * j:C * j + C], ACT.Exp,
                        bias=nxmax[:, u % 2, h:h + 1],
                        accum_out=xsum[:, u % 2, h:h + 1])
                drains(last, key)

            def cross_T(b, u):
                key = (b, "PT", u)
                g, at = u % 2, P * (u // 2 % 2)
                src = filled(act, key).rearrange("p (h q) -> p h q", h=4)
                if u == NB:
                    filled(act, (b, "XO", 0))
                drains(copy(XPT[:, 4 * g:4 * g + 4, at:at + P], src), key)

            def cross_rest_T(b, u):
                g, at = u % 2, P * (u // 2 % 2)
                move(XPR[:, g, at:at + P], (b, "PR", u), P)

            def cross_out(b, half):
                key = (b, "XO", half)
                src = filled(act, key)[:, 0:S // 2]
                drains(nc.scalar.activation(xoT[:, S // 2 * half:S // 2 * (half + 1)], src,
                                            ACT.Identity, bias=col("bproj")), key)

            def hidden(b, i):
                if i % 2 == 0:
                    src = filled(act, (b, "hid", i))
                    nc.scalar.activation(htanh[:, i // 2, :], src, ACT.Tanh, scale=0.5
                                         ).then_inc(htanh_ready, 1)

            work = {"qkv": qkv, "qk_norm": qk_norm, "norm": norm, "qkT": qkT,
                    "xk": lambda b: cross_split(b, 1), "xq": lambda b: cross_split(b, 0),
                    "ST": exponentials, "mT": max_T,
                    "PV_out": lambda b, a, g: move(pvraw[:, :], (b, "PV", a, g)),
                    "ctxT": lambda b, a: move(ctxT[:, :], (b, "ctxT", a)),
                    "wT": setup_T, "wM": setup_products,
                    "G": lambda b, n: move(flat(G[:, 2 * n:2 * n + 2, :]), (b, "G", n), 2 * C),
                    "Vm": lambda b, n: move(flat(VM[:, 4 * n:4 * n + 4, :]), (b, "Vm", n)),
                    "Vr": lambda b: move(flat(VR[:, :, :]), (b, "Vr"), 2 * D),
                    "gate_exps": gate_exps_,
                    "gT": lambda b: move(gT[:, :], (b, "gT"), P, NB * E), "phi": phi_,
                    "kp": lambda b: move(flat(kp), (b, "kp")), "XS": cross_exps,
                    "PT": cross_T, "PR": cross_rest_T, "XO": cross_out, "hid": hidden}
            work |= {f"x{n}T": lambda b, n: move(xT[n][:, :], (b, f"x{n}T", n))
                     for n in range(6)}
            act.wait_ge(zero_ready, 1)
            nc.scalar.activation(
                words(K6[0][0:MAX_ROW, :, :]),
                zero[0:MAX_ROW, :].to_broadcast([MAX_ROW, H * S // 2]),
                ACT.Copy).then_inc(key_zeros_ready, 1)
            act.wait_ge(consts_ready, 1)
            for b, what, *at in steps:
                if what in work:
                    work[what](b, *at)

        @block.vector
        def _(dve):
            vec = nc.vector
            done = [0]

            def step(ins):
                ins.then_inc(dve_step, 1)
                done[0] += 1

            def now():
                dve.wait_ge(dve_step, done[0])

            def flat(t):
                return t.rearrange("p n d -> p (n d)")

            def qk_moments(b):
                for n in range(NB):
                    src = filled(dve, (b, "qkv", n))
                    dve.wait_ge(v_copied, NB * b + n + 1)
                    for w in range(2):
                        last = vec.bn_stats(qkstats[:, n, w, :], src[:, D * w:D * w + D])
                step(last)
                now()
                for n in range(NB):
                    for w in range(2):
                        last = vec.bn_aggr(qkmoments[:, n, w, :], qkstats[:, n, w, :])
                last.then_inc(qk_stats_ready, 1)

            def qk_norm(b):
                dve.wait_ge(qk_rstd_ready, b + 1)
                qkn_free(dve, b)
                for n in DVE_BLOCKS:
                    key = (b, "qkv", n)
                    for w in range(2):
                        last = vec.tensor_scalar(
                            qkn[:, w, n, :], bank(key)[:, D * w:D * w + D],
                            qkmoments[:, n, w, 0:1], qkrstd[:, n, w:w + 1],
                            ALU.subtract, ALU.mult)
                    drains(last, key)

            splits = []

            def left_free():
                if splits:
                    dve.wait_ge(*splits[-1])

            def split(rest, three, ready, n):
                vec.tensor_copy(three[:, 1, :], rest).then_inc(ready[1], 1)
                dve.wait_ge(ready[1], n)
                vec.tensor_tensor(three[:, 2, :], rest, three[:, 1, :], ALU.subtract
                                  ).then_inc(ready[2], 1)
                splits.append((ready[2], n))

            def qkT(b, w):
                key = (b, "qkT", w)
                dve.wait_ge(part_ready[0][0], 2 * b + w + 1)
                left_free()
                drains(vec.scalar_tensor_tensor(left[:, :], bank(key),
                                                col("k_scale") if w else col(QS),
                                                parts[:, w, 0, :], ALU.mult, ALU.subtract), key)
                drained(dve, key)
                split(left[:, :], parts[:, w, :, :], part_ready[0], 2 * b + w + 1)

            def cross_split(b, w):
                n = (S, C)[w]
                drained(dve, (b, ("xq", "xk")[w]))
                left_free()
                three, whole = (xkparts, xkf[:, :]) if w else (xparts, xqf)
                step(vec.tensor_tensor(left[:, 0:n], whole, three[:, 0, :], ALU.subtract))
                now()
                split(left[:, 0:n], three, part_ready[1], 2 * b + 2 - w)

            def maxima(b, a, g, u):
                key = (b, "S", a, g, u)
                src = filled(dve, key)
                pieces = PIECES[a][u]
                if len(pieces) == 2 and pieces[0][2] == pieces[1][2]:
                    (_, h, q), (w, _, _) = pieces
                    drains(vec.tensor_reduce(
                        nmax[:, h:h + 2, q:q + 1],
                        src[:, 0:2 * w].rearrange("p (h k) -> p h k", h=2),
                        AX.X, ALU.max, negate=True), key)
                else:
                    for at, h, q in pieces:
                        last = vec.tensor_reduce(nmax[:, h, q:q + 1], src[:, at:at + P * (q + 1)],
                                                 AX.X, ALU.max, negate=True)
                    drains(last, key)
                if u == len(PIECES[a]) - 1:
                    drained(dve, key)
                    if before(b, a, g):
                        b0, a0, g0 = before(b, a, g)
                        filled(dve, (b0, "mT", a0, g0))
                    m = nmax[:, :, :].rearrange("p h q -> p (h q)")
                    three = mparts[:, g % 2, :, :]
                    step(vec.tensor_copy(three[:, 0, :], m))
                    now()
                    step(vec.tensor_tensor(nrest[:, :], m, three[:, 0, :], ALU.subtract))
                    now()
                    step(vec.tensor_copy(three[:, 1, :], nrest[:, :]))
                    now()
                    vec.tensor_tensor(three[:, 2, :], nrest[:, :], three[:, 1, :],
                                      ALU.subtract).then_inc(mparts_ready, 1)

            def divided(b, a, g):
                key = (b, "cT", a, g)
                src = filled(dve, key).rearrange("p (n h d) -> p n h d", n=NB, h=4)
                step(vec.reciprocal(rsum[:, :, :], src[:, :, :, HD]))
                now()
                drains(vec.tensor_tensor(
                    ctx[:, :, 4 * g:4 * g + 4, :], src[:, :, :, 0:HD],
                    rsum[:, :, :].rearrange("p n (h o) -> p n h o", o=1).to_broadcast(
                        [P, NB, 4, HD]), ALU.mult), key)

            def moments_(b, n):
                r = int(n >= 2)
                y = Y[r]
                if n == 3:
                    linear_sum(b)
                else:
                    key = (b, "out", n) if n < 2 else (b, {2: "mb", 4: "XOT", 5: "down"}[n])
                    src = filled(dve, key)
                    if n == 1:
                        dve.wait_ge(xb_ready[0], b + 1)
                    if n == 2:
                        for i in range(NB):
                            drained(dve, (b, "ex", 2 * i + 1))
                    res = {0: X0[:, b % 2, :, :], 1: XB[0][:, :, :], 2: y[:, :, :]}.get(n)
                    if res is None:
                        res = X[n][:, :, :]
                    drains(vec.tensor_tensor(flat(y[:, :, :]), src, flat(res), ALU.add), key)
                    drained(dve, key)
                for i in range(NB):
                    last = vec.bn_stats(stats[r][:, i, :], y[:, i, :])
                step(last)
                now()
                for i in range(NB):
                    last = vec.bn_aggr(moments[r][:, i, :], stats[r][:, i, :])
                last.then_inc(stats_ready[n], 1)

            def norm(b, n):
                r = int(n >= 2)
                dst = XB[1] if n == 5 else X[n + 1]
                dve.wait_ge(rstd_ready[n], b + 1)
                for i in DVE_BLOCKS:
                    vec.tensor_scalar(dst[:, i, :], Y[r][:, i, :], moments[r][:, i, 0:1],
                                      rstd[r][:, i:i + 1], ALU.subtract, ALU.mult
                                      ).then_inc(x_ready[n + 1], 1)

            def setup_T(b, n):
                if n == SETUP_TRANSPOSES - 4:
                    dve.wait_ge(late_loaded, 16 * N_LATE)
                    for i in range(3):
                        vec.tensor_scalar(ff[i], fi[:, i, :], (0.5 if i == 2 else 1.0) / 127.0,
                                          None, ALU.mult)
                    vec.tensor_copy(bvb, col("lbv").to_broadcast([P, P])
                                    ).then_inc(ff_ready, 1)

            def clear_q(b):
                filled(dve, (b, "wM", SETUP_PRODUCTS - 1))
                vec.memset(raw, 0.0).then_inc(q_cleared, 1)

            def cross_v(b):
                key = (b, "xv")
                src = filled(dve, key)
                for j in range(4):
                    at = slice(32 * j, 32 * j + CR)
                    vec.tensor_tensor(
                        VXR[at, :, 32 * j:32 * j + HD],
                        src[at, P:2 * P].rearrange("p (g h d) -> p g h d", g=NQ, h=4)[:, :, j, :],
                        rows[at, BV, :].rearrange("p (g h d) -> p g h d", g=NQ, h=4)[:, :, j, :],
                        ALU.add)
                drains(vec.tensor_tensor(VX[:, :, 0:HD],
                                         src[:, 0:P].rearrange("p (h d) -> p h d", d=HD),
                                         rows[:, BV, :].rearrange("p (h d) -> p h d", d=HD),
                                         ALU.add), key)

            def over(t):
                return t[:, :].rearrange("p (n o) -> p n o", o=1).to_broadcast([P, NB, E])

            def gate_logits(b):
                key = (b, "gate")
                src = filled(dve, key)[:, 0:NB * E].rearrange("p (n e) -> p n e", n=NB)
                bias = gb[:, :].rearrange("p (o e) -> p o e", o=1).to_broadcast([P, NB, E])
                drains(vec.tensor_tensor(gl[:, :, :], src, bias, ALU.add), key)
                drained(dve, key)
                step(vec.tensor_reduce(gs[:, :], gl[:, :, :], AX.X, ALU.max))
                now()
                vec.tensor_tensor(gl[:, :, :], gl[:, :, :], over(gs), ALU.subtract
                                  ).then_inc(gate_shifted, 1)

            def gates(b):
                dve.wait_ge(gate_exps, b + 1)
                step(vec.tensor_reduce(gs[:, :], ge[:, :, :], AX.X, ALU.add))
                now()
                step(vec.reciprocal(gr[:, :], gs[:, :]))
                now()
                step(vec.tensor_tensor(ge[:, :, :], ge[:, :, :], over(gr), ALU.mult))
                now()
                step(vec.scalar_tensor_tensor(gl[:, :, :], ge[:, :, :], 0.1, ge[:, :, :],
                                              ALU.is_ge, ALU.mult))
                now()
                step(vec.tensor_reduce(gs[:, :], gl[:, :, :], AX.X, ALU.add))
                now()
                step(vec.scalar_tensor_tensor(gr[:, :], gs[:, :], 0.0, gs[:, :],
                                              ALU.is_equal, ALU.add))
                now()
                step(vec.reciprocal(gs[:, :], gr[:, :]))
                now()
                vec.tensor_tensor(gl[:, :, :], gl[:, :, :], over(gs), ALU.mult
                                  ).then_inc(gates_ready, 1)

            def combine(b, n):
                if n == 0:
                    dve.wait_ge(gates_ready, b + 1)
                y = Y[1][:, n, :]
                for e in range(E):
                    key = (b, "ex", 2 * n + e // 4)
                    src = filled(dve, key)
                    if e == 4:
                        drained(dve, (b, "ex", 2 * n))
                    elif e:
                        now()
                    at = P * (e % 4)
                    last = vec.scalar_tensor_tensor(y, src[:, at:at + P], gl[:, n, e:e + 1],
                                                    y if e else X[2][:, n, :],
                                                    ALU.mult, ALU.add)
                    if e % 4 == 3:
                        drains(last, key)
                    else:
                        step(last)

            def clamp(b, w):
                key = (b, ("lq", "lk")[w])
                src = filled(dve, key)
                bias = col("lbk" if w else "lbq")
                vec.tensor_scalar(lexp[:, w, :], src, bias, 0.0, ALU.add, ALU.min
                                  ).then_inc(phi_clamped, 1)
                drains(vec.tensor_scalar(lpos[:, w, :], src, bias, 0.0, ALU.add, ALU.max), key)

            def phi_(b, w):
                dve.wait_ge(phi_exps, 2 * b + 2 - w)
                drained(dve, (b, ("lq", "lk")[w]))
                vec.tensor_tensor(phi[:, w, :], lexp[:, w, :], lpos[:, w, :], ALU.add
                                  ).then_inc(phi_ready, 1)

            def linear_v(b):
                key = (b, "lv")
                src = filled(dve, key).rearrange("p (n d) -> p n d", n=NB)
                drains(vec.tensor_tensor(vaug[:, :, 0:D], src,
                                         rows[:, LBV:LBV + 1, :].to_broadcast([P, NB, D]),
                                         ALU.add), key)

            def linear_mask(b):
                key = (b, "A")
                src = filled(dve, key).rearrange("p (n d) -> p n d", n=NB)
                drains(vec.tensor_tensor(
                    AT, src, causal[:, :].rearrange("p (o q) -> p o q", o=1).to_broadcast(
                        [P, NB, P]), ALU.mult), key)

            def linear_states(b):
                key = (b, "KV")
                src = filled(dve, key)[:, 0:3 * (D + 1)].rearrange("p (n d) -> p n d", n=3)
                step(vec.tensor_copy(state[:, 0, :], src[:, 0, :]))
                now()
                step(vec.tensor_tensor(state[:, 1, :], src[:, 1, :], state[:, 0, :], ALU.add))
                now()
                drains(vec.tensor_tensor(state[:, 2, :], src[:, 2, :], state[:, 1, :], ALU.add),
                       key)

            def linear_sum(b):
                dve.wait_ge(xb_ready[1], b + 1)
                for i in range(2):
                    key = (b, "lo", i)
                    src = filled(dve, key)[:, 0:2 * (D + 1)].rearrange("p (n d) -> p n d", n=2)
                    step(vec.tensor_scalar(den[:, 2 * i:2 * i + 2], src[:, :, D], 1e-6, None,
                                           ALU.add))
                    now()
                    step(vec.reciprocal(den[:, 2 * i:2 * i + 2], den[:, 2 * i:2 * i + 2]))
                    now()
                    for n in range(2):
                        m = 2 * i + n
                        last = vec.scalar_tensor_tensor(Y[1][:, m, :], src[:, n, 0:D],
                                                        den[:, m:m + 1], XB[1][:, m, :],
                                                        ALU.mult, ALU.add)
                    drains(last, key)
                drained(dve, key)

            def cross_maxima(b, i):
                u, at = i // 2, 2 * (i % 2)
                src = filled(dve, (b, "XS", i))[:, 0:2 * C].rearrange("p (h c) -> p h c", h=2)
                vec.tensor_reduce(nxmax[:, u % 2, at:at + 2], src, AX.X, ALU.max,
                                  negate=True).then_inc(xmax_ready, 1)

            def sums(b, u):
                drained(dve, (b, "XS", 2 * u + 1))
                vec.reciprocal(xrs[:, u % 2, :], xsum[:, u % 2, :]).then_inc(xrs_ready, 1)

            def gated(b, c):
                gate, up = (b, "hid", 2 * c), (b, "hid", 2 * c + 1)
                dve.wait_ge(htanh_ready, HC * b + c + 1)
                drains(vec.scalar_tensor_tensor(hT[:, c, :], htanh[:, c, :], 1.0, bank(gate),
                                                ALU.add, ALU.mult), gate)
                drained(dve, gate)
                src = filled(dve, up)
                drains(vec.tensor_tensor(hT[:, c, :], src, hT[:, c, :], ALU.mult), up)

            def by_feature(w):
                return w.rearrange("p (h d) -> p d h", d=HD)

            def by_head(w):
                return w.rearrange("p (d h) -> p d h", d=HD)

            dve.wait_ge(qkv_loaded, 48)
            for w in range(2):
                vec.tensor_copy(by_head(wqkv_p[:, D * w:D * w + D]),
                                by_feature(wqkv[:, D * w:D * w + D]))
            vec.tensor_copy(wqkv_p[:, 2 * D:3 * D], wqkv[:, 2 * D:3 * D]).then_inc(wqkv_ready, 1)
            vec.tensor_scalar(col(QS), col("q_scale"), HEAD_SCALE, None, ALU.mult
                              ).then_inc(bias_cols_ready, 1)
            vec.memset(V[:, :, :, HD:32], 0.0)
            step(vec.memset(VX[:, :, HD:32], 0.0))
            now()
            vec.memset(V[:, :, :, HD:HD + 1], 1.0)
            vec.memset(VX[:, :, HD:HD + 1], 1.0)

            def cross_weights():
                dve.wait_ge(early_loaded, 16 * N_EARLY)
                vec.tensor_scalar(col(XBQ), col("xbq"), HEAD_SCALE, None, ALU.mult)
                vec.tensor_copy(by_head(xwq[:, :]), by_feature(xw_raw[:, 0, :]))
                vec.tensor_copy(by_head(xwk[:, :]), by_feature(xw_raw[:, 1, :])
                                ).then_inc(x0_weights_ready, 1)

            work = {"qk_moments": qk_moments, "qk_norm": qk_norm, "qkT": qkT,
                    "xk": lambda b: cross_split(b, 1), "xq": lambda b: cross_split(b, 0),
                    "xv": cross_v, "S": maxima, "cT": divided, "moments": moments_,
                    "norm": norm, "wT": setup_T, "clear_q": clear_q,
                    "gate_logits": gate_logits, "gates": gates, "combine": combine,
                    "lk": lambda b: clamp(b, 1), "lq": lambda b: clamp(b, 0), "phi": phi_,
                    "lv": linear_v, "A": linear_mask, "KV": linear_states,
                    "XS": cross_maxima, "sums": sums, "gated": gated}
            for b, what, *at in steps:
                if (b, what, *at) == (0, "xk"):
                    cross_weights()
                if what in work:
                    work[what](b, *at)


_INS = ["x", "ctx_1024", "L0_attn_W_qkv", "L0_attn_q_scale", "L0_attn_k_scale", "L0_attn_W_out",
        "L0_xattn_Wq", "L0_xattn_bq", "L0_xattn_Wk", "L0_xattn_bk", "L0_xattn_Wv", "L0_xattn_bv",
        "L0_xattn_Wo", "L0_xattn_bo", "L0_ffn_gate_w", "L0_ffn_gate_b", "L0_ffn_expert_w",
        "L0_ffn_expert_b", "L1_attn_Wq", "L1_attn_bq", "L1_attn_Wk", "L1_attn_bk", "L1_attn_Wv",
        "L1_attn_bv", "L1_attn_Wo", "L1_attn_bo", "L1_xattn_Wq", "L1_xattn_Wkv", "L1_xattn_Wproj",
        "L1_xattn_b_proj", "L1_ffn_w_gate", "L1_ffn_w_up", "L1_ffn_w_down"]


def kernel(**inputs):
    import numpy as np
    import concourse.bacc as bacc
    from concourse.bass_utils import run_bass_kernel_spmd

    nc = bacc.Bacc("TRN2", target_bir_lowering=False, num_devices=1)
    arrays, args = {}, []
    for name in _INS:
        a = np.ascontiguousarray(inputs[name])
        arrays[f"in_{name}"] = a
        args.append(nc.dram_tensor(f"in_{name}", a.shape, mybir.dt.from_np(a.dtype),
                                   kind="ExternalInput").ap())
    out = nc.dram_tensor("out", (B, S, D), F32, kind="ExternalOutput").ap()
    build(nc, *args, out)
    return run_bass_kernel_spmd(nc, [arrays], core_ids=[0]).results[0]["out"]
```
